# Optimizing a Trainium2 kernel written in Bass

```python
import numpy as np
import jax
import jax.numpy as jnp

def _softmax(x, axis=-1):
    return jax.nn.softmax(x, axis=axis)

def _gelu(x):
    return jax.nn.gelu(x, approximate=True)

def _silu(x):
    return jax.nn.silu(x)

def _sigmoid(x):
    return jax.nn.sigmoid(x)

def _layernorm(x, axis=-1, eps=1e-05):
    m = jnp.mean(x, axis=axis, keepdims=True)
    v = jnp.var(x, axis=axis, keepdims=True)
    return (x - m) / jnp.sqrt(v + eps)

def _scatter_add(tgt, idx, src, axis=0):
    return tgt.at[idx].add(src)

def _segment_sum(src, seg, n):
    return jax.ops.segment_sum(src, seg, n)
kernel_name = 'mk_cond_seq_d4_seqx_r4_7ec04a'

def setup_inputs(seed: int=0):
    np.random.seed(seed)
    _w = jnp.asarray

    def _rec_inputs():
        import jax
        import jax.numpy as jnp
        _rk = jax.random.key(seed)
        x = 7.22e-05 + 1 * jax.random.normal(jax.random.fold_in(_rk, 1), (4, 512, 256), jnp.float32)
        _lenS = 512 - jax.random.randint(jax.random.fold_in(_rk, 7), (4,), 0, max(1, 512 // 4) + 1, jnp.int32)
        _lenS2 = 512 - jax.random.randint(jax.random.fold_in(_rk, 8), (4,), 0, max(1, 512 // 4) + 1, jnp.int32)
        condB_gatescore = jax.random.uniform(jax.random.fold_in(_rk, 11), (4,), jnp.float32, 0.0, 0.581427)
        itok_B_0_15 = jax.random.randint(jax.random.fold_in(_rk, 12), (4,), 0, 16, jnp.int32)
        itok_B_0_7 = jax.random.randint(jax.random.fold_in(_rk, 13), (4,), 0, 8, jnp.int32)
        itok_B_34_63 = jax.random.randint(jax.random.fold_in(_rk, 15), (4,), 34, 64, jnp.int32)
        fside_Bx16xSxS_0 = -1.47943e-05 + 1.00017 * jax.random.normal(jax.random.fold_in(_rk, 16), (4, 16, 512, 512), jnp.float32)
        _validS = jnp.arange(512)[None, :] < _lenS[:, None]
        _validS2 = jnp.arange(512)[None, :] < _lenS2[:, None]
        _causal = jnp.tril(jnp.ones((512, 512), dtype=bool))
        mask_Bx1xSxS_bk0 = jnp.logical_not(jnp.broadcast_to(_validS[:, None, None, :], (4, 1, 512, 512)))
        return (x, condB_gatescore, itok_B_0_15, itok_B_0_7, itok_B_34_63, fside_Bx16xSxS_0, mask_Bx1xSxS_bk0)
    x, condB_gatescore, itok_B_0_15, itok_B_0_7, itok_B_34_63, fside_Bx16xSxS_0, mask_Bx1xSxS_bk0 = _rec_inputs()

    def _L0_cond_setup():
        import jax, jax.numpy as jnp
        import numpy as np
        D_MODEL = 256
        N_HEADS = 16
        D_HEAD = D_MODEL // N_HEADS
        D_FF = 1024
        EPS = 1e-05

        def layernorm(x, gamma, beta):
            mu = jnp.mean(x, axis=-1, keepdims=True)
            var = jnp.var(x, axis=-1, keepdims=True)
            return (x - mu) * jax.lax.rsqrt(var + EPS) * gamma + beta
        key = jax.random.key(seed)
        ks = jax.random.split(key, 16)
        B, T = (4, 512)
        s = 1.0 / np.sqrt(D_MODEL)
        sf = 1.0 / np.sqrt(D_FF)
        return {'x': jax.random.normal(ks[0], (B, T, D_MODEL), jnp.float32), 'gate_score': jax.random.uniform(ks[1], (B,), jnp.float32), 'Wq': jax.random.normal(ks[2], (D_MODEL, D_MODEL), jnp.float32) * s, 'bq': jnp.zeros((D_MODEL,), jnp.float32), 'Wk': jax.random.normal(ks[3], (D_MODEL, D_MODEL), jnp.float32) * s, 'bk': jnp.zeros((D_MODEL,), jnp.float32), 'Wv': jax.random.normal(ks[4], (D_MODEL, D_MODEL), jnp.float32) * s, 'bv': jnp.zeros((D_MODEL,), jnp.float32), 'Wo': jax.random.normal(ks[5], (D_MODEL, D_MODEL), jnp.float32) * s, 'bo': jnp.zeros((D_MODEL,), jnp.float32), 'W1': jax.random.normal(ks[6], (D_MODEL, D_FF), jnp.float32) * s, 'b1': jnp.zeros((D_FF,), jnp.float32), 'W2': jax.random.normal(ks[7], (D_FF, D_MODEL), jnp.float32) * sf, 'b2': jnp.zeros((D_MODEL,), jnp.float32), 'gamma1': jnp.ones((D_MODEL,), jnp.float32), 'beta1': jnp.zeros((D_MODEL,), jnp.float32), 'gamma2': jnp.ones((D_MODEL,), jnp.float32), 'beta2': jnp.zeros((D_MODEL,), jnp.float32)}
    _L0_cond_all = _L0_cond_setup()
    _L0_cond_in = {k: v for k, v in _L0_cond_all.items() if k in ('Wq', 'bq', 'Wk', 'bk', 'Wv', 'bv', 'Wo', 'bo', 'W1', 'b1', 'W2', 'b2', 'gamma1', 'beta1', 'gamma2', 'beta2')}
    del _L0_cond_all

    def _L1_cond_setup():
        import jax, jax.numpy as jnp
        import numpy as np
        B, S, D = (32, 256, 256)
        A = 64
        E = 16
        LN_EPS = 1e-05
        key = jax.random.key(seed)
        ks = jax.random.split(key, 10)
        s = lambda fan_in: 1.0 / np.sqrt(fan_in)
        return {'hidden_states': jax.random.normal(ks[0], (B, S, D), dtype=jnp.float32), 'domain_id': jax.random.randint(ks[1], (B,), 0, E, dtype=jnp.int64), 'down_W': jax.random.uniform(ks[2], (A, D), jnp.float32, -s(D), s(D)), 'down_b': jax.random.uniform(ks[3], (A,), jnp.float32, -s(D), s(D)), 'up_W': jax.random.uniform(ks[4], (D, A), jnp.float32, -s(A), s(A)), 'up_b': jax.random.uniform(ks[5], (D,), jnp.float32, -s(A), s(A)), 'expert_W': jax.random.uniform(ks[6], (E, A, A), jnp.float32, -s(A), s(A)), 'expert_b': jax.random.uniform(ks[7], (E, A), jnp.float32, -s(A), s(A)), 'domain_emb': jax.random.normal(ks[8], (E, A), dtype=jnp.float32), 'ln_gamma': jnp.ones((D,), jnp.float32), 'ln_beta': jnp.zeros((D,), jnp.float32)}
    _L1_cond_all = _L1_cond_setup()
    _L1_cond_in = {k: v for k, v in _L1_cond_all.items() if k in ('down_W', 'down_b', 'up_W', 'up_b', 'expert_W', 'expert_b', 'domain_emb', 'ln_gamma', 'ln_beta')}
    del _L1_cond_all

    def _L2_cond_setup():
        import jax, jax.numpy as jnp
        import numpy as np
        E, H, I = (8, 256, 1024)
        B, S = (4, 256)
        LN_EPS = 1e-12
        key = jax.random.key(seed)
        ks = jax.random.split(key, 8)
        x = jax.random.normal(ks[0], (B, S, H), dtype=jnp.float32)
        expert_idx = jax.random.randint(ks[1], (B,), 0, E, dtype=jnp.int64)
        Wi = jax.random.normal(ks[2], (E, H, I), dtype=jnp.float32) * 0.02
        bi = jnp.zeros((E, I), dtype=jnp.float32)
        Wo = jax.random.normal(ks[3], (E, I, H), dtype=jnp.float32) * 0.02
        bo = jnp.zeros((E, H), dtype=jnp.float32)
        gamma = jnp.ones((E, H), dtype=jnp.float32)
        beta = jnp.zeros((E, H), dtype=jnp.float32)
        return {'input_tensor': x, 'expert_idx': expert_idx, 'Wi': Wi, 'bi': bi, 'Wo': Wo, 'bo': bo, 'gamma': gamma, 'beta': beta}
    _L2_cond_all = _L2_cond_setup()
    _L2_cond_in = {k: v for k, v in _L2_cond_all.items() if k in ('Wi', 'bi', 'Wo', 'bo', 'gamma', 'beta')}
    del _L2_cond_all

    def _L3_cond_setup():
        import jax, jax.numpy as jnp
        import numpy as np
        import math
        D_MODEL = 256
        N_HEAD = 16
        HEAD_DIM = D_MODEL // N_HEAD
        D_FF = 1024
        NUM_STEPS = 100.0
        RESCALE = 4000.0
        EPS = 1e-05

        def _sin_emb(t):
            half = D_MODEL // 2
            x = t.astype(jnp.float32) / NUM_STEPS * RESCALE
            freqs = jnp.exp(jnp.arange(half, dtype=jnp.float32) * (-math.log(10000.0) / (half - 1)))
            e = x[:, None] * freqs[None, :]
            return jnp.concatenate([jnp.sin(e), jnp.cos(e)], axis=-1)

        def _ln(x):
            m = jnp.mean(x, axis=-1, keepdims=True)
            v = jnp.var(x, axis=-1, keepdims=True)
            return (x - m) / jnp.sqrt(v + EPS)

        def _gelu2(x):
            return x * jax.nn.sigmoid(1.702 * x)
        key = jax.random.key(seed)
        ks = jax.random.split(key, 24)
        B, S, D, F = (4, 128, D_MODEL, D_FF)
        std = 0.02
        inp = {'src': jax.random.normal(ks[0], (B, S, D), dtype=jnp.float32), 'src_mask': jax.random.randint(ks[1], (B, 1, S, S), 0, 2).astype(bool), 'timestep': jax.random.randint(ks[2], (B,), 0, 100, dtype=jnp.int32), 'attention_bias': jax.random.normal(ks[3], (B, N_HEAD, S, S), dtype=jnp.float32), 'W_ada': jax.random.normal(ks[4], (D, 2 * D), dtype=jnp.float32) * std, 'b_ada': jnp.zeros((2 * D,), dtype=jnp.float32), 'Wq': jax.random.normal(ks[5], (D, D), dtype=jnp.float32) * std, 'bq': jnp.zeros((D,), dtype=jnp.float32), 'Wk': jax.random.normal(ks[6], (D, D), dtype=jnp.float32) * std, 'bk': jnp.zeros((D,), dtype=jnp.float32), 'Wv': jax.random.normal(ks[7], (D, D), dtype=jnp.float32) * std, 'bv': jnp.zeros((D,), dtype=jnp.float32), 'Wo': jax.random.normal(ks[8], (D, D), dtype=jnp.float32) * std, 'bo': jnp.zeros((D,), dtype=jnp.float32), 'W1': jax.random.normal(ks[9], (D, F), dtype=jnp.float32) * std, 'b1': jnp.zeros((F,), dtype=jnp.float32), 'W2': jax.random.normal(ks[10], (F, D), dtype=jnp.float32) * std, 'b2': jnp.zeros((D,), dtype=jnp.float32), 'g2': jnp.ones((D,), dtype=jnp.float32), 'beta2': jnp.zeros((D,), dtype=jnp.float32)}
        return inp
    _L3_cond_all = _L3_cond_setup()
    _L3_cond_in = {k: v for k, v in _L3_cond_all.items() if k in ('W_ada', 'b_ada', 'Wq', 'bq', 'Wk', 'bk', 'Wv', 'bv', 'Wo', 'bo', 'W1', 'b1', 'W2', 'b2', 'g2', 'beta2')}
    del _L3_cond_all
    return {'x': x, 'condB_gatescore': condB_gatescore, 'itok_B_0_15': itok_B_0_15, 'itok_B_0_7': itok_B_0_7, 'itok_B_34_63': itok_B_34_63, 'fside_Bx16xSxS_0': fside_Bx16xSxS_0, 'mask_Bx1xSxS_bk0': mask_Bx1xSxS_bk0, 'L0_cond_Wq': _L0_cond_in['Wq'], 'L0_cond_bq': _L0_cond_in['bq'], 'L0_cond_Wk': _L0_cond_in['Wk'], 'L0_cond_bk': _L0_cond_in['bk'], 'L0_cond_Wv': _L0_cond_in['Wv'], 'L0_cond_bv': _L0_cond_in['bv'], 'L0_cond_Wo': _L0_cond_in['Wo'], 'L0_cond_bo': _L0_cond_in['bo'], 'L0_cond_W1': _L0_cond_in['W1'], 'L0_cond_b1': _L0_cond_in['b1'], 'L0_cond_W2': _L0_cond_in['W2'], 'L0_cond_b2': _L0_cond_in['b2'], 'L0_cond_gamma1': _L0_cond_in['gamma1'], 'L0_cond_beta1': _L0_cond_in['beta1'], 'L0_cond_gamma2': _L0_cond_in['gamma2'], 'L0_cond_beta2': _L0_cond_in['beta2'], 'L1_cond_down_W': _L1_cond_in['down_W'], 'L1_cond_down_b': _L1_cond_in['down_b'], 'L1_cond_up_W': _L1_cond_in['up_W'], 'L1_cond_up_b': _L1_cond_in['up_b'], 'L1_cond_expert_W': _L1_cond_in['expert_W'], 'L1_cond_expert_b': _L1_cond_in['expert_b'], 'L1_cond_domain_emb': _L1_cond_in['domain_emb'], 'L1_cond_ln_gamma': _L1_cond_in['ln_gamma'], 'L1_cond_ln_beta': _L1_cond_in['ln_beta'], 'L2_cond_Wi': _L2_cond_in['Wi'], 'L2_cond_bi': _L2_cond_in['bi'], 'L2_cond_Wo': _L2_cond_in['Wo'], 'L2_cond_bo': _L2_cond_in['bo'], 'L2_cond_gamma': _L2_cond_in['gamma'], 'L2_cond_beta': _L2_cond_in['beta'], 'L3_cond_W_ada': _L3_cond_in['W_ada'], 'L3_cond_b_ada': _L3_cond_in['b_ada'], 'L3_cond_Wq': _L3_cond_in['Wq'], 'L3_cond_bq': _L3_cond_in['bq'], 'L3_cond_Wk': _L3_cond_in['Wk'], 'L3_cond_bk': _L3_cond_in['bk'], 'L3_cond_Wv': _L3_cond_in['Wv'], 'L3_cond_bv': _L3_cond_in['bv'], 'L3_cond_Wo': _L3_cond_in['Wo'], 'L3_cond_bo': _L3_cond_in['bo'], 'L3_cond_W1': _L3_cond_in['W1'], 'L3_cond_b1': _L3_cond_in['b1'], 'L3_cond_W2': _L3_cond_in['W2'], 'L3_cond_b2': _L3_cond_in['b2'], 'L3_cond_g2': _L3_cond_in['g2'], 'L3_cond_beta2': _L3_cond_in['beta2']}

def reference(x, condB_gatescore, itok_B_0_15, itok_B_0_7, itok_B_34_63, fside_Bx16xSxS_0, mask_Bx1xSxS_bk0, L0_cond_Wq, L0_cond_bq, L0_cond_Wk, L0_cond_bk, L0_cond_Wv, L0_cond_bv, L0_cond_Wo, L0_cond_bo, L0_cond_W1, L0_cond_b1, L0_cond_W2, L0_cond_b2, L0_cond_gamma1, L0_cond_beta1, L0_cond_gamma2, L0_cond_beta2, L1_cond_down_W, L1_cond_down_b, L1_cond_up_W, L1_cond_up_b, L1_cond_expert_W, L1_cond_expert_b, L1_cond_domain_emb, L1_cond_ln_gamma, L1_cond_ln_beta, L2_cond_Wi, L2_cond_bi, L2_cond_Wo, L2_cond_bo, L2_cond_gamma, L2_cond_beta, L3_cond_W_ada, L3_cond_b_ada, L3_cond_Wq, L3_cond_bq, L3_cond_Wk, L3_cond_bk, L3_cond_Wv, L3_cond_bv, L3_cond_Wo, L3_cond_bo, L3_cond_W1, L3_cond_b1, L3_cond_W2, L3_cond_b2, L3_cond_g2, L3_cond_beta2):
    import jax
    import jax.numpy as jnp

    def _L0_cond_ref(x, gate_score, Wq, bq, Wk, bk, Wv, bv, Wo, bo, W1, b1, W2, b2, gamma1, beta1, gamma2, beta2):
        import jax, jax.numpy as jnp
        import numpy as np
        D_MODEL = 256
        N_HEADS = 16
        D_HEAD = D_MODEL // N_HEADS
        D_FF = 1024
        EPS = 1e-05

        def layernorm(x, gamma, beta):
            mu = jnp.mean(x, axis=-1, keepdims=True)
            var = jnp.var(x, axis=-1, keepdims=True)
            return (x - mu) * jax.lax.rsqrt(var + EPS) * gamma + beta
        B, T, C = x.shape
        h = layernorm(x, gamma1, beta1)
        Q = (h @ Wq + bq).reshape(B, T, N_HEADS, D_HEAD).transpose(0, 2, 1, 3)
        K = (h @ Wk + bk).reshape(B, T, N_HEADS, D_HEAD).transpose(0, 2, 1, 3)
        V = (h @ Wv + bv).reshape(B, T, N_HEADS, D_HEAD).transpose(0, 2, 1, 3)
        scores = jnp.einsum('bhqd,bhkd->bhqk', Q, K) / np.sqrt(D_HEAD)
        causal = jnp.tril(jnp.ones((T, T), dtype=bool))
        scores = jnp.where(causal, scores, -jnp.inf)
        attn = jax.nn.softmax(scores, axis=-1)
        ctx = jnp.einsum('bhqk,bhkd->bhqd', attn, V)
        ctx = ctx.transpose(0, 2, 1, 3).reshape(B, T, C)
        attn_out = ctx @ Wo + bo
        x1 = x + attn_out
        h2 = layernorm(x1, gamma2, beta2)
        ff = jax.nn.gelu(h2 @ W1 + b1, approximate=False) @ W2 + b2
        x2 = x1 + ff
        g = gate_score[:, None, None]
        return x + g * (x2 - x)

    def _L1_cond_ref(hidden_states, domain_id, down_W, down_b, up_W, up_b, expert_W, expert_b, domain_emb, ln_gamma, ln_beta):
        import jax, jax.numpy as jnp
        import numpy as np
        B, S, D = (32, 256, 256)
        A = 64
        E = 16
        LN_EPS = 1e-05
        residual = hidden_states
        hidden = jnp.einsum('bsd,ad->bsa', hidden_states, down_W) + down_b
        hidden = jax.nn.gelu(hidden, approximate=False)
        valid = (domain_id >= 0) & (domain_id < E)
        idx = jnp.clip(domain_id, 0, E - 1)
        Wsel = expert_W[idx]
        bsel = expert_b[idx]
        expert_out = jnp.einsum('bsa,boa->bso', hidden, Wsel) + bsel[:, None, :]
        domain_output = jnp.where(valid[:, None, None], expert_out, hidden)
        hidden = domain_output + domain_emb[idx][:, None, :]
        hidden = jnp.einsum('bsa,da->bsd', hidden, up_W) + up_b
        x = hidden + residual
        mu = jnp.mean(x, axis=-1, keepdims=True)
        var = jnp.mean(jnp.square(x - mu), axis=-1, keepdims=True)
        return (x - mu) * jax.lax.rsqrt(var + LN_EPS) * ln_gamma + ln_beta

    def _L2_cond_ref(input_tensor, expert_idx, Wi, bi, Wo, bo, gamma, beta):
        import jax, jax.numpy as jnp
        import numpy as np
        E, H, I = (8, 256, 1024)
        B, S = (4, 256)
        LN_EPS = 1e-12
        Wi_b = Wi[expert_idx]
        bi_b = bi[expert_idx]
        Wo_b = Wo[expert_idx]
        bo_b = bo[expert_idx]
        g_b = gamma[expert_idx]
        be_b = beta[expert_idx]
        h = jax.nn.gelu(jnp.einsum('bsh,bhi->bsi', input_tensor, Wi_b) + bi_b[:, None, :], approximate=False)
        o = jnp.einsum('bsi,bih->bsh', h, Wo_b) + bo_b[:, None, :]
        r = o + input_tensor
        mu = jnp.mean(r, axis=-1, keepdims=True)
        var = jnp.mean(jnp.square(r - mu), axis=-1, keepdims=True)
        y = (r - mu) * jax.lax.rsqrt(var + LN_EPS)
        return y * g_b[:, None, :] + be_b[:, None, :]

    def _L3_cond_ref(src, src_mask, timestep, attention_bias, W_ada, b_ada, Wq, bq, Wk, bk, Wv, bv, Wo, bo, W1, b1, W2, b2, g2, beta2):
        import jax, jax.numpy as jnp
        import numpy as np
        import math
        D_MODEL = 256
        N_HEAD = 16
        HEAD_DIM = D_MODEL // N_HEAD
        D_FF = 1024
        NUM_STEPS = 100.0
        RESCALE = 4000.0
        EPS = 1e-05

        def _sin_emb(t):
            half = D_MODEL // 2
            x = t.astype(jnp.float32) / NUM_STEPS * RESCALE
            freqs = jnp.exp(jnp.arange(half, dtype=jnp.float32) * (-math.log(10000.0) / (half - 1)))
            e = x[:, None] * freqs[None, :]
            return jnp.concatenate([jnp.sin(e), jnp.cos(e)], axis=-1)

        def _ln(x):
            m = jnp.mean(x, axis=-1, keepdims=True)
            v = jnp.var(x, axis=-1, keepdims=True)
            return (x - m) / jnp.sqrt(v + EPS)

        def _gelu2(x):
            return x * jax.nn.sigmoid(1.702 * x)
        B, S, D = src.shape
        emb = jax.nn.silu(_sin_emb(timestep)) @ W_ada + b_ada
        scale, shift = jnp.split(emb[:, None, :], 2, axis=-1)
        x = _ln(src) * (1.0 + scale) + shift
        q = (x @ Wq + bq).reshape(B, S, N_HEAD, HEAD_DIM).transpose(0, 2, 1, 3)
        k = (x @ Wk + bk).reshape(B, S, N_HEAD, HEAD_DIM).transpose(0, 2, 1, 3)
        v = (x @ Wv + bv).reshape(B, S, N_HEAD, HEAD_DIM).transpose(0, 2, 1, 3)
        scores = jnp.einsum('bhqd,bhkd->bhqk', q / math.sqrt(HEAD_DIM), k)
        scores = scores + attention_bias
        scores = jnp.where(src_mask, -jnp.inf, scores.astype(jnp.float32))
        probs = jax.nn.softmax(scores, axis=-1).astype(v.dtype)
        ctx = jnp.einsum('bhqk,bhkd->bhqd', probs, v)
        ctx = ctx.transpose(0, 2, 1, 3).reshape(B, S, D)
        x = x + (ctx @ Wo + bo)
        h = _ln(x) * g2 + beta2
        ff = _gelu2(h @ W1 + b1) @ W2 + b2
        return x + ff
    x = _L0_cond_ref(x, condB_gatescore, L0_cond_Wq, L0_cond_bq, L0_cond_Wk, L0_cond_bk, L0_cond_Wv, L0_cond_bv, L0_cond_Wo, L0_cond_bo, L0_cond_W1, L0_cond_b1, L0_cond_W2, L0_cond_b2, L0_cond_gamma1, L0_cond_beta1, L0_cond_gamma2, L0_cond_beta2)
    x = _L1_cond_ref(x, itok_B_0_15, L1_cond_down_W, L1_cond_down_b, L1_cond_up_W, L1_cond_up_b, L1_cond_expert_W, L1_cond_expert_b, L1_cond_domain_emb, L1_cond_ln_gamma, L1_cond_ln_beta)
    x = _L2_cond_ref(x, itok_B_0_7, L2_cond_Wi, L2_cond_bi, L2_cond_Wo, L2_cond_bo, L2_cond_gamma, L2_cond_beta)
    x = _L3_cond_ref(x, mask_Bx1xSxS_bk0, itok_B_34_63, fside_Bx16xSxS_0, L3_cond_W_ada, L3_cond_b_ada, L3_cond_Wq, L3_cond_bq, L3_cond_Wk, L3_cond_bk, L3_cond_Wv, L3_cond_bv, L3_cond_Wo, L3_cond_bo, L3_cond_W1, L3_cond_b1, L3_cond_W2, L3_cond_b2, L3_cond_g2, L3_cond_beta2)
    return x

_drawn_inputs = setup_inputs


def setup_inputs(seed=0):
    import zlib

    import numpy as np

    out = dict(_drawn_inputs(seed))
    spreads = {'L0_cond_bq': (0.0, 0.8),
     'L0_cond_bk': (0.0, 0.8),
     'L0_cond_bv': (0.0, 0.1),
     'L0_cond_bo': (0.0, 0.1),
     'L0_cond_b1': (0.0, 0.395),
     'L0_cond_b2': (0.0, 0.293),
     'L0_cond_gamma1': (1.0, 0.6),
     'L0_cond_beta1': (0.0, 0.1),
     'L0_cond_gamma2': (1.0, 0.2),
     'L0_cond_beta2': (0.0, 0.405),
     'L1_cond_ln_gamma': (1.0, 0.2),
     'L1_cond_ln_beta': (0.0, 0.1),
     'L2_cond_bi': (0.0, 0.1),
     'L2_cond_bo': (0.0, 0.1),
     'L2_cond_gamma': (1.0, 0.2),
     'L2_cond_beta': (0.0, 0.1),
     'L3_cond_b_ada': (0.0, 0.1),
     'L3_cond_bq': (0.0, 0.8),
     'L3_cond_bk': (0.0, 0.8),
     'L3_cond_bv': (0.0, 0.1),
     'L3_cond_bo': (0.0, 0.1),
     'L3_cond_b1': (0.0, 0.1),
     'L3_cond_b2': (0.0, 0.1),
     'L3_cond_g2': (1.0, 0.6),
     'L3_cond_beta2': (0.0, 0.777)}
    factors = {'fside_Bx16xSxS_0': 8.0, 'L1_cond_down_b': 8.0, 'L3_cond_Wq': 8.0, 'L3_cond_Wk': 8.0}
    for name, (base, spread) in spreads.items():
        noise = np.random.default_rng([zlib.crc32(name.encode()), seed]).standard_normal(out[name].shape)
        drawn = base * np.exp(spread * noise) if base else spread * noise
        out[name] = jnp.asarray(drawn.astype(out[name].dtype))
    for name, factor in factors.items():
        out[name] = (out[name] * factor).astype(out[name].dtype)
    return out
```

```python
from contextlib import ExitStack

import concourse.bass as bass
from concourse import mybir

P = 128
B, S, D, F = 4, 512, 256, 1024
H, DH = 16, 16
NT = S // P
ND = D // P
NF = F // P
A = 64
GH = 4
NG = H // GH
HH = H // 2
UNITS = H * NT
PT_RING = 6
BIAS_RING = 3
NEG = -1e30
PARTS_Q = 5
PARTS_K = 3
STACK = [(0, 2, 0, 0), (2, 3, 1, 0), (5, 3, 2, 0)]

ALU = mybir.AluOpType
ACT = mybir.ActivationFunctionType
AX_X = mybir.AxisListType.X
F32 = mybir.dt.float32
BF16 = mybir.dt.bfloat16
I32 = mybir.dt.int32
U8 = mybir.dt.uint8

TWO_PI = 6.283185307179586
PI_HI = 6.28125
PI_MID = round((TWO_PI - PI_HI) * 2 ** 23) / 2 ** 23
PI_LO = TWO_PI - PI_HI - PI_MID
PI_LIMIT = 3.1415925
ROUND = 12582912.0
RSQRT_MAGIC = 1597463007.0


def build(nc, T, out):
    with ExitStack() as ctx:
        def sb(name, shape, dt=F32):
            return ctx.enter_context(nc.sbuf_tensor(name, shape, dt))

        def sem(name):
            return ctx.enter_context(nc.semaphore(name))

        ident = sb("ident", [P, P])
        identb = sb("identb", [P, P], BF16)
        sumrow = sb("sumrow", [P, P])
        causal = sb("causal", [P, P], BF16)
        wq = [sb(f"wq{l}", [P, ND, D]) for l in range(2)]
        wk = [sb(f"wk{l}", [P, ND, D]) for l in range(2)]
        wv = [sb(f"wv{l}", [P, ND, D]) for l in range(2)]
        wo = [sb(f"wo{l}", [P, NG, D]) for l in range(2)]
        bqk = [sb(f"bqk{l}", [P, 4]) for l in range(2)]
        bv = [sb(f"bv{l}", [P, D]) for l in range(2)]
        b2 = [sb(f"b2_{l}", [P, D]) for l in range(2)]
        b1 = [sb(f"b1_{l}", [P, NF]) for l in range(3)]
        norm_w = [sb(f"norm_w{l}", [P, 4]) for l in range(3)]
        w1 = sb("w1", [P, ND, F])
        w2 = sb("w2", [P, NF, D])
        down_t = sb("down_t", [P, ND, A])
        up_t = sb("up_t", [A + 1, D])
        down_b = sb("down_b", [A, 1])
        ln1 = sb("ln1", [P, 2, D])
        exp_w = sb("exp_w", [A, A])
        exp_wt = sb("exp_wt", [A, A])
        exp_b = sb("exp_b", [A, 3])
        l2row = sb("l2row", [P, 3, D])
        ada = sb("ada", [P, 2 * D])
        gate = sb("gate", [P, B])
        idx = sb("idx", [1, 2 * B], I32)

        xin = sb("xin", [P, NT, D])
        x1 = sb("x1", [P, NT, D])
        y = sb("y", [P, NT, D])
        ctxn = sb("ctxn", [P, NG, S])
        h = ctxn[:, 0:2].rearrange("p a (b d) -> p (a b) d", d=D)
        hT = ctxn[:, 2:4]
        parts = [sb(f"parts{i}", [P, 3, S], BF16) for i in range(2)]
        rest = [sb(f"rest{i}", [P, S]) for i in range(2)]
        qs = sb("qs", [P, H, S], BF16)
        ks = sb("ks", [P, H, S], BF16)
        va = sb("va", [P, NT, H, 32])
        pT = sb("pT", [P, PT_RING, NT, S])
        gT = pT[:, 0:2].rearrange("p a b s -> p (a b) s")
        bias = sb("bias", [P, BIAS_RING, NT, S])
        prob = sb("prob", [P, 3, S])
        mrow = sb("mrow", [P, UNITS])
        negmask = sb("negmask", [P, NT, S], BF16)
        maskraw = prob[:, 0].bitcast(U8).rearrange("p (t s) -> p t s", s=S)
        ctxu, rsum = rest
        aT = rest[0][0:A, :]
        eT = sb("eT", [A + 1, S])
        stats = sb("stats", [P, NT, 6])
        mv = sb("mv", [P, NT, 2])
        rstd = sb("rstd", [P, NT])
        nwt = sb("nwt", [P, 3, NT])

        w_ada = pT[:, 0, 0:2, :]
        b_ada = pT[0:B, 0, 2, :]
        down_raw = pT[0:A, 1, 0, 0:D]
        up_raw = pT[:, 1, 1, 0:ND * A].rearrange("p (c a) -> p c a", a=A)
        ada4 = pT[0:B, 1, 2, :]
        sin_t = pT[:, 1, 3, 0:96].rearrange("p (n b) -> p n b", b=B)
        tok_i = pT[:, 1, 3, 96:96 + B].bitcast(I32)
        freq = pT[:, 1, 3, 104:105]

        q_dram = nc.dram_tensor("q_parts", (H, PARTS_Q, DH, S), BF16).ap()
        k_dram = nc.dram_tensor("k_parts", (H, PARTS_K, DH, S), BF16).ap()
        ada_dram = nc.dram_tensor("ada_rows", (B, 2 * D), F32).ap()

        bank = [ctx.enter_context(nc.psum_tensor(f"bank{i}", [P, S], F32)) for i in range(8)]

        load_a = sem("load_a")
        load_b = sem("load_b")
        consts = sem("consts")
        setup_v = sem("setup_v")
        setup_p = sem("setup_p")
        setup_a = sem("setup_a")
        setup_t = sem("setup_t")
        ada_out = sem("ada_out")
        x_in = sem("x_in")
        par_in = sem("par_in")
        mask_in = sem("mask_in")
        mask_done = sem("mask_done")
        w1_in = sem("w1_in")
        w2_in = sem("w2_in")
        bias_in = [sem(f"bias_in{i}") for i in range(BIAS_RING)]
        tok = sem("tok")
        t_psum = sem("t_psum")
        hT_a = sem("hT_a")
        hT_v = sem("hT_v")
        qk_psum = sem("qk_psum")
        v_psum = sem("v_psum")
        hi_done = sem("hi_done")
        rest_done = sem("rest_done")
        mid_done = sem("mid_done")
        lo_done = sem("lo_done")
        parts_out = [sem(f"parts_out{i}") for i in range(4)]
        stack_in = [sem(f"stack_in{i}") for i in range(2)]
        v_done = sem("v_done")
        s_psum = sem("s_psum")
        max_done = sem("max_done")
        p_done = sem("p_done")
        pt_psum = sem("pt_psum")
        pt_a = sem("pt_a")
        pt_v = sem("pt_v")
        ctx_psum = sem("ctx_psum")
        ctx_copy = sem("ctx_copy")
        sum_psum = sem("sum_psum")
        ctx_norm = sem("ctx_norm")
        wo_psum = sem("wo_psum")
        f1_psum = sem("f1_psum")
        g_done = sem("g_done")
        f2_psum = sem("f2_psum")
        res_pool = sem("res_pool")
        ad_psum = sem("ad_psum")
        ad_act = sem("ad_act")
        ad_wt = sem("ad_wt")
        vec = sem("vec")
        fin = sem("fin")
        stored = sem("stored")

        PAR = 8
        LN_STEPS = 2 * NT + 12
        VEC = 6 * LN_STEPS + 4 * NT + 2 * NG + 5 * 2

        ctx.enter_context(nc.allow_non_contiguous_dma(reason="vectors of a few hundred elements, features on the partitions"))
        x1_free = sem("x1_free")
        waits_alone = sem("waits_alone")
        block = ctx.enter_context(nc.Block())

        def alone(eng):
            eng.nop().then_inc(waits_alone, 1)

        @block.sync
        def _(sp):
            def sp_wait(s, value):
                sp.wait_ge(s, value)
                alone(sp)

            sp.dma_start(wq[0][:], T["L0_cond_Wq"].rearrange("(c p) n -> p c n", p=P)).then_inc(load_a, 16)
            sp.dma_start(wk[0][:], T["L0_cond_Wk"].rearrange("(c p) n -> p c n", p=P)).then_inc(load_a, 16)
            sp.dma_start(wv[0][:], T["L0_cond_Wv"].rearrange("(c p) n -> p c n", p=P)).then_inc(load_a, 16)
            for c in range(2):
                sp.dma_start(bqk[0][:, 2 * c:2 * c + 1], T["L0_cond_bq"][c * P:(c + 1) * P].unsqueeze(1)).then_inc(load_a, 16)
                sp.dma_start(bqk[0][:, 2 * c + 1:2 * c + 2], T["L0_cond_bk"][c * P:(c + 1) * P].unsqueeze(1)).then_inc(load_a, 16)
            sp.dma_start(bv[0][:], T["L0_cond_bv"].partition_broadcast(P)).then_inc(load_a, 16)
            sp.dma_start(norm_w[0][:, 0:2], T["L0_cond_gamma1"].rearrange("(c p) -> p c", p=P)).then_inc(load_a, 16)
            sp.dma_start(norm_w[0][:, 2:4], T["L0_cond_beta1"].rearrange("(c p) -> p c", p=P)).then_inc(load_a, 16)
            sp.dma_start(idx[:, 0:B], T["itok_B_0_15"].unsqueeze(0)).then_inc(load_a, 16)
            sp.dma_start(idx[:, B:2 * B], T["itok_B_0_7"].unsqueeze(0)).then_inc(load_a, 16)
            sp.wait_ge(load_a, 16 * LOADS_A)

            def stacks(b, l):
                for i in range(4):
                    c, is_k = i // 2, i % 2
                    hs = slice(c * HH, (c + 1) * HH)
                    sp_wait(lo_done, b * 8 + (4 * l + i + 1))
                    dram, n = (k_dram, PARTS_K) if is_k else (q_dram, PARTS_Q)
                    for j in range(n):
                        sp.dma_start(dram[hs, j].rearrange("h d t -> h (d t)"),
                                     parts[i % 2][:, j % 3, :]).then_inc(parts_out[i], 16)
                    if is_k == 0:
                        continue
                    sp_wait(parts_out[i - 1], b * (2 * 16 * PARTS_Q) + 16 * PARTS_Q * (l + 1) + CREDIT)
                    sp_wait(parts_out[i], b * (2 * 16 * PARTS_K) + 16 * PARTS_K * (l + 1) + CREDIT)
                    for r, k, q0, k0 in STACK:
                        rows = slice(r * DH, (r + k) * DH)
                        sp.dma_start(qs[rows, hs, :],
                                     q_dram[hs, q0:q0 + k].rearrange("h p d t -> (p d) h t")).then_inc(stack_in[c], 16)
                        sp.dma_start(ks[rows, hs, :],
                                     k_dram[hs, k0:k0 + k].rearrange("h p d t -> (p d) h t")).then_inc(stack_in[c], 16)

            def ffn_weights(b, f, w1_src, w2_src):
                sp_wait(f1_psum, b * 24 + 8 * f + CREDIT)
                sp.dma_start(w1[:], w1_src.rearrange("(c p) n -> p c n", p=P)).then_inc(w1_in, 16)
                sp_wait(f2_psum, b * 6 + 2 * f + CREDIT)
                sp.dma_start(w2[:], w2_src.rearrange("(c p) n -> p c n", p=P)).then_inc(w2_in, 16)

            def load_bias(b, hd):
                slot = hd % BIAS_RING
                if hd < BIAS_RING:
                    sp_wait(pt_psum, b * 128 + CREDIT)
                else:
                    sp_wait(pt_psum, b * 128 + UNITS + NT * (hd - BIAS_RING + 1) + CREDIT)
                sp.dma_start(bias[:, slot], T["fside_Bx16xSxS_0"][bass.ds(b, 1), hd].rearrange(
                    "a (t p) k -> p (a t) k", p=P)).then_inc(bias_in[slot], 16)

            with sp.Fori(0, B) as b:
                sp_wait(hT_a, 6 * b + CREDIT)
                sp_wait(hT_v, 6 * b + CREDIT)
                sp.dma_start(xin[:], T["x"][bass.ds(b, 1)].rearrange("a (t p) d -> p (a t) d", p=P)).then_inc(x_in, 16)
                e16 = sp.value_load(idx[0:1, bass.ds(b, 1)], min_val=0, max_val=15)
                e8 = sp.value_load(idx[0:1, bass.ds(b + B, 1)], min_val=0, max_val=7)
                ffn_weights(b, 0, T["L0_cond_W1"], T["L0_cond_W2"])
                sp.dma_start(exp_w[:], T["L1_cond_expert_W"][bass.ds(e16, 1)].rearrange("a o i -> (a o) i")).then_inc(par_in, 16)
                sp.dma_start(exp_b[:, 0:1], T["L1_cond_expert_b"][bass.ds(e16, 1)].rearrange("a o -> o a")).then_inc(par_in, 16)
                sp.dma_start(exp_b[:, 1:2], T["L1_cond_domain_emb"][bass.ds(e16, 1)].rearrange("a o -> o a")).then_inc(par_in, 16)
                sp.dma_start(b1[1][:], T["L2_cond_bi"][bass.ds(e8, 1)].rearrange("a (j p) -> p (a j)", p=P)).then_inc(par_in, 16)
                for j, name in enumerate(["L2_cond_bo", "L2_cond_gamma", "L2_cond_beta"]):
                    sp.dma_start(l2row[:, j, :], T[name][bass.ds(e8, 1)].rearrange("a d -> (a d)").partition_broadcast(P)).then_inc(par_in, 16)
                sp.wait_ge(ada_out, 16)
                sp.dma_start(ada[:], ada_dram[bass.ds(b, 1)].rearrange("a d -> (a d)").partition_broadcast(P)).then_inc(par_in, 16)
                for hd in range(BIAS_RING):
                    load_bias(b, hd)
                stacks(b, 0)
                ffn_weights(b, 1, T["L2_cond_Wi"][bass.ds(e8, 1)].rearrange("a d f -> (a d) f"),
                            T["L2_cond_Wo"][bass.ds(e8, 1)].rearrange("a d f -> (a d) f"))
                sp_wait(pt_psum, b * 128 + UNITS + CREDIT)
                sp.dma_start(maskraw, T["mask_Bx1xSxS_bk0"][bass.ds(b, 1), 0].rearrange(
                    "a (t p) k -> p (a t) k", p=P)).then_inc(mask_in, 16)
                ffn_weights(b, 2, T["L3_cond_W1"], T["L3_cond_W2"])
                stacks(b, 1)
                for hd in range(BIAS_RING, H):
                    load_bias(b, hd)

        @block.gpsimd
        def _(pool):
            for s in (f1_psum, f2_psum, pt_psum, hT_a, hT_v, x1_free, fin, *parts_out):
                pool.sem_inc(s, CREDIT)

            n_const = [0]

            def const(ins):
                n_const[0] += 1
                ins.then_inc(consts, 1)
                pool.wait_ge(consts, n_const[0])

            const(pool.memset(ident[:], 0.0))
            const(pool.memset(identb[:], 0.0))
            const(pool.memset(sumrow[:], 0.0))
            const(pool.memset(causal[:], 0.0))
            for l in range(2):
                const(pool.memset(wo[l][:], 0.0))
            const(pool.memset(va[:], 0.0))
            const(pool.memset(eT[A:A + 1, :], 1.0))
            for m in (ident, identb):
                const(pool.affine_select(out=m[:], in_=m[:], compare_op=ALU.not_equal, fill=1.0, base=0,
                                         pattern=[[-1, P]], channel_multiplier=1))
            const(pool.affine_select(out=sumrow[:].rearrange("p (j r) -> p j r", r=32),
                                     in_=sumrow[:].rearrange("p (j r) -> p j r", r=32),
                                     compare_op=ALU.not_equal, fill=1.0, base=-DH,
                                     pattern=[[-32, GH], [0, 32]], channel_multiplier=1))
            const(pool.affine_select(out=causal[:], in_=causal[:], compare_op=ALU.is_ge, fill=NEG, base=0,
                                     pattern=[[-1, P]], channel_multiplier=1))
            const(pool.memset(va[:, :, :, DH:DH + 1], 1.0))
            assert n_const[0] == CONSTS

            def late(dst, src):
                pool.dma_start(dst, src).then_inc(load_b, 16)

            late(tok_i, T["itok_B_34_63"].partition_broadcast(P))
            late(freq, T["freqs"].unsqueeze(1))
            late(w_ada, T["L3_cond_W_ada"].rearrange("(c p) n -> p c n", p=P))
            late(b_ada, T["L3_cond_b_ada"].partition_broadcast(B))
            late(down_raw, T["L1_cond_down_W"])
            late(up_raw, T["L1_cond_up_W"].rearrange("(c p) a -> p c a", p=P))
            late(up_t[A:A + 1, :], T["L1_cond_up_b"].unsqueeze(0))
            late(down_b[:], T["L1_cond_down_b"].unsqueeze(1))
            late(gate[:], T["condB_gatescore"].partition_broadcast(P))
            for l, name in enumerate(["L0", "L3"]):
                wo_rows = T[f"{name}_cond_Wo"].rearrange("(g j r) n -> j r g n", g=NG, j=GH)
                for j in range(GH):
                    late(wo[l][32 * j:32 * j + DH, :, :], wo_rows[j])
                late(wo[l][DH:DH + 1, 0, :], T[f"{name}_cond_bo"].unsqueeze(0))
                late(b2[l][:], T[f"{name}_cond_b2"].partition_broadcast(P))
                late(b1[2 * l][:], T[f"{name}_cond_b1"].rearrange("(j p) -> p j", p=P))
            late(norm_w[1][:, 0:2], T["L0_cond_gamma2"].rearrange("(c p) -> p c", p=P))
            late(norm_w[1][:, 2:4], T["L0_cond_beta2"].rearrange("(c p) -> p c", p=P))
            late(norm_w[2][:, 0:2], T["L3_cond_g2"].rearrange("(c p) -> p c", p=P))
            late(norm_w[2][:, 2:4], T["L3_cond_beta2"].rearrange("(c p) -> p c", p=P))
            late(ln1[:, 0, :], T["L1_cond_ln_gamma"].partition_broadcast(P))
            late(ln1[:, 1, :], T["L1_cond_ln_beta"].partition_broadcast(P))
            late(wq[1][:], T["L3_cond_Wq"].rearrange("(c p) n -> p c n", p=P))
            late(wk[1][:], T["L3_cond_Wk"].rearrange("(c p) n -> p c n", p=P))
            late(wv[1][:], T["L3_cond_Wv"].rearrange("(c p) n -> p c n", p=P))
            for c in range(2):
                late(bqk[1][:, 2 * c:2 * c + 1], T["L3_cond_bq"][c * P:(c + 1) * P].unsqueeze(1))
                late(bqk[1][:, 2 * c + 1:2 * c + 2], T["L3_cond_bk"][c * P:(c + 1) * P].unsqueeze(1))
            late(bv[1][:], T["L3_cond_bv"].partition_broadcast(P))
            pool.wait_ge(load_b, 16 * LOADS_B)
            pool.tensor_copy(sin_t[:, 0, :], tok_i).then_inc(setup_p, 1)
            pool.wait_ge(setup_p, 1)
            pool.tensor_scalar(wq[1][:], wq[1][:], 0.25, None, ALU.mult).then_inc(setup_p, 1)
            pool.wait_ge(setup_p, 2)
            pool.tensor_scalar(bqk[1][:, 0:4:2], bqk[1][:, 0:4:2], 0.25, None, ALU.mult).then_inc(setup_p, 1)

            pool.wait_ge(setup_p, 3)
            pool.wait_ge(setup_v, SILU_READY + 2)
            pool.dma_start(ada_dram, ada4).then_inc(ada_out, 16)

            with pool.Fori(0, B) as b:
                pool.wait_ge(tok, b * 24 + 8)
                pool.tensor_tensor(x1[:], x1[:], xin[:], ALU.subtract).then_inc(res_pool, 1)
                pool.wait_ge(res_pool, b * 4 + 1)
                pool.tensor_tensor(x1[:], x1[:], b2[0][:].unsqueeze(1).broadcast_to([P, NT, D]), ALU.add).then_inc(res_pool, 1)
                pool.wait_ge(mask_in, b * 16 + 16)
                alone(pool)
                pool.wait_ge(res_pool, b * 4 + 2)
                alone(pool)
                pool.tensor_scalar(negmask[:], maskraw, NEG, None, ALU.mult).then_inc(mask_done, 1)
                pool.wait_ge(par_in, b * 16 * PAR + 16 * PAR)
                pool.wait_ge(t_psum, b * 6 + 4)
                pool.wait_ge(mask_done, b + 1)
                pool.tensor_tensor(y[:], y[:], l2row[:, 0:1, :].broadcast_to([P, NT, D]), ALU.add).then_inc(res_pool, 1)
                pool.wait_ge(tok, b * 24 + 24)
                pool.wait_ge(res_pool, b * 4 + 3)
                pool.tensor_tensor(x1[:], x1[:], b2[1][:].unsqueeze(1).broadcast_to([P, NT, D]), ALU.add).then_inc(res_pool, 1)
                pool.wait_ge(fin, b * NT + NT + CREDIT)
                pool.dma_start(out[bass.ds(b, 1)].rearrange("a (t p) d -> p (a t) d", p=P), x1[:]).then_inc(stored, 16)
                pool.wait_ge(stored, b * 16 + 16)
                pool.sem_inc(x1_free, 1)
            pool.wait_ge(stored, 16 * B)

        @block.scalar
        def _(act):
            act.wait_ge(setup_v, SIN_READY)
            act.activation(sin_t[:, 14:16, :], sin_t[:, 12:14, :], ACT.Sin).then_inc(setup_a, 1)
            act.wait_ge(setup_a, 1)
            act.activation(sin_t[:, 16:18, :], sin_t[:, 14:16, :], ACT.Exp, scale=-1.0).then_inc(setup_a, 1)

            def feature_half(b, k, w):
                act.wait_ge(t_psum, b * 6 + k + 1)
                if w is None:
                    act.activation(hT[:, 0, :], bank[0][:], ACT.Identity).then_inc(hT_a, 1)
                else:
                    act.activation(hT[:, 0, :], bank[0][:], ACT.Identity, scale=w[:, 0:1], bias=w[:, 2:3]).then_inc(hT_a, 1)

            def qk_parts(b, l):
                def mid(i):
                    act.wait_ge(rest_done, b * 8 + 4 * l + i + 1)
                    act.activation(parts[i % 2][:, 1, :], rest[i % 2][:], ACT.Identity).then_inc(mid_done, 1)

                for i in range(4):
                    act.wait_ge(qk_psum, b * 8 + 4 * l + i + 1)
                    if i >= 2:
                        n = PARTS_K if i % 2 else PARTS_Q
                        act.wait_ge(parts_out[i - 2], b * (2 * 16 * n) + 16 * n * (l + 1) + CREDIT)
                    else:
                        n = PARTS_K if i % 2 else PARTS_Q
                        act.wait_ge(parts_out[i + 2], b * (2 * 16 * n) + 16 * n * l + CREDIT)
                    act.activation(parts[i % 2][:, 0, :], bank[2 + i][:], ACT.Identity,
                                   bias=bqk[l][:, i:i + 1]).then_inc(hi_done, 1)
                    if i >= 1:
                        mid(i - 1)
                mid(3)

            def attention(b, l):
                def copy(u):
                    hd, t = divmod(u, NT)
                    n = (t + 1) * P if l == 0 else S
                    act.wait_ge(pt_psum, b * 128 + UNITS * l + u + 1 + CREDIT)
                    if hd >= PT_RING and t < 2:
                        act.wait_ge(ctx_psum, b * 8 + NG * l + (hd - PT_RING) // GH + 1)
                    act.activation(pT[:, hd % PT_RING, 0:n // P, t * P:(t + 1) * P],
                                   bank[3 + u % 3][:, 0:n].rearrange("p (k q) -> p k q", q=P),
                                   ACT.Identity).then_inc(pt_a, 1)

                def ctx_out(g):
                    act.wait_ge(ctx_psum, b * 8 + NG * l + g + 1)
                    if g:
                        act.wait_ge(ctx_norm, b * 8 + NG * l + g)
                    act.activation(ctxu[:], bank[6][:], ACT.Identity).then_inc(ctx_copy, 1)

                for u in range(UNITS + ACT_LAG):
                    if u < UNITS:
                        hd, t = divmod(u, NT)
                        n = (t + 1) * P if l == 0 else S
                        act.wait_ge(max_done, b * 128 + UNITS * l + u + 1)
                        if l == 0:
                            if u >= 3:
                                act.wait_ge(pt_psum, b * 128 + UNITS * l + u - 2 + CREDIT)
                            act.activation(prob[:, u % 3, 0:n], bank[u % 3][:, 0:n], ACT.Exp,
                                           bias=mrow[:, u:u + 1]).then_inc(p_done, 1)
                        else:
                            s = bias[:, hd % BIAS_RING, t, :]
                            act.activation(s, s, ACT.Exp, scale=-1.0, bias=mrow[:, u:u + 1]).then_inc(p_done, 1)
                    if u >= ACT_LAG and (u - ACT_LAG) % 2 == 1:
                        copy(u - ACT_LAG)
                    g = (u - CTX_LAG) // (GH * NT) - 1
                    if u >= CTX_LAG and (u - CTX_LAG) % (GH * NT) == 0 and 0 <= g < NG - 1:
                        ctx_out(g)
                ctx_out(NG - 1)

            def gelu(b, f, func):
                for j in range(NF):
                    act.wait_ge(f1_psum, b * 24 + NF * f + j + 1 + CREDIT)
                    act.activation(gT[:, j, :], bank[2 + j % 4][:], func, bias=b1[f][:, j:j + 1]).then_inc(g_done, 1)

            act.wait_ge(load_a, 16 * LOADS_A)
            act.wait_ge(load_b, 16 * LOADS_B)
            act.wait_ge(setup_p, 3)
            act.wait_ge(setup_v, SETUP_V)
            act.wait_ge(ada_out, 16)
            with act.Fori(0, B) as b:
                feature_half(b, 0, norm_w[0])
                qk_parts(b, 0)
                attention(b, 0)
                feature_half(b, 1, norm_w[1])
                gelu(b, 0, ACT.Gelu)
                feature_half(b, 2, None)
                act.wait_ge(ad_psum, b * 5 + 2)
                act.activation(aT[:], bank[2][0:A, :], ACT.Gelu, bias=down_b[:]).then_inc(ad_act, 1)
                act.wait_ge(ad_psum, b * 5 + 3)
                act.wait_ge(ad_wt, b * 2 + 2)
                act.activation(eT[0:A, :], bank[3][0:A, :], ACT.Identity, bias=exp_b[:, 2:3]).then_inc(ad_act, 1)
                feature_half(b, 3, None)
                act.wait_ge(par_in, b * 16 * PAR + 16 * PAR)
                gelu(b, 1, ACT.Gelu)
                feature_half(b, 4, None)
                qk_parts(b, 1)
                attention(b, 1)
                feature_half(b, 5, norm_w[2])
                gelu(b, 2, ACT.Gelu_apprx_sigmoid)

        @block.vector
        def _(v):
            n_setup = [0]

            def step(ins):
                n_setup[0] += 1
                ins.then_inc(setup_v, 1)
                v.wait_ge(setup_v, n_setup[0])

            v.wait_ge(setup_p, 1)
            r = lambda i: sin_t[:, i, :]
            step(v.tensor_scalar(r(2), r(0), 0.01, None, ALU.mult))
            step(v.scalar_tensor_tensor(out=r(3), in0=r(2), scalar=-64.0, in1=r(0), op0=ALU.mult, op1=ALU.add))
            step(v.scalar_tensor_tensor(out=r(4), in0=r(2), scalar=-32.0, in1=r(3), op0=ALU.mult, op1=ALU.add))
            step(v.scalar_tensor_tensor(out=r(5), in0=r(2), scalar=-4.0, in1=r(4), op0=ALU.mult, op1=ALU.add))
            step(v.scalar_tensor_tensor(out=r(1), in0=r(5), scalar=0.01, in1=r(2), op0=ALU.mult, op1=ALU.add))
            step(v.tensor_scalar(r(2), r(1), 4000.0, None, ALU.mult))
            step(v.tensor_scalar(r(3), r(2), freq, None, ALU.mult))
            for i, quarter in ((0, 0.0), (1, 0.25)):
                step(v.tensor_scalar(r(4), r(3), 1.0 / TWO_PI, quarter, ALU.mult, ALU.add))
                step(v.tensor_scalar(r(5), r(4), ROUND, None, ALU.add))
                step(v.tensor_scalar(r(6), r(5), ROUND, None, ALU.subtract))
                step(v.scalar_tensor_tensor(out=r(7), in0=r(6), scalar=-PI_HI, in1=r(3), op0=ALU.mult, op1=ALU.add))
                step(v.scalar_tensor_tensor(out=r(8), in0=r(6), scalar=-PI_MID, in1=r(7), op0=ALU.mult, op1=ALU.add))
                step(v.scalar_tensor_tensor(out=r(9), in0=r(6), scalar=-PI_LO, in1=r(8), op0=ALU.mult, op1=ALU.add))
                step(v.tensor_scalar(r(10), r(9), quarter * TWO_PI, PI_LIMIT, ALU.add, ALU.min))
                step(v.tensor_scalar(r(12 + i), r(10), -PI_LIMIT, None, ALU.max))
            assert n_setup[0] == SIN_READY
            v.wait_ge(setup_a, 2)
            step(v.tensor_scalar(sin_t[:, 18:20, :], sin_t[:, 16:18, :], 1.0, None, ALU.add))
            step(v.reciprocal(sin_t[:, 20:22, :], sin_t[:, 18:20, :]))
            step(v.tensor_tensor(sin_t[:, 22:24, :], sin_t[:, 20:22, :], sin_t[:, 14:16, :], ALU.mult))
            assert n_setup[0] == SILU_READY
            v.wait_ge(setup_t, 1)
            step(v.tensor_tensor(ada4, bank[0][0:B, :], b_ada, ALU.add))
            step(v.tensor_scalar(ada4[:, 0:D], ada4[:, 0:D], 1.0, None, ALU.add))
            v.wait_ge(setup_t, 2)
            step(v.tensor_copy(down_t[:], bank[1][:, 0:ND * A].rearrange("p (c a) -> p c a", a=A)))
            step(v.tensor_copy(up_t[0:A, :], bank[2][0:A, 0:D]))
            v.wait_ge(load_a, 16 * LOADS_A)
            step(v.tensor_scalar(wq[0][:], wq[0][:], 0.25, None, ALU.mult))
            step(v.tensor_scalar(bqk[0][:, 0:4:2], bqk[0][:, 0:4:2], 0.25, None, ALU.mult))
            assert n_setup[0] == SETUP_V

            count = [0]

            def link(ins):
                count[0] += 1
                ins.then_inc(vec, 1)
                v.wait_ge(vec, base_vec + count[0])

            def norm_stats(src, eps):
                for t in range(NT):
                    count[0] += 1
                    v.bn_stats(stats[:, t, :], src[:, t, :]).then_inc(vec, 1)
                v.wait_ge(vec, base_vec + count[0])
                alone(v)
                for t in range(NT):
                    count[0] += 1
                    v.bn_aggr(mv[:, t, :], stats[:, t, :]).then_inc(vec, 1)
                v.wait_ge(vec, base_vec + count[0])
                var, bits, guess, sq = nwt[:, 0, :], nwt[:, 1, :], rstd[:], nwt[:, 2, :]
                link(v.tensor_scalar(var, mv[:, :, 1], eps, None, ALU.add))
                link(v.tensor_scalar(bits.bitcast(I32), var.bitcast(I32), 1, None, ALU.logical_shift_right))
                link(v.tensor_scalar(guess.bitcast(I32), bits.bitcast(I32), -1.0, RSQRT_MAGIC, ALU.mult, ALU.add))
                for _ in range(3):
                    link(v.tensor_tensor(sq, guess, guess, ALU.mult))
                    link(v.scalar_tensor_tensor(out=bits, in0=sq, scalar=-0.5, in1=var, op0=ALU.mult, op1=ALU.mult))
                    link(v.scalar_tensor_tensor(out=guess, in0=bits, scalar=1.5, in1=guess, op0=ALU.add, op1=ALU.mult))

            def norm_to_h(src):
                for t in range(NT):
                    v.tensor_scalar(h[:, t, :], src[:, t, :], mv[:, t, 0:1], rstd[:, t:t + 1],
                                    ALU.subtract, ALU.mult).then_inc(tok, 1)

            def norm_in_y(gamma, beta, done):
                first = count[0] + 1
                for t in range(NT):
                    count[0] += 1
                    v.scalar_tensor_tensor(out=y[:, t, :], in0=y[:, t, :], scalar=mv[:, t, 0:1], in1=gamma,
                                           op0=ALU.subtract, op1=ALU.mult).then_inc(vec, 1)
                for t in range(NT):
                    v.wait_ge(vec, base_vec + first + t)
                    ins = v.scalar_tensor_tensor(out=y[:, t, :], in0=y[:, t, :], scalar=rstd[:, t:t + 1], in1=beta,
                                                 op0=ALU.mult, op1=ALU.add)
                    ins.then_inc(done, 1)
                if done is vec:
                    count[0] += NT
                    v.wait_ge(vec, base_vec + count[0])

            def feature_half(b, k, w):
                v.wait_ge(t_psum, b * 6 + k + 1)
                if w is None:
                    v.tensor_copy(hT[:, 1, :], bank[1][:]).then_inc(hT_v, 1)
                else:
                    v.tensor_scalar(hT[:, 1, :], bank[1][:], w[:, 1:2], w[:, 3:4], ALU.mult, ALU.add).then_inc(hT_v, 1)

            def qk_parts(b, l):
                def lo(i):
                    v.wait_ge(mid_done, b * 8 + 4 * l + i + 1)
                    v.tensor_tensor(parts[i % 2][:, 2, :], rest[i % 2][:], parts[i % 2][:, 1, :],
                                    ALU.subtract).then_inc(lo_done, 1)

                for i in range(4):
                    v.wait_ge(hi_done, b * 8 + 4 * l + i + 1)
                    v.scalar_tensor_tensor(out=rest[i % 2][:], in0=bank[2 + i][:], scalar=bqk[l][:, i:i + 1],
                                           in1=parts[i % 2][:, 0, :], op0=ALU.add, op1=ALU.subtract).then_inc(rest_done, 1)
                    if i >= 1:
                        lo(i - 1)
                lo(3)
                for t in range(NT):
                    v.wait_ge(v_psum, b * 4 + 2 * l + t // 2 + 1)
                    v.tensor_tensor(va[:, t, :, 0:DH],
                                    bank[6 + t // 2][:, (t % 2) * D:(t % 2 + 1) * D].rearrange("p (h d) -> p h d", d=DH),
                                    bv[l][:].rearrange("p (h d) -> p h d", d=DH), ALU.add).then_inc(v_done, 1)

            def attention(b, l):
                def copy(u):
                    hd, t = divmod(u, NT)
                    n = (t + 1) * P if l == 0 else S
                    v.wait_ge(pt_psum, b * 128 + UNITS * l + u + 1 + CREDIT)
                    if hd >= PT_RING and t < 2:
                        v.wait_ge(ctx_psum, b * 8 + NG * l + (hd - PT_RING) // GH + 1)
                    v.tensor_copy(pT[:, hd % PT_RING, 0:n // P, t * P:(t + 1) * P],
                                  bank[3 + u % 3][:, 0:n].rearrange("p (k q) -> p k q", q=P)).then_inc(pt_v, 1)

                def normalize(g):
                    v.wait_ge(sum_psum, b * 8 + NG * l + g + 1)
                    link(v.reciprocal(rsum[:], bank[7][:]))
                    v.tensor_tensor(ctxn[:, g, :], ctxu[:], rsum[:], ALU.mult).then_inc(ctx_norm, 1)

                for u in range(UNITS + VEC_LAG):
                    if u < UNITS:
                        hd, t = divmod(u, NT)
                        n = (t + 1) * P if l == 0 else S
                        v.wait_ge(s_psum, b * 128 + UNITS * l + u + 1)
                        if l == 0:
                            v.tensor_reduce(mrow[:, u:u + 1], bank[u % 3][:, 0:n], AX_X, ALU.max,
                                            negate=True).then_inc(max_done, 1)
                        else:
                            if t == 0:
                                slot = hd % BIAS_RING
                                v.wait_ge(bias_in[slot], b * 16 * BIAS_PER[slot] + 16 * (hd // BIAS_RING + 1))
                            alone(v)
                            s = bias[:, hd % BIAS_RING, t, :]
                            v.tensor_tensor_reduce(out=s, in0=bank[u % 3][:], in1=s, scale=-1.0, scalar=3e38,
                                                   op0=ALU.add, op1=ALU.min,
                                                   accum_out=mrow[:, u:u + 1]).then_inc(max_done, 1)
                    if u >= VEC_LAG and (u - VEC_LAG) % 2 == 0:
                        copy(u - VEC_LAG)
                    g = (u - SUM_LAG) // (GH * NT) - 1
                    if u >= SUM_LAG and (u - SUM_LAG) % (GH * NT) == 0 and 0 <= g < NG - 1:
                        normalize(g)
                normalize(NG - 1)

            def project(b, l, res):
                if l == 0:
                    v.wait_ge(x1_free, b + CREDIT)
                for i in range(2):
                    v.wait_ge(wo_psum, b * 4 + 2 * l + i + 1)
                    link(v.tensor_tensor(x1[:, 2 * i:2 * i + 2, :], bank[i][:].rearrange("p (t d) -> p t d", d=D),
                                         res[:, 2 * i:2 * i + 2, :], ALU.add))

            v.wait_ge(load_b, 16 * LOADS_B)
            v.wait_ge(ada_out, 16)
            with v.Fori(0, B) as b:
                base_vec = b * VEC
                v.wait_ge(x_in, b * 16 + 16)
                norm_stats(xin, 1e-5)
                norm_to_h(xin)
                feature_half(b, 0, norm_w[0])
                qk_parts(b, 0)
                attention(b, 0)
                project(b, 0, xin)
                norm_stats(x1, 1e-5)
                norm_to_h(x1)
                feature_half(b, 1, norm_w[1])
                v.wait_ge(res_pool, b * 4 + 2)
                for i in range(2):
                    v.wait_ge(f2_psum, b * 6 + i + 1 + CREDIT)
                    link(v.tensor_tensor(x1[:, 2 * i:2 * i + 2, :], bank[6 + i][:].rearrange("p (t d) -> p t d", d=D),
                                         x1[:, 2 * i:2 * i + 2, :], ALU.add))
                    for t in (2 * i, 2 * i + 1):
                        v.scalar_tensor_tensor(out=y[:, t, :], in0=x1[:, t, :], scalar=gate[:, bass.ds(b, 1)],
                                               in1=xin[:, t, :], op0=ALU.mult, op1=ALU.add).then_inc(tok, 1)
                feature_half(b, 2, None)
                v.wait_ge(ad_psum, b * 5 + 1)
                v.tensor_copy(exp_wt[:], bank[4][0:A, 0:A]).then_inc(ad_wt, 1)
                v.wait_ge(par_in, b * 16 * PAR + 16 * PAR)
                v.tensor_tensor(exp_b[:, 2:3], exp_b[:, 0:1], exp_b[:, 1:2], ALU.add).then_inc(ad_wt, 1)
                for i in range(2):
                    v.wait_ge(ad_psum, b * 5 + 4 + i)
                    link(v.tensor_tensor(y[:, 2 * i:2 * i + 2, :], bank[6 + i][:].rearrange("p (t d) -> p t d", d=D),
                                         y[:, 2 * i:2 * i + 2, :], ALU.add))
                norm_stats(y, 1e-5)
                norm_in_y(ln1[:, 0, :], ln1[:, 1, :], tok)
                feature_half(b, 3, None)
                v.wait_ge(res_pool, b * 4 + 3)
                for i in range(2):
                    v.wait_ge(f2_psum, b * 6 + 2 + i + 1 + CREDIT)
                    link(v.tensor_tensor(y[:, 2 * i:2 * i + 2, :], bank[6 + i][:].rearrange("p (t d) -> p t d", d=D),
                                         y[:, 2 * i:2 * i + 2, :], ALU.add))
                norm_stats(y, 1e-12)
                norm_in_y(l2row[:, 1, :], l2row[:, 2, :], vec)
                norm_stats(y, 1e-5)
                norm_in_y(ada[:, 0:D], ada[:, D:2 * D], tok)
                feature_half(b, 4, None)
                qk_parts(b, 1)
                attention(b, 1)
                project(b, 1, y)
                norm_stats(x1, 1e-5)
                norm_to_h(x1)
                feature_half(b, 5, norm_w[2])
                v.wait_ge(res_pool, b * 4 + 4)
                for i in range(2):
                    v.wait_ge(f2_psum, b * 6 + 4 + i + 1 + CREDIT)
                    v.tensor_tensor(x1[:, 2 * i:2 * i + 2, :], bank[6 + i][:].rearrange("p (t d) -> p t d", d=D),
                                    x1[:, 2 * i:2 * i + 2, :], ALU.add).then_inc(fin, 2)
                assert count[0] == VEC, (count[0], VEC)

        @block.tensor
        def _(pe):
            pe.wait_ge(consts, CONSTS)
            pe.wait_ge(load_b, 16 * LOADS_B)
            pe.wait_ge(setup_v, SILU_READY)
            for c in range(ND):
                mm = pe.matmul(bank[0][0:B, :], sin_t[:, 22 + c, :], w_ada[:, c, :], start=c == 0, stop=c == ND - 1)
            mm.then_inc(setup_t, 1)
            for c in range(ND):
                pe.transpose(bank[1][:, c * A:(c + 1) * A], down_raw[:, c * P:(c + 1) * P], ident[0:A, 0:A])
            for c in range(ND):
                mm = pe.transpose(bank[2][0:A, c * P:(c + 1) * P], up_raw[:, c, :], ident[:])
            mm.then_inc(setup_t, 1)

            def transposes(b, k, src):
                for t in range(NT):
                    pe.wait_ge(tok, b * 24 + NT * k + t + 1)
                    for c in range(ND):
                        mm = pe.transpose(bank[c][:, t * P:(t + 1) * P], src[:, t, c * P:(c + 1) * P], ident[:])
                mm.then_inc(t_psum, 1)

            def hT_ready(b, k):
                pe.wait_ge(hT_a, b * 6 + k + 1 + CREDIT)
                pe.wait_ge(hT_v, b * 6 + k + 1 + CREDIT)

            def qkv(b, l):
                for i in range(4):
                    w, c0 = (wk[l] if i % 2 else wq[l]), (i // 2) * P
                    for c in range(ND):
                        mm = pe.matmul(bank[2 + i][:], w[:, c, c0:c0 + P], hT[:, c, :], start=c == 0, stop=c == ND - 1)
                    mm.then_inc(qk_psum, 1)
                if l == 0:
                    pe.wait_ge(fin, NT * b + CREDIT)
                for t in range(NT):
                    for c in range(ND):
                        mm = pe.matmul(bank[6 + t // 2][:, (t % 2) * D:(t % 2 + 1) * D], hT[:, c, t * P:(t + 1) * P],
                                       wv[l][:, c, :], start=c == 0, stop=c == ND - 1)
                    if t % 2:
                        mm.then_inc(v_psum, 1)

            def attention(b, l):
                def scores(u):
                    hd, t = divmod(u, NT)
                    n = (t + 1) * P if l == 0 else S
                    if t == 0 and hd % HH == 0:
                        pe.wait_ge(stack_in[hd // HH], b * (2 * 96) + 96 * (l + 1))
                    if u >= 3:
                        pe.wait_ge(p_done if l == 0 else max_done, b * 128 + UNITS * l + u - 2)
                    if l == 1 and u == 0:
                        pe.wait_ge(mask_done, b + 1)
                    pe.matmul(bank[u % 3][:, 0:n], qs[:, hd, t * P:(t + 1) * P], ks[:, hd, 0:n], start=True, stop=False)
                    if l == 0:
                        mm = pe.matmul(bank[u % 3][:, n - P:n], identb[:], causal[:], start=False, stop=True)
                    else:
                        mm = pe.matmul(bank[u % 3][:], identb[:], negmask[:, t, :], start=False, stop=True)
                    mm.then_inc(s_psum, 1)

                def copies(u):
                    pe.wait_ge(pt_v, b * 64 + 32 * l + (u + 1) // 2)
                    if u // 2:
                        pe.wait_ge(pt_a, b * 64 + 32 * l + u // 2)

                def turn(u):
                    hd, t = divmod(u, NT)
                    pe.wait_ge(p_done, b * 128 + UNITS * l + u + 1)
                    if u == 0:
                        pe.wait_ge(hi_done, b * 8 + 4 * l + 4)
                        pe.wait_ge(rest_done, b * 8 + 4 * l + 4)
                    if u >= 3:
                        copies(u - 2)
                    src = prob[:, u % 3] if l == 0 else bias[:, hd % BIAS_RING, t]
                    for k in range(t + 1 if l == 0 else NT):
                        mm = pe.transpose(bank[3 + u % 3][:, k * P:(k + 1) * P], src[:, k * P:(k + 1) * P], ident[:])
                    mm.then_inc(pt_psum, 1)

                def values(g):
                    copies(GH * NT * (g + 1))
                    if g == 0:
                        pe.wait_ge(v_done, b * 8 + 4 * l + 4)
                    else:
                        pe.wait_ge(ctx_copy, b * 8 + NG * l + g)
                    for k in range(NT):
                        q0 = k * P if l == 0 else 0
                        for j in range(GH):
                            hd = GH * g + j
                            mm = pe.matmul(bank[6][32 * j:32 * (j + 1), q0:S], va[:, k, hd, :],
                                           pT[:, hd % PT_RING, k, q0:S], start=k == 0, stop=k == NT - 1)
                    mm.then_inc(ctx_psum, 1)

                def sums(g):
                    pe.wait_ge(ctx_copy, b * 8 + NG * l + g + 1)
                    if g:
                        pe.wait_ge(ctx_norm, b * 8 + NG * l + g)
                    pe.matmul(bank[7][:], sumrow[:], ctxu[:], start=True, stop=True).then_inc(sum_psum, 1)

                for u in range(UNITS + PE_LAG):
                    if u < UNITS:
                        scores(u)
                    if u >= PE_LAG:
                        w = u - PE_LAG
                        turn(w)
                        if w >= GH * NT and w % (GH * NT) == VALUES_AT:
                            values(w // (GH * NT) - 1)
                        if w >= GH * NT and w % (GH * NT) == SUMS_AT:
                            sums(w // (GH * NT) - 1)
                values(NG - 1)
                sums(NG - 1)
                pe.wait_ge(ctx_norm, b * 8 + NG * l + NG)
                for t in range(NT):
                    for g in range(NG):
                        mm = pe.matmul(bank[t // 2][:, (t % 2) * D:(t % 2 + 1) * D], ctxn[:, g, t * P:(t + 1) * P],
                                       wo[l][:, g, :], start=g == 0, stop=g == NG - 1)
                    if t % 2:
                        mm.then_inc(wo_psum, 1)

            def feed_forward(b, f):
                pe.wait_ge(w1_in, b * 48 + 16 * (f + 1))
                for j in range(NF):
                    if j >= 4:
                        pe.wait_ge(g_done, b * 24 + NF * f + j - 3)
                    for c in range(ND):
                        mm = pe.matmul(bank[2 + j % 4][:], w1[:, c, j * P:(j + 1) * P], hT[:, c, :],
                                       start=c == 0, stop=c == ND - 1)
                    mm.then_inc(f1_psum, 1)
                pe.wait_ge(w2_in, b * 48 + 16 * (f + 1))
                for t in range(NT):
                    for j in range(NF):
                        if t == 0:
                            pe.wait_ge(g_done, b * 24 + NF * f + j + 1)
                        mm = pe.matmul(bank[6 + t // 2][:, (t % 2) * D:(t % 2 + 1) * D], gT[:, j, t * P:(t + 1) * P],
                                       w2[:, j, :], start=j == 0, stop=j == NF - 1)
                    if t % 2:
                        mm.then_inc(f2_psum, 1)

            pe.wait_ge(load_a, 16 * LOADS_A)
            pe.wait_ge(setup_v, SETUP_V)
            pe.wait_ge(setup_p, 3)
            with pe.Fori(0, B) as b:
                transposes(b, 0, h)
                hT_ready(b, 0)
                qkv(b, 0)
                attention(b, 0)
                transposes(b, 1, h)
                hT_ready(b, 1)
                feed_forward(b, 0)
                pe.wait_ge(par_in, b * 16 * PAR + 16 * PAR)
                alone(pe)
                pe.transpose(bank[4][0:A, 0:A], exp_w[:], ident[0:A, 0:A]).then_inc(ad_psum, 1)
                transposes(b, 2, y)
                hT_ready(b, 2)
                for c in range(ND):
                    mm = pe.matmul(bank[2][0:A, :], down_t[:, c, :], hT[:, c, :], start=c == 0, stop=c == ND - 1)
                mm.then_inc(ad_psum, 1)
                pe.wait_ge(ad_act, b * 2 + 1)
                pe.wait_ge(ad_wt, b * 2 + 1)
                alone(pe)
                pe.matmul(bank[3][0:A, :], exp_wt[:], aT[:], start=True, stop=True).then_inc(ad_psum, 1)
                pe.wait_ge(ad_act, b * 2 + 2)
                for t in range(NT):
                    mm = pe.matmul(bank[6 + t // 2][:, (t % 2) * D:(t % 2 + 1) * D], eT[:, t * P:(t + 1) * P], up_t[:],
                                   start=True, stop=True)
                    if t % 2:
                        mm.then_inc(ad_psum, 1)
                transposes(b, 3, y)
                hT_ready(b, 3)
                feed_forward(b, 1)
                transposes(b, 4, y)
                hT_ready(b, 4)
                qkv(b, 1)
                attention(b, 1)
                transposes(b, 5, h)
                hT_ready(b, 5)
                feed_forward(b, 2)


LOADS_A = 12
LOADS_B = 9 + 2 * 7 + 6 + 3 + 4 + 1
CONSTS = 13
CREDIT = 1
SIN_READY = 5 + 2 + 2 * 8
SILU_READY = SIN_READY + 3
SETUP_V = SILU_READY + 2 + 2 + 2
BIAS_PER = [len(range(s, H, BIAS_RING)) for s in range(BIAS_RING)]
ACT_LAG = 3
VEC_LAG = 4
PE_LAG = 2
VALUES_AT = 4
SUMS_AT = 8
CTX_LAG = 8
SUM_LAG = 12

_NAMES = ["x", "condB_gatescore", "itok_B_0_15", "itok_B_0_7", "itok_B_34_63", "fside_Bx16xSxS_0", "mask_Bx1xSxS_bk0"]
_NAMES += ["L0_cond_" + n for n in "Wq bq Wk bk Wv bv Wo bo W1 b1 W2 b2 gamma1 beta1 gamma2 beta2".split()]
_NAMES += ["L1_cond_" + n for n in "down_W down_b up_W up_b expert_W expert_b domain_emb ln_gamma ln_beta".split()]
_NAMES += ["L2_cond_" + n for n in "Wi bi Wo bo gamma beta".split()]
_NAMES += ["L3_cond_" + n for n in "W_ada b_ada Wq bq Wk bk Wv bv Wo bo W1 b1 W2 b2 g2 beta2".split()]


def kernel(**inputs):
    import math
    import numpy as np
    from concourse import bacc
    from concourse.bass_utils import run_bass_kernel_spmd

    nc = bacc.Bacc("TRN2", target_bir_lowering=False, num_devices=1)
    arrays = {}
    for name in _NAMES:
        a = np.ascontiguousarray(inputs[name])
        arrays[name] = a
    half = D // 2
    step = np.float32(-math.log(10000.0) / (half - 1))
    arrays["freqs"] = np.exp(np.arange(half, dtype=np.float32) * step).astype(np.float32)
    T = {n: nc.dram_tensor("in_" + n, a.shape, mybir.dt.from_np(a.dtype), kind="ExternalInput").ap()
         for n, a in arrays.items()}
    out = nc.dram_tensor("out_0", (B, S, D), F32, kind="ExternalOutput").ap()
    build(nc, T, out)
    r = run_bass_kernel_spmd(nc, [{"in_" + n: a for n, a in arrays.items()}], core_ids=[0])
    return r.results[0]["out_0"]
```

```python
from contextlib import ExitStack

import concourse.bass as bass
from concourse import mybir

P = 128
B, S, D, F = 4, 512, 256, 1024
H, DH = 16, 16
NT = S // P
ND = D // P
NF = F // P
A = 64
E16, E8 = 16, 8
GH = 4
NG = H // GH
HH = H // 2
UNITS = H * NT
QUADS = UNITS // GH
PT_RING = 8
ROW_RING = 16
BIAS_RING = 3
NEG = -1e30
PARTS_Q = 5
PARTS_K = 3
STACK = [(0, 2, 0, 0), (2, 3, 1, 0), (5, 3, 2, 0)]

ALU = mybir.AluOpType
ACT = mybir.ActivationFunctionType
AX_X = mybir.AxisListType.X
F32 = mybir.dt.float32
BF16 = mybir.dt.bfloat16
I32 = mybir.dt.int32
U8 = mybir.dt.uint8

TWO_PI = 6.283185307179586
PI_HI = 6.28125
PI_MID = round((TWO_PI - PI_HI) * 2 ** 23) / 2 ** 23
PI_LO = TWO_PI - PI_HI - PI_MID
PI_LIMIT = 3.1415925
ROUND = 12582912.0
RSQRT_MAGIC = 1597463007.0

ATTENTIONS = [(0, 0), (1, 0), (2, 0), (0, 1), (3, 0), (1, 1), (2, 1), (3, 1)]
ATT = {sl: a for a, sl in enumerate(ATTENTIONS)}
ALL_UNITS = UNITS * len(ATTENTIONS)
BIASED = {a: n for n, a in enumerate(a for a, (_, l) in enumerate(ATTENTIONS) if l == 1)}

TURN_LAG = 2
ACT_LAG = 3
VEC_LAG = 3
SUM_AT = 9
VALUES_AT = 7 + 2
SPREAD_AT = 13
SPREAD_COPY_AT = 14
NORM_AT = 15
OUT_AT = NORM_AT - 2 * GH + 1

EVENTS = []


def at(tick, engine, step, *args):
    EVENTS.append((tick, engine, step, args))


def plan_norm(t, s, k):
    at(t, "v", "stats", s, k, 0)
    at(t, "v", "stats", s, k, 1)
    at(t + 1, "v", "rsqrt", s, k, 0)
    at(t + 2, "v", "rsqrt", s, k, 1)
    if k in (3, 4, 5):
        at(t + 1, "v", "apply", s, k, 0)
        at(t + 2, "v", "apply", s, k, 1)
        at(t + 3, "v", "apply_late", s, k, 0)
        at(t + 3, "v", "apply_late", s, k, 1)
    else:
        at(t + 3, "v", "apply", s, k, 0)
        at(t + 3, "v", "apply", s, k, 1)


def plan_turn(t, s, k):
    at(t, "pe", "turn_tokens", s, k)
    at(t + 1, "v", "feature_half", s, k)
    at(t + 1, "a", "feature_half", s, k)


def plan_qkv(t, s, l):
    at(t, "pe", "qk", s, l, 0)
    at(t, "pe", "qk", s, l, 1)
    at(t + 3, "pe", "qk", s, l, 2)
    at(t + 3, "pe", "qk", s, l, 3)
    for i in range(4):
        u = t + 1 + 3 * (i // 2)
        at(u, "a", "hi", s, l, i)
        at(u + 1, "v", "rest", s, l, i)
        at(u + 1, "a", "mid", s, l, i)
        at(u + 2, "v", "lo", s, l, i)
    at(t + 4, "pe", "v", s, l, 0)
    at(t + 6, "pe", "v", s, l, 1)
    at(t + 5, "v", "v", s, l, 0)
    at(t + 7, "v", "v", s, l, 1)


def plan_ffn(t, s, f):
    for j, (dt, da) in enumerate(zip((0, 0, 1, 2, 2, 4, 4, 4), (1, 1, 3, 3, 3, 5, 5, 5))):
        at(t + dt, "pe", "hidden", s, f, j)
        at(t + da, "a", "gelu", s, f, j)
    for i in range(NT):
        at(t + 6 + i, "pe", "ff_out", s, f, i)
    at(t + 8, "v", "ff_add", s, f, 0)
    at(t + 10, "v", "ff_add", s, f, 1)


def plan_out(t, s, l):
    for i in range(2):
        at(t + i, "pe", "project", s, l, i)
        at(t + i + 1, "v", "residual", s, l, i)


def plan_qkv0(t, s):
    plan_norm(t, s, 0)
    plan_turn(t + 4, s, 0)
    plan_qkv(t + 6, s, 0)


def plan_block0(t, s):
    plan_norm(t, s, 1)
    at(t + 3, "p", "res_l0", s)
    plan_turn(t + 4, s, 1)
    plan_ffn(t + 6, s, 0)
    t += 17
    at(t, "pe", "turn_expert", s)
    plan_turn(t, s, 2)
    at(t + 1, "v", "expert", s)
    at(t + 2, "pe", "down", s)
    at(t + 2, "a", "down", s)
    at(t + 3, "pe", "expert", s)
    at(t + 3, "a", "expert", s)
    at(t + 4, "pe", "up", s)
    at(t + 4, "v", "up_add", s, 0)
    at(t + 5, "v", "up_add", s, 1)


def plan_block2(t, s):
    plan_norm(t, s, 3)
    plan_turn(t + 4, s, 3)
    at(t + 5, "p", "res_l2", s)
    plan_ffn(t + 6, s, 1)
    plan_norm(t + 17, s, 4)


def plan_qkv3(t, s):
    plan_norm(t, s, 5)
    plan_turn(t + 4, s, 4)
    plan_qkv(t + 6, s, 1)


def plan_block3(t, s):
    plan_norm(t, s, 6)
    at(t + 3, "p", "res_l3", s)
    plan_turn(t + 4, s, 5)
    plan_ffn(t + 6, s, 2)
    at(t + 17, "a", "store", s)


BESIDE = [
    [(4, plan_qkv0, 1)],
    [(11, plan_block0, 0), (36, plan_qkv0, 2)],
    [(11, plan_block2, 0), (32, plan_qkv3, 0), (46, plan_block0, 1)],
    [(11, plan_block2, 1), (38, plan_qkv0, 3)],
    [(11, plan_block3, 0), (29, plan_qkv3, 1), (44, plan_block0, 2)],
    [(11, plan_block2, 2), (32, plan_qkv3, 2), (46, plan_block0, 3)],
    [(11, plan_block2, 3), (32, plan_qkv3, 3), (46, plan_block3, 1)],
    [(11, plan_block3, 2)],
    [(11, plan_block3, 3)],
]
plan_qkv0(-14, 0)
at(0, "v", "setup_angles")
at(0, "a", "setup_sin")
at(20, "v", "setup_silu")
at(21, "pe", "setup")
at(22, "v", "setup_weights")
for _a, _stages in enumerate(BESIDE):
    if _a:
        plan_out(UNITS * _a + OUT_AT, *ATTENTIONS[_a - 1])
    for _t, _plan, _s in _stages:
        _plan(UNITS * _a + _t, _s)
LAST = max(e[0] for e in EVENTS)
FIRST = min(e[0] for e in EVENTS)


def dense_steps(engine):
    steps = {}
    for t, e, step, args in EVENTS:
        if e == engine:
            steps.setdefault(t, []).append((step, args))
    return steps


def order(engine, step, key):
    found = sorted(((t, n, key(args)) for n, (t, e, st, args) in enumerate(EVENTS) if e == engine and st == step),
                   key=lambda x: x[:2])
    out = {}
    for _, _, k in found:
        out.setdefault(k, len(out))
    return out


TURN = order("pe", "turn_tokens", lambda a: a)
NTH = {(s, k): sum(1 for x in TURN if x[1] == k and TURN[x] < n) for (s, k), n in TURN.items()}
FFN = order("pe", "hidden", lambda a: a[:2])
QKV = order("pe", "qk", lambda a: a[:2])
OUTP = order("pe", "project", lambda a: a[:2])
QKV_BEFORE = {sf: sum(1 for t, e, st, a in EVENTS if e == "pe" and st == "qk" and a[2] == 0 and t < t0)
              for t0, sf in sorted((t, a[:2]) for t, e, st, a in EVENTS if e == "pe" and st == "hidden" and a[2] == 0)}
D2 = order("pe", "down", lambda a: a[0])
assert QKV == ATT and OUTP == ATT

LOADS_A = 12
LOADS_B = 9 + 2 * 7 + 6 + 3 + 4 + 1
PAR = 8
BIAS_TILES = QUADS * len(BIASED)


def build(nc, T, out):
    with ExitStack() as ctx:
        def sb(name, shape, dt=F32):
            return ctx.enter_context(nc.sbuf_tensor(name, shape, dt))

        def sem(name):
            return ctx.enter_context(nc.semaphore(name))

        ident = sb("ident", [P, P])
        causal = sb("causal", [P, P], BF16)
        identb = sb("identb", [P, P], BF16)
        wq = [sb(f"wq{l}", [P, ND, D]) for l in range(2)]
        wk = [sb(f"wk{l}", [P, ND, D]) for l in range(2)]
        wv = [sb(f"wv{l}", [P, ND, D]) for l in range(2)]
        wo = [sb(f"wo{l}", [P, NG, D]) for l in range(2)]
        bqk = [sb(f"bqk{l}", [P, 4]) for l in range(2)]
        bv = [sb(f"bv{l}", [P, D]) for l in range(2)]
        bo = [sb(f"bo{l}", [P, D]) for l in range(2)]
        b2 = [sb(f"b2_{l}", [P, D]) for l in range(2)]
        b1 = [sb(f"b1_{l}", [P, NF]) for l in range(3)]
        norm_w = [sb(f"norm_w{l}", [P, 4]) for l in range(3)]
        w1 = sb("w1", [P, ND, F])
        w2 = sb("w2", [P, NF, D])
        down_t = sb("down_t", [P, ND, A])
        up_t = sb("up_t", [A + 1, D])
        down_b = sb("down_b", [A, 1])
        ln1 = sb("ln1", [P, 2, D])
        exp_w = sb("exp_w", [A, A])
        exp_wt = sb("exp_wt", [A, A])
        exp_b = sb("exp_b", [A, 3])
        l2row = sb("l2row", [P, 3, D])
        ada = sb("ada", [P, 2 * D])
        gate = sb("gate", [P, B])
        idx = sb("idx", [1, 2 * B], I32)

        xy = [sb(f"xy{i}", [P, NT, D]) for i in range(B)]
        x1 = sb("x1", [P, NT, D])
        h = sb("h", [P, NT, D])
        hT = sb("hT", [P, ND, S])
        qs = sb("qs", [P, H, S], BF16)
        ks = sb("ks", [P, H, S], BF16)
        va = [sb(f"va{i}", [P, NT, H, 32]) for i in range(2)]
        pT = sb("pT", [P, PT_RING, NT, P])
        gT = sb("gT", [P, NF, S])
        bias = sb("bias", [P, BIAS_RING, GH, S])
        prob = sb("prob", [P, 3, S])
        mrow = sb("mrow", [P, ROW_RING])
        rsum = sb("rsum", [P, ROW_RING])
        rinv = sb("rinv", [P, 2 * GH])
        rwide = sb("rwide", [P, 2, P])
        negmask = sb("negmask", [P, NT, S], BF16)
        maskraw = sb("maskraw", [P, 2, S], U8)
        spread = sb("spread", [P, 2 * P])
        ctxn = sb("ctxn", [P, NG, S])
        parts = [gT[:, 0:3, :].rearrange("p n t -> p (n t)").bitcast(BF16)[:, 3 * S * i:3 * S * (i + 1)]
                 .rearrange("p (n t) -> p n t", t=S) for i in range(2)]
        rest = [gT[:, 6 + i, :] for i in range(2)]
        aT = gT[0:A, 0, :]
        eT = sb("eT", [A + 1, S])
        stats = sb("stats", [P, NT, 6])
        mv = sb("mv", [P, NT, 2])
        rstd = sb("rstd", [P, NT])
        nwt = sb("nwt", [P, 3, NT])

        scratch = bias[:].rearrange("p r h k -> p (r h) k")
        w_ada = scratch[:, 0:2, :]
        b_ada = scratch[0:B, 2, :]
        ada4 = scratch[0:B, 3, :]
        down_raw = scratch[0:A, 4, 0:D]
        up_raw = scratch[:, 4, D:D + ND * A].rearrange("p (c a) -> p c a", a=A)
        sin_t = scratch[:, 5, 0:96].rearrange("p (n b) -> p n b", b=B)
        tok_i = scratch[:, 5, 96:96 + B].bitcast(I32)
        freq = scratch[:, 5, 104:105]

        q_dram = nc.dram_tensor("q_parts", (H, PARTS_Q, DH, S), BF16).ap()
        k_dram = nc.dram_tensor("k_parts", (H, PARTS_K, DH, S), BF16).ap()
        ada_dram = nc.dram_tensor("ada_rows", (B, 2 * D), F32).ap()

        bank = [ctx.enter_context(nc.psum_tensor(f"bank{i}", [P, S], F32)) for i in range(8)]
        score_bank, turn_bank, ctx_bank, dense_bank = bank[0:2], bank[2:4], bank[4], bank[5:8]

        load_a = sem("load_a")
        load_b = sem("load_b")
        consts = sem("consts")
        setup_v = sem("setup_v")
        setup_p = sem("setup_p")
        setup_a = sem("setup_a")
        setup_t = sem("setup_t")
        ada_out = sem("ada_out")
        x_in = [sem(f"x_in{s}") for s in range(B)]
        par_in = sem("par_in")
        mask_in = [sem(f"mask_in{i}") for i in range(2)]
        mask_neg = sem("mask_neg")
        w1_in = sem("w1_in")
        w2_in = sem("w2_in")
        bias_in = [sem(f"bias_in{i}") for i in range(BIAS_RING)]
        masked = sem("masked")
        tok = [sem(f"tok{k}") for k in range(6)]
        t_psum = sem("t_psum")
        hT_a = sem("hT_a")
        hT_v = sem("hT_v")
        qk_psum = sem("qk_psum")
        v_psum = sem("v_psum")
        hi_done = sem("hi_done")
        rest_done = sem("rest_done")
        mid_done = sem("mid_done")
        lo_done = sem("lo_done")
        parts_out = [sem(f"parts_out{i}") for i in range(4)]
        stack_in = [sem(f"stack_in{i}") for i in range(2)]
        v_done = sem("v_done")
        s_psum = sem("s_psum")
        max_done = sem("max_done")
        p_done = sem("p_done")
        pt_psum = sem("pt_psum")
        pt_a = sem("pt_a")
        pt_v = sem("pt_v")
        inv_done = sem("inv_done")
        ctx_psum = sem("ctx_psum")
        spread_psum = sem("spread_psum")
        spread_done = sem("spread_done")
        ctx_norm = sem("ctx_norm")
        wo_psum = sem("wo_psum")
        wo_done = sem("wo_done")
        f1_psum = sem("f1_psum")
        g_done = sem("g_done")
        f2_psum = sem("f2_psum")
        ff_done = sem("ff_done")
        res_pool = sem("res_pool")
        ad_psum = sem("ad_psum")
        ad_act = sem("ad_act")
        ad_wt = sem("ad_wt")
        vec = sem("vec")
        stored = sem("stored")

        ctx.enter_context(nc.allow_non_contiguous_dma(reason="vectors of a few hundred elements, features on the partitions"))
        block = ctx.enter_context(nc.Block())

        def unit(U):
            a, u = divmod(U, UNITS)
            l = ATTENTIONS[a][1]
            g, t, j = u // (NT * GH), u // GH % NT, u % GH
            return a, l, g, t, j, GH * g + j, (t + 1) * P if l == 0 else S

        def bias_tile(U):
            return BIASED[U // UNITS] * QUADS + U % UNITS // GH

        def prob_of(U):
            _, l, _, _, j, _, n = unit(U)
            return prob[:, U % 3, 0:n] if l == 0 else bias[:, bias_tile(U) % BIAS_RING, j, :]

        def res_count(s, layer):
            name, n = {0: ("res_l0", 2), 2: ("res_l2", 1), 3: ("res_l3", 1)}[layer]
            total = 0
            for _, _, step, args in sorted((t, i, st, a) for i, (t, e, st, a) in enumerate(EVENTS)
                                           if e == "p" and st.startswith("res")):
                total += 2 if step == "res_l0" else 1
                if step == name and args[0] == s:
                    return total

        def load_bias(eng, n):
            a = [x for x in BIASED if BIASED[x] == n // QUADS][0]
            g, t = divmod(n % QUADS, NT)
            src = T["fside_Bx16xSxS_0"][ATTENTIONS[a][0], g * GH:(g + 1) * GH, t * P:(t + 1) * P, :]
            eng.dma_start(bias[:, n % BIAS_RING, :, :], src.rearrange("h p k -> p h k")).then_inc(bias_in[n % BIAS_RING], 16)

        @block.sync
        def _(sp):
            sp.dma_start(xy[0][:], T["x"][0].rearrange("(t p) d -> p t d", p=P)).then_inc(x_in[0], 16)
            sp.dma_start(norm_w[0][:, 0:2], T["L0_cond_gamma1"].rearrange("(c p) -> p c", p=P)).then_inc(load_a, 16)
            sp.dma_start(norm_w[0][:, 2:4], T["L0_cond_beta1"].rearrange("(c p) -> p c", p=P)).then_inc(load_a, 16)
            sp.dma_start(wq[0][:], T["L0_cond_Wq"].rearrange("(c p) n -> p c n", p=P)).then_inc(load_a, 16)
            sp.dma_start(wk[0][:], T["L0_cond_Wk"].rearrange("(c p) n -> p c n", p=P)).then_inc(load_a, 16)
            for c in range(2):
                sp.dma_start(bqk[0][:, 2 * c:2 * c + 1], T["L0_cond_bq"][c * P:(c + 1) * P].unsqueeze(1)).then_inc(load_a, 16)
                sp.dma_start(bqk[0][:, 2 * c + 1:2 * c + 2], T["L0_cond_bk"][c * P:(c + 1) * P].unsqueeze(1)).then_inc(load_a, 16)
            sp.dma_start(wv[0][:], T["L0_cond_Wv"].rearrange("(c p) n -> p c n", p=P)).then_inc(load_a, 16)
            sp.dma_start(bv[0][:], T["L0_cond_bv"].partition_broadcast(P)).then_inc(load_a, 16)
            sp.dma_start(idx[:, 0:B], T["itok_B_0_15"].unsqueeze(0)).then_inc(load_a, 16)
            sp.dma_start(idx[:, B:2 * B], T["itok_B_0_7"].unsqueeze(0)).then_inc(load_a, 16)
            for s in range(1, B):
                sp.dma_start(xy[s][:], T["x"][s].rearrange("(t p) d -> p t d", p=P)).then_inc(x_in[s], 16)

            def weights(n, w1_src, w2_src):
                if n:
                    sp.wait_ge(f1_psum, NF * n)
                sp.dma_start(w1[:], w1_src.rearrange("(c p) n -> p c n", p=P)).then_inc(w1_in, 16)
                if n:
                    sp.wait_ge(f2_psum, 2 * n)
                sp.dma_start(w2[:], w2_src.rearrange("(c p) n -> p c n", p=P)).then_inc(w2_in, 16)

            def stacks(s, l):
                a = ATT[s, l]
                for c in range(2):
                    hs = slice(c * HH, (c + 1) * HH)
                    if a:
                        sp.wait_ge(stack_in[c], 96 * a)
                    for i in (2 * c, 2 * c + 1):
                        sp.wait_ge(lo_done, 4 * a + i + 1)
                        dram, n = (k_dram, PARTS_K) if i % 2 else (q_dram, PARTS_Q)
                        for j in range(n):
                            sp.dma_start(dram[hs, j].rearrange("h d t -> h (d t)"),
                                         parts[i % 2][:, j % 3, :]).then_inc(parts_out[i], 16)
                    sp.wait_ge(parts_out[2 * c], 16 * PARTS_Q * (a + 1))
                    sp.wait_ge(parts_out[2 * c + 1], 16 * PARTS_K * (a + 1))
                    if a:
                        sp.wait_ge(s_psum, UNITS * (a - 1) + UNITS // 2 * (c + 1))
                    for r, k, q0, k0 in STACK:
                        rows = slice(r * DH, (r + k) * DH)
                        sp.dma_start(qs[rows, hs, :],
                                     q_dram[hs, q0:q0 + k].rearrange("h p d t -> (p d) h t")).then_inc(stack_in[c], 16)
                        sp.dma_start(ks[rows, hs, :],
                                     k_dram[hs, k0:k0 + k].rearrange("h p d t -> (p d) h t")).then_inc(stack_in[c], 16)

            def picked(s):
                if D2[s]:
                    last = [x for x in D2 if D2[x] == D2[s] - 1][0]
                    sp.wait_ge(hT_a, TURN[last, 4] + 1)
                    sp.wait_ge(hT_v, TURN[last, 4] + 1)
                e16 = sp.value_load(idx[0:1, s:s + 1], min_val=0, max_val=E16 - 1)
                e8 = sp.value_load(idx[0:1, B + s:B + s + 1], min_val=0, max_val=E8 - 1)
                sp.dma_start(exp_w[:], T["L1_cond_expert_W"][bass.ds(e16, 1)].rearrange("a o i -> (a o) i")).then_inc(par_in, 16)
                sp.dma_start(exp_b[:, 0:1], T["L1_cond_expert_b"][bass.ds(e16, 1)].rearrange("a o -> o a")).then_inc(par_in, 16)
                sp.dma_start(exp_b[:, 1:2], T["L1_cond_domain_emb"][bass.ds(e16, 1)].rearrange("a o -> o a")).then_inc(par_in, 16)
                sp.dma_start(b1[1][:], T["L2_cond_bi"][bass.ds(e8, 1)].rearrange("a (j p) -> p (a j)", p=P)).then_inc(par_in, 16)
                for j, name in enumerate(["L2_cond_bo", "L2_cond_gamma", "L2_cond_beta"]):
                    sp.dma_start(l2row[:, j, :], T[name][bass.ds(e8, 1)].rearrange("a d -> (a d)").partition_broadcast(P)).then_inc(par_in, 16)
                if not D2[s]:
                    sp.wait_ge(ada_out, 16)
                sp.dma_start(ada[:], ada_dram[s].partition_broadcast(P)).then_inc(par_in, 16)

            def layer_0(s):
                weights(FFN[s, 0], T["L0_cond_W1"], T["L0_cond_W2"])

            def layer_2(s):
                e8 = sp.value_load(idx[0:1, B + s:B + s + 1], min_val=0, max_val=E8 - 1)
                weights(FFN[s, 1], T["L2_cond_Wi"][bass.ds(e8, 1)].rearrange("a d f -> (a d) f"),
                        T["L2_cond_Wo"][bass.ds(e8, 1)].rearrange("a d f -> (a d) f"))

            def layer_3(s):
                weights(FFN[s, 2], T["L3_cond_W1"], T["L3_cond_W2"])

            sp.wait_ge(load_a, 16 * LOADS_A)
            stacks(0, 0)
            layer_0(0)
            stacks(1, 0)
            picked(0)
            sp.wait_ge(setup_v, SETUP_V)
            for n in range(BIAS_RING):
                load_bias(sp, n)
            layer_2(0)
            stacks(2, 0)
            layer_0(1)
            picked(1)
            stacks(0, 1)
            layer_2(1)
            layer_3(0)
            stacks(3, 0)
            layer_0(2)
            picked(2)
            stacks(1, 1)
            layer_2(2)
            layer_0(3)
            picked(3)
            stacks(2, 1)
            layer_2(3)
            layer_3(1)
            stacks(3, 1)
            layer_3(2)
            layer_3(3)

        @block.gpsimd
        def _(pool):
            n_const = [0]

            def const(ins):
                n_const[0] += 1
                ins.then_inc(consts, 1)
                pool.wait_ge(consts, n_const[0])

            const(pool.memset(ident[:], 0.0))
            const(pool.affine_select(out=ident[:], in_=ident[:], compare_op=ALU.not_equal, fill=1.0, base=0,
                                     pattern=[[-1, P]], channel_multiplier=1))
            for l in range(2):
                const(pool.memset(wo[l][:], 0.0))
            assert n_const[0] == CONST_WO

            def late(dst, src):
                pool.dma_start(dst, src).then_inc(load_b, 16)

            late(tok_i, T["itok_B_34_63"].partition_broadcast(P))
            late(freq, T["freqs"].unsqueeze(1))
            const(pool.memset(identb[:], 0.0))
            const(pool.affine_select(out=identb[:], in_=identb[:], compare_op=ALU.not_equal, fill=1.0, base=0,
                                     pattern=[[-1, P]], channel_multiplier=1))
            const(pool.memset(causal[:], 0.0))
            const(pool.affine_select(out=causal[:], in_=causal[:], compare_op=ALU.is_ge, fill=NEG, base=0,
                                     pattern=[[-1, P]], channel_multiplier=1))
            const(pool.memset(va[0][:], 0.0))
            const(pool.memset(va[1][:], 0.0))
            const(pool.memset(eT[A:A + 1, :], 1.0))
            assert n_const[0] == CONSTS
            late(w_ada, T["L3_cond_W_ada"].rearrange("(c p) n -> p c n", p=P))
            late(b_ada, T["L3_cond_b_ada"].partition_broadcast(B))
            late(down_raw, T["L1_cond_down_W"])
            late(up_raw, T["L1_cond_up_W"].rearrange("(c p) a -> p c a", p=P))
            late(up_t[A:A + 1, :], T["L1_cond_up_b"].unsqueeze(0))
            late(down_b[:], T["L1_cond_down_b"].unsqueeze(1))
            late(gate[:], T["condB_gatescore"].partition_broadcast(P))
            for l, name in enumerate(["L0", "L3"]):
                wo_rows = T[f"{name}_cond_Wo"].rearrange("(g j r) n -> j r g n", g=NG, j=GH)
                for j in range(GH):
                    late(wo[l][32 * j:32 * j + DH, :, :], wo_rows[j])
                late(bo[l][:], T[f"{name}_cond_bo"].partition_broadcast(P))
                late(b2[l][:], T[f"{name}_cond_b2"].partition_broadcast(P))
                late(b1[2 * l][:], T[f"{name}_cond_b1"].rearrange("(j p) -> p j", p=P))
            late(norm_w[1][:, 0:2], T["L0_cond_gamma2"].rearrange("(c p) -> p c", p=P))
            late(norm_w[1][:, 2:4], T["L0_cond_beta2"].rearrange("(c p) -> p c", p=P))
            late(norm_w[2][:, 0:2], T["L3_cond_g2"].rearrange("(c p) -> p c", p=P))
            late(norm_w[2][:, 2:4], T["L3_cond_beta2"].rearrange("(c p) -> p c", p=P))
            late(ln1[:, 0, :], T["L1_cond_ln_gamma"].partition_broadcast(P))
            late(ln1[:, 1, :], T["L1_cond_ln_beta"].partition_broadcast(P))
            late(wq[1][:], T["L3_cond_Wq"].rearrange("(c p) n -> p c n", p=P))
            late(wk[1][:], T["L3_cond_Wk"].rearrange("(c p) n -> p c n", p=P))
            late(wv[1][:], T["L3_cond_Wv"].rearrange("(c p) n -> p c n", p=P))
            for c in range(2):
                late(bqk[1][:, 2 * c:2 * c + 1], T["L3_cond_bq"][c * P:(c + 1) * P].unsqueeze(1))
                late(bqk[1][:, 2 * c + 1:2 * c + 2], T["L3_cond_bk"][c * P:(c + 1) * P].unsqueeze(1))
            late(bv[1][:], T["L3_cond_bv"].partition_broadcast(P))
            pool.wait_ge(load_b, 16 * LOADS_B)
            pool.tensor_copy(sin_t[:, 0, :], tok_i).then_inc(setup_p, 1)
            pool.wait_ge(setup_p, 1)
            pool.tensor_scalar(wq[1][:], wq[1][:], 0.25, None, ALU.mult).then_inc(setup_p, 1)
            pool.wait_ge(setup_p, 2)
            pool.tensor_scalar(bqk[1][:, 0:4:2], bqk[1][:, 0:4:2], 0.25, None, ALU.mult).then_inc(setup_p, 1)
            pool.wait_ge(setup_p, 3)

            pool.wait_ge(setup_v, SETUP_ADA)
            pool.dma_start(ada_dram, ada4).then_inc(ada_out, 16)

            pooled = [0]

            def res(ins):
                pooled[0] += 1
                ins.then_inc(res_pool, 1)
                pool.wait_ge(res_pool, pooled[0])

            def res_l0(s):
                pool.wait_ge(tok[1], NT * NTH[s, 1] + NT)
                res(pool.tensor_tensor(x1[:], x1[:], xy[s][:], ALU.subtract))
                res(pool.tensor_tensor(x1[:], x1[:], b2[0][:].unsqueeze(1).broadcast_to([P, NT, D]), ALU.add))

            def res_l2(s):
                pool.wait_ge(par_in, 16 * PAR * (D2[s] + 1))
                pool.wait_ge(t_psum, TURN[s, 3] + 1)
                res(pool.tensor_tensor(xy[s][:], xy[s][:], l2row[:, 0:1, :].broadcast_to([P, NT, D]), ALU.add))

            def res_l3(s):
                pool.wait_ge(tok[5], NT * NTH[s, 5] + NT)
                res(pool.tensor_tensor(xy[s][:], xy[s][:], b2[1][:].unsqueeze(1).broadcast_to([P, NT, D]), ALU.add))

            def mask_load(m):
                pool.dma_start(maskraw[:, m % 2, :],
                               T["mask_Bx1xSxS_bk0"][m // NT, 0, m % NT * P:(m % NT + 1) * P, :]).then_inc(mask_in[m % 2], 16)

            def mask_term(m):
                pool.wait_ge(mask_in[m % 2], 16 * (m // 2 + 1))
                pool.tensor_scalar(negmask[:, m % NT, :], maskraw[:, m % 2, :], NEG, None, ALU.mult).then_inc(mask_neg, 1)
                pool.wait_ge(mask_neg, m + 1)
                if m + 2 < NT * B:
                    mask_load(m + 2)

            def mask_quad(n):
                pool.wait_ge(bias_in[n % BIAS_RING], 16 * (n // BIAS_RING + 1))
                b_n = bias[:, n % BIAS_RING, :, :]
                pool.tensor_tensor(b_n, b_n, negmask[:, n % NT:n % NT + 1, :].broadcast_to([P, GH, S]),
                                   ALU.add).then_inc(masked, 1)
                pool.wait_ge(masked, n + 1)

            for m in range(2):
                mask_load(m)
            steps, do = dense_steps("p"), {"res_l0": res_l0, "res_l2": res_l2, "res_l3": res_l3}
            for U in range(FIRST, LAST + 1):
                V = U + MASK_AHEAD
                if 0 <= V < ALL_UNITS and V // UNITS in BIASED and V % GH == 0:
                    n, s = bias_tile(V), ATTENTIONS[V // UNITS][0]
                    if n % QUADS < NT:
                        mask_term(NT * s + n % QUADS)
                    mask_quad(n)
                for step, args in steps.get(U, []):
                    do[step](*args)

        @block.scalar
        def _(act):
            def exponentials(U):
                a, l, g, t, j, hd, n = unit(U)
                act.wait_ge(max_done, U + 1)
                if l == 0:
                    if U >= 3:
                        act.wait_ge(pt_psum, U - 2)
                    act.activation(prob_of(U), score_bank[U % 2][:, 0:n], ACT.Exp, bias=mrow[:, U % ROW_RING:U % ROW_RING + 1],
                                   accum_out=rsum[:, U % ROW_RING:U % ROW_RING + 1]).then_inc(p_done, 1)
                else:
                    act.activation(prob_of(U), prob_of(U), ACT.Exp, scale=-1.0, bias=mrow[:, U % ROW_RING:U % ROW_RING + 1],
                                   accum_out=rsum[:, U % ROW_RING:U % ROW_RING + 1]).then_inc(p_done, 1)

            def copy(U):
                a, l, g, t, j, hd, n = unit(U)
                act.wait_ge(pt_psum, U + 1)
                if U >= PT_RING:
                    act.wait_ge(ctx_psum, (U - PT_RING) // GH + 1)
                act.activation(pT[:, U % PT_RING, 0:n // P, :],
                               turn_bank[U % 2][:, 0:n].rearrange("p (k q) -> p k q", q=P),
                               ACT.Identity).then_inc(pt_a, 1)
                if U % GH == GH - 1 and a in BIASED and bias_tile(U) + BIAS_RING < BIAS_TILES:
                    load_bias(act, bias_tile(U) + BIAS_RING)

            def spread_copy(p):
                act.wait_ge(spread_psum, p + 1)
                if p:
                    act.wait_ge(ctx_norm, p)
                act.activation(spread[:], ctx_bank[:, 2 * P:4 * P], ACT.Identity).then_inc(spread_done, 1)

            def feature_half(s, k):
                act.wait_ge(t_psum, TURN[s, k] + 1)
                w = {0: 0, 1: 1, 5: 2}.get(k)
                if w is None:
                    act.activation(hT[:, 0, :], dense_bank[0][:], ACT.Identity).then_inc(hT_a, 1)
                else:
                    act.activation(hT[:, 0, :], dense_bank[0][:], ACT.Identity, scale=norm_w[w][:, 0:1],
                                   bias=norm_w[w][:, 2:3]).then_inc(hT_a, 1)

            def hi(s, l, i):
                a = ATT[s, l]
                act.wait_ge(qk_psum, 4 * a + i + 1)
                n = PARTS_K if i % 2 else PARTS_Q
                if i >= 2:
                    act.wait_ge(parts_out[i - 2], 16 * n * (a + 1))
                elif a:
                    act.wait_ge(parts_out[i + 2], 16 * n * a)
                act.activation(parts[i % 2][:, 0, :], dense_bank[QK_BANK[i]][:], ACT.Identity,
                               bias=bqk[l][:, i:i + 1]).then_inc(hi_done, 1)

            def mid(s, l, i):
                act.wait_ge(rest_done, 4 * ATT[s, l] + i + 1)
                act.activation(parts[i % 2][:, 1, :], rest[i % 2], ACT.Identity).then_inc(mid_done, 1)

            def gelu(s, f, j):
                n = FFN[s, f]
                if j == 0:
                    for i in (2, 3):
                        act.wait_ge(parts_out[i], 16 * (PARTS_K if i % 2 else PARTS_Q) * QKV_BEFORE[s, f])
                if f == 1 and j == 0:
                    act.wait_ge(par_in, 16 * PAR * (D2[s] + 1))
                act.wait_ge(f1_psum, NF * n + j + 1)
                act.activation(gT[:, j, :], dense_bank[FF_BANK[j]][:], ACT.Gelu_apprx_sigmoid if f == 2 else ACT.Gelu,
                               bias=b1[f][:, j:j + 1]).then_inc(g_done, 1)

            def down(s):
                act.wait_ge(ad_psum, 5 * D2[s] + 2)
                act.activation(aT, dense_bank[0][0:A, :], ACT.Gelu, bias=down_b[:]).then_inc(ad_act, 1)

            def expert(s):
                act.wait_ge(ad_psum, 5 * D2[s] + 3)
                act.wait_ge(ad_wt, 2 * D2[s] + 2)
                act.activation(eT[0:A, :], dense_bank[1][0:A, :], ACT.Identity, bias=exp_b[:, 2:3]).then_inc(ad_act, 1)

            def store(s):
                act.wait_ge(ff_done, 2 * FFN[s, 2] + 2)
                act.dma_start(out[s].rearrange("(t p) d -> p t d", p=P), xy[s][:]).then_inc(stored, 16)

            def setup_sin():
                act.wait_ge(setup_v, SETUP_ANGLES)
                act.activation(sin_t[:, 14:16, :], sin_t[:, 12:14, :], ACT.Sin).then_inc(setup_a, 1)
                act.wait_ge(setup_a, 1)
                act.activation(sin_t[:, 16:18, :], sin_t[:, 14:16, :], ACT.Exp, scale=-1.0).then_inc(setup_a, 1)

            steps = dense_steps("a")
            do = {"feature_half": feature_half, "hi": hi, "mid": mid, "gelu": gelu, "down": down, "expert": expert,
                  "store": store, "setup_sin": setup_sin}
            act.wait_ge(load_a, 16 * LOADS_A)
            act.wait_ge(setup_v, SETUP_SCALE)
            for U in range(FIRST, max(LAST + 1, ALL_UNITS + NORM_AT)):
                V = U - ACT_LAG
                if 0 <= V < ALL_UNITS and V % 2 == 1:
                    copy(V)
                if 0 <= U < ALL_UNITS:
                    exponentials(U)
                V = U - SPREAD_COPY_AT
                if 0 <= V < ALL_UNITS and V % (2 * GH) == 0:
                    spread_copy(V // (2 * GH))
                if U == 16:
                    act.wait_ge(load_b, 16 * LOADS_B)
                    act.wait_ge(setup_p, 3)
                for step, args in steps.get(U, []):
                    do[step](*args)
            act.wait_ge(stored, 16 * B)

        @block.vector
        def _(v):
            n_setup = [0]

            def step(ins):
                n_setup[0] += 1
                ins.then_inc(setup_v, 1)
                v.wait_ge(setup_v, n_setup[0])

            count = [0]

            def link(ins):
                count[0] += 1
                ins.then_inc(vec, 1)
                v.wait_ge(vec, count[0])

            r = lambda i: sin_t[:, i, :]

            def setup_scale():
                v.wait_ge(load_a, 16 * LOADS_A)
                step(v.tensor_scalar(wq[0][:], wq[0][:], 0.25, None, ALU.mult))
                step(v.tensor_scalar(bqk[0][:, 0:4:2], bqk[0][:, 0:4:2], 0.25, None, ALU.mult))
                assert n_setup[0] == SETUP_SCALE

            def setup_angles():
                v.wait_ge(setup_p, 1)
                step(v.tensor_scalar(r(2), r(0), 0.01, None, ALU.mult))
                step(v.scalar_tensor_tensor(out=r(3), in0=r(2), scalar=-64.0, in1=r(0), op0=ALU.mult, op1=ALU.add))
                step(v.scalar_tensor_tensor(out=r(4), in0=r(2), scalar=-32.0, in1=r(3), op0=ALU.mult, op1=ALU.add))
                step(v.scalar_tensor_tensor(out=r(5), in0=r(2), scalar=-4.0, in1=r(4), op0=ALU.mult, op1=ALU.add))
                step(v.scalar_tensor_tensor(out=r(1), in0=r(5), scalar=0.01, in1=r(2), op0=ALU.mult, op1=ALU.add))
                step(v.tensor_scalar(r(2), r(1), 4000.0, None, ALU.mult))
                step(v.tensor_scalar(r(3), r(2), freq, None, ALU.mult))
                for i, quarter in ((0, 0.0), (1, 0.25)):
                    step(v.tensor_scalar(r(4), r(3), 1.0 / TWO_PI, quarter, ALU.mult, ALU.add))
                    step(v.tensor_scalar(r(5), r(4), ROUND, None, ALU.add))
                    step(v.tensor_scalar(r(6), r(5), ROUND, None, ALU.subtract))
                    step(v.scalar_tensor_tensor(out=r(7), in0=r(6), scalar=-PI_HI, in1=r(3), op0=ALU.mult, op1=ALU.add))
                    step(v.scalar_tensor_tensor(out=r(8), in0=r(6), scalar=-PI_MID, in1=r(7), op0=ALU.mult, op1=ALU.add))
                    step(v.scalar_tensor_tensor(out=r(9), in0=r(6), scalar=-PI_LO, in1=r(8), op0=ALU.mult, op1=ALU.add))
                    step(v.tensor_scalar(r(10), r(9), quarter * TWO_PI, PI_LIMIT, ALU.add, ALU.min))
                    step(v.tensor_scalar(r(12 + i), r(10), -PI_LIMIT, None, ALU.max))
                assert n_setup[0] == SETUP_ANGLES

            def setup_silu():
                v.wait_ge(setup_a, 2)
                step(v.tensor_scalar(sin_t[:, 18:20, :], sin_t[:, 16:18, :], 1.0, None, ALU.add))
                step(v.reciprocal(sin_t[:, 20:22, :], sin_t[:, 18:20, :]))
                step(v.tensor_tensor(sin_t[:, 22:24, :], sin_t[:, 20:22, :], sin_t[:, 14:16, :], ALU.mult))
                assert n_setup[0] == SETUP_SILU

            def setup_weights():
                v.wait_ge(setup_t, 3)
                step(v.tensor_tensor(ada4, dense_bank[0][0:B, :], b_ada, ALU.add))
                step(v.tensor_scalar(ada4[:, 0:D], ada4[:, 0:D], 1.0, None, ALU.add))
                assert n_setup[0] == SETUP_ADA
                step(v.tensor_copy(down_t[:], dense_bank[1][:, 0:ND * A].rearrange("p (c a) -> p c a", a=A)))
                step(v.tensor_copy(up_t[0:A, :], dense_bank[2][0:A, 0:D]))
                assert n_setup[0] == SETUP_V

            def state(s, k):
                return x1 if k == 1 else xy[s]

            def stats_of(s, k, i):
                if k == 0:
                    v.wait_ge(x_in[s], 16)
                for t in (2 * i, 2 * i + 1):
                    count[0] += 1
                    v.bn_stats(stats[:, t, :], state(s, k)[:, t, :]).then_inc(vec, 1)

            def rsqrt(s, k, i):
                var, bits, guess, sq = nwt[:, 0, :], nwt[:, 1, :], rstd[:], nwt[:, 2, :]
                if i == 0:
                    v.wait_ge(vec, count[0])
                    for t in range(NT):
                        count[0] += 1
                        v.bn_aggr(mv[:, t, :], stats[:, t, :]).then_inc(vec, 1)
                    v.wait_ge(vec, count[0])
                    link(v.tensor_scalar(var, mv[:, :, 1], 1e-12 if k == 4 else 1e-5, None, ALU.add))
                    link(v.tensor_scalar(bits.bitcast(I32), var.bitcast(I32), 1, None, ALU.logical_shift_right))
                    link(v.tensor_scalar(guess.bitcast(I32), bits.bitcast(I32), -1.0, RSQRT_MAGIC, ALU.mult, ALU.add))
                for _ in range(1 + i):
                    link(v.tensor_tensor(sq, guess, guess, ALU.mult))
                    link(v.scalar_tensor_tensor(out=bits, in0=sq, scalar=-0.5, in1=var, op0=ALU.mult, op1=ALU.mult))
                    link(v.scalar_tensor_tensor(out=guess, in0=bits, scalar=1.5, in1=guess, op0=ALU.add, op1=ALU.mult))

            def norm_rows(k):
                return {3: (ln1[:, 0, :], ln1[:, 1, :]), 4: (l2row[:, 1, :], l2row[:, 2, :]),
                        5: (ada[:, 0:D], ada[:, D:2 * D])}[k]

            def apply(s, k, i):
                if k in (0, 1, 6):
                    for t in (2 * i, 2 * i + 1):
                        v.tensor_scalar(h[:, t, :], state(s, k)[:, t, :], mv[:, t, 0:1], rstd[:, t:t + 1],
                                        ALU.subtract, ALU.mult).then_inc(tok[min(k, 5)], 1)
                else:
                    y = xy[s]
                    if k == 4:
                        v.wait_ge(par_in, 16 * PAR * (D2[s] + 1))
                    for t in (2 * i, 2 * i + 1):
                        count[0] += 1
                        v.scalar_tensor_tensor(out=y[:, t, :], in0=y[:, t, :], scalar=mv[:, t, 0:1], in1=norm_rows(k)[0],
                                               op0=ALU.subtract, op1=ALU.mult).then_inc(vec, 1)

            def apply_late(s, k, i):
                y = xy[s]
                v.wait_ge(vec, count[0])
                for t in (2 * i, 2 * i + 1):
                    ins = v.scalar_tensor_tensor(out=y[:, t, :], in0=y[:, t, :], scalar=rstd[:, t:t + 1],
                                                 in1=norm_rows(k)[1], op0=ALU.mult, op1=ALU.add)
                    if k == 4:
                        count[0] += 1
                        ins.then_inc(vec, 1)
                    else:
                        ins.then_inc(tok[3 if k == 3 else 4], 1)
                if k == 4:
                    v.wait_ge(vec, count[0])

            def feature_half(s, k):
                v.wait_ge(t_psum, TURN[s, k] + 1)
                w = {0: 0, 1: 1, 5: 2}.get(k)
                if w is None:
                    v.tensor_copy(hT[:, 1, :], dense_bank[1][:]).then_inc(hT_v, 1)
                else:
                    v.tensor_scalar(hT[:, 1, :], dense_bank[1][:], norm_w[w][:, 1:2], norm_w[w][:, 3:4],
                                    ALU.mult, ALU.add).then_inc(hT_v, 1)

            def rest_of(s, l, i):
                v.wait_ge(hi_done, 4 * ATT[s, l] + i + 1)
                v.scalar_tensor_tensor(out=rest[i % 2], in0=dense_bank[QK_BANK[i]][:], scalar=bqk[l][:, i:i + 1],
                                       in1=parts[i % 2][:, 0, :], op0=ALU.add, op1=ALU.subtract).then_inc(rest_done, 1)

            def lo(s, l, i):
                v.wait_ge(mid_done, 4 * ATT[s, l] + i + 1)
                v.tensor_tensor(parts[i % 2][:, 2, :], rest[i % 2], parts[i % 2][:, 1, :],
                                ALU.subtract).then_inc(lo_done, 1)

            def values_out(s, l, i):
                a = ATT[s, l]
                if a < 2:
                    v.wait_ge(consts, CONSTS)
                v.wait_ge(v_psum, 2 * a + i + 1)
                for t in (2 * i, 2 * i + 1):
                    v.tensor_tensor(va[a % 2][:, t, :, 0:DH],
                                    dense_bank[V_BANK[i]][:, (t % 2) * D:(t % 2 + 1) * D].rearrange("p (h d) -> p h d", d=DH),
                                    bv[l][:].rearrange("p (h d) -> p h d", d=DH), ALU.add).then_inc(v_done, 1)

            def pairs(psum):
                return psum[:].rearrange("p (t d) -> p t d", d=D)

            def residual(s, l, i):
                v.wait_ge(wo_psum, 2 * ATT[s, l] + i + 1)
                tt = slice(2 * i, 2 * i + 2)
                dst = xy[s] if l else x1
                link(v.tensor_tensor(dst[:, tt, :], pairs(dense_bank[i]), xy[s][:, tt, :], ALU.add))
                v.tensor_tensor(dst[:, tt, :], dst[:, tt, :], bo[l][:].unsqueeze(1).broadcast_to([P, 2, D]),
                                ALU.add).then_inc(wo_done, 1)
                v.wait_ge(wo_done, 2 * ATT[s, l] + i + 1)

            def ff_add(s, f, i):
                n, tt = FFN[s, f], slice(2 * i, 2 * i + 2)
                if i == 0:
                    v.wait_ge(res_pool, res_count(s, (0, 2, 3)[f]))
                v.wait_ge(f2_psum, 2 * n + i + 1)
                psum = pairs(dense_bank[FF_OUT_BANK[i]])
                dst = xy[s] if f else x1
                v.tensor_tensor(dst[:, tt, :], psum, dst[:, tt, :], ALU.add).then_inc(ff_done, 1)
                v.wait_ge(ff_done, 2 * n + i + 1)
                if f == 0:
                    for t in (2 * i, 2 * i + 1):
                        v.scalar_tensor_tensor(out=xy[s][:, t, :], in0=x1[:, t, :], scalar=gate[:, s:s + 1],
                                               in1=xy[s][:, t, :], op0=ALU.mult, op1=ALU.add).then_inc(tok[2], 1)
                        v.wait_ge(tok[2], NT * NTH[s, 2] + t + 1)

            def expert(s):
                v.wait_ge(ad_psum, 5 * D2[s] + 1)
                v.tensor_copy(exp_wt[:], dense_bank[2][0:A, 0:A]).then_inc(ad_wt, 1)
                v.wait_ge(par_in, 16 * PAR * (D2[s] + 1))
                v.tensor_tensor(exp_b[:, 2:3], exp_b[:, 0:1], exp_b[:, 1:2], ALU.add).then_inc(ad_wt, 1)

            def up_add(s, i):
                v.wait_ge(ad_psum, 5 * D2[s] + 4 + i)
                tt = slice(2 * i, 2 * i + 2)
                link(v.tensor_tensor(xy[s][:, tt, :], pairs(dense_bank[UP_BANK[i]]), xy[s][:, tt, :], ALU.add))

            def maxima(U):
                a, l, g, t, j, hd, n = unit(U)
                m = mrow[:, U % ROW_RING:U % ROW_RING + 1]
                if l == 0:
                    v.wait_ge(s_psum, U + 1)
                    v.tensor_reduce(m, score_bank[U % 2][:, 0:n], AX_X, ALU.max, negate=True).then_inc(max_done, 1)
                else:
                    if j == 0:
                        v.wait_ge(masked, bias_tile(U) + 1)
                    v.wait_ge(s_psum, U + 1)
                    v.tensor_tensor_reduce(out=prob_of(U), in0=score_bank[U % 2][:], in1=prob_of(U), scale=-1.0,
                                           scalar=3e38, op0=ALU.add, op1=ALU.min, accum_out=m).then_inc(max_done, 1)

            def copy(U):
                a, l, g, t, j, hd, n = unit(U)
                v.wait_ge(pt_psum, U + 1)
                if U >= PT_RING:
                    v.wait_ge(ctx_psum, (U - PT_RING) // GH + 1)
                v.tensor_copy(pT[:, U % PT_RING, 0:n // P, :],
                              turn_bank[U % 2][:, 0:n].rearrange("p (k q) -> p k q", q=P)).then_inc(pt_v, 1)

            def invert(p):
                u = 2 * GH * p % ROW_RING
                v.wait_ge(p_done, 2 * GH * (p + 1))
                link(v.reciprocal(rinv[:], rsum[:, u:u + 2 * GH]))
                if p:
                    v.wait_ge(spread_psum, p)
                v.tensor_copy(rwide[:].rearrange("p w (j r) -> p (w j) r", r=32),
                              rinv[:].unsqueeze(2).broadcast_to([P, 2 * GH, 32])).then_inc(inv_done, 1)

            def normalize(p):
                a, w = p // (QUADS // 2), p % (QUADS // 2) * 2
                g, t = divmod(w, NT)
                if w == 0 and a:
                    v.wait_ge(wo_psum, 2 * a)
                v.wait_ge(spread_done, p + 1)
                v.tensor_tensor(ctxn[:, g, t * P:(t + 2) * P], ctx_bank[:, 0:2 * P], spread[:], ALU.mult).then_inc(ctx_norm, 1)

            steps = dense_steps("v")
            do = {"stats": stats_of, "rsqrt": rsqrt, "apply": apply, "apply_late": apply_late,
                  "feature_half": feature_half, "rest": rest_of, "lo": lo, "v": values_out, "residual": residual,
                  "ff_add": ff_add, "expert": expert, "up_add": up_add, "setup_angles": setup_angles,
                  "setup_silu": setup_silu, "setup_weights": setup_weights}
            setup_scale()
            for U in range(FIRST, max(LAST + 1, ALL_UNITS + NORM_AT + 1)):
                V = U - VEC_LAG
                if 0 <= V < ALL_UNITS and V % 2 == 0:
                    copy(V)
                if 0 <= U < ALL_UNITS:
                    maxima(U)
                V = U - SUM_AT
                if 0 <= V < ALL_UNITS and V % (2 * GH) == 0:
                    invert(V // (2 * GH))
                V = U - NORM_AT
                if 0 <= V < ALL_UNITS and V % (2 * GH) == 0:
                    normalize(V // (2 * GH))
                if U == 16:
                    v.wait_ge(load_b, 16 * LOADS_B)
                for name, args in steps.get(U, []):
                    do[name](*args)

        @block.tensor
        def _(pe):
            def dense_banks_free(upto):
                if upto["qkv"]:
                    pe.wait_ge(v_done, 4 * upto["qkv"])
                if upto["ffn"]:
                    pe.wait_ge(ff_done, 2 * upto["ffn"])
                if upto["out"]:
                    pe.wait_ge(wo_done, 2 * upto["out"])
                if upto["turn"]:
                    pe.wait_ge(hT_a, upto["turn"])
                    pe.wait_ge(hT_v, upto["turn"])

            issued = {"qkv": 0, "ffn": 0, "out": 0, "turn": 0}

            def turn_tokens(s, k):
                dense_banks_free(issued)
                src = h if k in (0, 1, 5) else xy[s]
                for t in range(NT):
                    pe.wait_ge(tok[k], NT * NTH[s, k] + t + 1)
                    for c in range(ND):
                        mm = pe.transpose(dense_bank[c][:, t * P:(t + 1) * P], src[:, t, c * P:(c + 1) * P], ident[:])
                mm.then_inc(t_psum, 1)
                issued["turn"] += 1

            def hT_ready(s, k):
                pe.wait_ge(hT_a, TURN[s, k] + 1)
                pe.wait_ge(hT_v, TURN[s, k] + 1)

            def qk(s, l, i):
                if i == 0:
                    hT_ready(s, 0 if l == 0 else 4)
                if l == 1 and i == 0:
                    pe.wait_ge(setup_p, 3)
                if i == 3:
                    pe.wait_ge(rest_done, 4 * ATT[s, l] + 1)
                w, c0 = (wk[l] if i % 2 else wq[l]), (i // 2) * P
                for c in range(ND):
                    mm = pe.matmul(dense_bank[QK_BANK[i]][:], w[:, c, c0:c0 + P], hT[:, c, :], start=c == 0, stop=c == ND - 1)
                mm.then_inc(qk_psum, 1)

            def v_rows(s, l, i):
                pe.wait_ge(rest_done, 4 * ATT[s, l] + i + 2)
                for t in (2 * i, 2 * i + 1):
                    for c in range(ND):
                        mm = pe.matmul(dense_bank[V_BANK[i]][:, (t % 2) * D:(t % 2 + 1) * D], hT[:, c, t * P:(t + 1) * P],
                                       wv[l][:, c, :], start=c == 0, stop=c == ND - 1)
                mm.then_inc(v_psum, 1)
                if i == 1:
                    issued["qkv"] += 1

            def project(s, l, i):
                if i == 0:
                    dense_banks_free(issued)
                    pe.wait_ge(ctx_norm, QUADS // 2 * (ATT[s, l] + 1))
                for t in (2 * i, 2 * i + 1):
                    for g in range(NG):
                        mm = pe.matmul(dense_bank[i][:, (t % 2) * D:(t % 2 + 1) * D], ctxn[:, g, t * P:(t + 1) * P],
                                       wo[l][:, g, :], start=g == 0, stop=g == NG - 1)
                mm.then_inc(wo_psum, 1)
                if i == 1:
                    issued["out"] += 1

            def hidden(s, f, j):
                n = FFN[s, f]
                if j == 0:
                    hT_ready(s, (1, 3, 5)[f])
                    pe.wait_ge(w1_in, 16 * (n + 1))
                if j >= 3:
                    pe.wait_ge(g_done, NF * n + j - 2)
                for c in range(ND):
                    mm = pe.matmul(dense_bank[FF_BANK[j]][:], w1[:, c, j * P:(j + 1) * P], hT[:, c, :],
                                   start=c == 0, stop=c == ND - 1)
                mm.then_inc(f1_psum, 1)

            def ff_out(s, f, t):
                n = FFN[s, f]
                if t == 0:
                    pe.wait_ge(w2_in, 16 * (n + 1))
                for j in range(NF):
                    if t == 0 and j in (0, 6, 7):
                        pe.wait_ge(g_done, NF * n + max(6, j + 1))
                    mm = pe.matmul(dense_bank[FF_OUT_BANK[t // 2]][:, (t % 2) * D:(t % 2 + 1) * D],
                                   gT[:, j, t * P:(t + 1) * P], w2[:, j, :], start=j == 0, stop=j == NF - 1)
                if t % 2:
                    mm.then_inc(f2_psum, 1)
                if t == NT - 1:
                    issued["ffn"] += 1

            def turn_expert(s):
                pe.wait_ge(par_in, 16 * PAR * (D2[s] + 1))
                pe.wait_ge(ff_done, 2 * FFN[s, 0] + 2)
                pe.transpose(dense_bank[2][0:A, 0:A], exp_w[:], ident[0:A, 0:A]).then_inc(ad_psum, 1)

            def down(s):
                hT_ready(s, 2)
                if not D2[s]:
                    pe.wait_ge(setup_v, SETUP_V)
                for c in range(ND):
                    mm = pe.matmul(dense_bank[0][0:A, :], down_t[:, c, :], hT[:, c, :], start=c == 0, stop=c == ND - 1)
                mm.then_inc(ad_psum, 1)

            def expert(s):
                pe.wait_ge(ad_act, 2 * D2[s] + 1)
                pe.wait_ge(ad_wt, 2 * D2[s] + 1)
                pe.matmul(dense_bank[1][0:A, :], exp_wt[:], aT, start=True, stop=True).then_inc(ad_psum, 1)

            def up(s):
                pe.wait_ge(ad_act, 2 * D2[s] + 2)
                for t in range(NT):
                    mm = pe.matmul(dense_bank[UP_BANK[t // 2]][:, (t % 2) * D:(t % 2 + 1) * D], eT[:, t * P:(t + 1) * P],
                                   up_t[:], start=True, stop=True)
                    if t % 2:
                        mm.then_inc(ad_psum, 1)

            def setup():
                dense_banks_free(issued)
                pe.wait_ge(load_b, 16 * LOADS_B)
                pe.wait_ge(setup_v, SETUP_SILU)
                for c in range(ND):
                    mm = pe.matmul(dense_bank[0][0:B, :], sin_t[:, 22 + c, :], w_ada[:, c, :], start=c == 0, stop=c == ND - 1)
                mm.then_inc(setup_t, 1)
                for c in range(ND):
                    mm = pe.transpose(dense_bank[1][:, c * A:(c + 1) * A], down_raw[:, c * P:(c + 1) * P], ident[0:A, 0:A])
                mm.then_inc(setup_t, 1)
                for c in range(ND):
                    mm = pe.transpose(dense_bank[2][0:A, c * P:(c + 1) * P], up_raw[:, c, :], ident[:])
                mm.then_inc(setup_t, 1)

            def scores(U):
                a, l, g, t, j, hd, n = unit(U)
                if U % (UNITS // 2) == 0:
                    pe.wait_ge(stack_in[hd // HH], 96 * (a + 1))
                if U >= 2:
                    pe.wait_ge(p_done if unit(U - 2)[1] == 0 else max_done, U - 1)
                mm = pe.matmul(score_bank[U % 2][:, 0:n], qs[:, hd, t * P:(t + 1) * P], ks[:, hd, 0:n],
                               start=True, stop=l == 1)
                if l == 0:
                    mm = pe.matmul(score_bank[U % 2][:, n - P:n], identb[:], causal[:], start=False, stop=True)
                mm.then_inc(s_psum, 1)

            def copied(U):
                pe.wait_ge(pt_v, (U + 1) // 2)
                if U // 2:
                    pe.wait_ge(pt_a, U // 2)

            def turn(U):
                a, l, g, t, j, hd, n = unit(U)
                pe.wait_ge(p_done, U + 1)
                if U >= 2:
                    copied(U - 1)
                for k in range(n // P):
                    mm = pe.transpose(turn_bank[U % 2][:, k * P:(k + 1) * P], prob_of(U)[:, k * P:(k + 1) * P], ident[:])
                mm.then_inc(pt_psum, 1)

            def values(w):
                a, l, g, t, _, _, n = unit(GH * w)
                copied(GH * (w + 1))
                if w % QUADS == 0:
                    pe.wait_ge(v_done, 4 * (a + 1))
                if w % 2 == 0 and w:
                    pe.wait_ge(ctx_norm, w // 2)
                for k in range(n // P):
                    for j in range(GH):
                        mm = pe.matmul(ctx_bank[32 * j:32 * (j + 1), w % 2 * P:(w % 2 + 1) * P], va[a % 2][:, k, GH * g + j, :],
                                       pT[:, (GH * w + j) % PT_RING, k, :], start=k == 0, stop=k == n // P - 1)
                mm.then_inc(ctx_psum, 1)

            def spread_sums(p):
                pe.wait_ge(inv_done, p + 1)
                if p:
                    pe.wait_ge(spread_done, p)
                for w in range(2):
                    mm = pe.transpose(ctx_bank[:, (2 + w) * P:(3 + w) * P], rwide[:, w, :], ident[:])
                mm.then_inc(spread_psum, 1)

            steps = dense_steps("pe")
            do = {"turn_tokens": turn_tokens, "qk": qk, "v": v_rows, "project": project, "hidden": hidden,
                  "ff_out": ff_out, "turn_expert": turn_expert, "down": down, "expert": expert, "up": up, "setup": setup}
            pe.wait_ge(consts, 2)
            pe.wait_ge(load_a, 16 * LOADS_A)
            pe.wait_ge(setup_v, SETUP_SCALE)
            for U in range(FIRST, max(LAST + 1, ALL_UNITS + NORM_AT + 1)):
                if U == 0:
                    pe.wait_ge(consts, CONSTS)
                if 0 <= U < ALL_UNITS:
                    scores(U)
                V = U - TURN_LAG
                if 0 <= V < ALL_UNITS:
                    turn(V)
                V = U - VALUES_AT
                if 0 <= V < ALL_UNITS and V % GH == 0:
                    values(V // GH)
                V = U - SPREAD_AT
                if 0 <= V < ALL_UNITS and V % (2 * GH) == 0:
                    spread_sums(V // (2 * GH))
                for step, args in steps.get(U, []):
                    do[step](*args)


QK_BANK = (2, 0, 1, 2)
V_BANK = (0, 1)
FF_BANK = (2, 0, 1, 2, 0, 1, 2, 0)
FF_OUT_BANK = (1, 2)
UP_BANK = (2, 0)
MASK_AHEAD = 4
CONST_WO = 4
CONSTS = CONST_WO + 7
SETUP_SCALE = 2
SETUP_ANGLES = SETUP_SCALE + 5 + 2 + 2 * 8
SETUP_SILU = SETUP_ANGLES + 3
SETUP_ADA = SETUP_SILU + 2
SETUP_V = SETUP_ADA + 2

_NAMES = ["x", "condB_gatescore", "itok_B_0_15", "itok_B_0_7", "itok_B_34_63", "fside_Bx16xSxS_0", "mask_Bx1xSxS_bk0"]
_NAMES += ["L0_cond_" + n for n in "Wq bq Wk bk Wv bv Wo bo W1 b1 W2 b2 gamma1 beta1 gamma2 beta2".split()]
_NAMES += ["L1_cond_" + n for n in "down_W down_b up_W up_b expert_W expert_b domain_emb ln_gamma ln_beta".split()]
_NAMES += ["L2_cond_" + n for n in "Wi bi Wo bo gamma beta".split()]
_NAMES += ["L3_cond_" + n for n in "W_ada b_ada Wq bq Wk bk Wv bv Wo bo W1 b1 W2 b2 g2 beta2".split()]


def kernel(**inputs):
    import math
    import numpy as np
    from concourse import bacc
    from concourse.bass_utils import run_bass_kernel_spmd

    nc = bacc.Bacc("TRN2", target_bir_lowering=False, num_devices=1)
    arrays = {name: np.ascontiguousarray(inputs[name]) for name in _NAMES}
    half = D // 2
    step = np.float32(-math.log(10000.0) / (half - 1))
    arrays["freqs"] = np.exp(np.arange(half, dtype=np.float32) * step).astype(np.float32)
    T = {n: nc.dram_tensor("in_" + n, a.shape, mybir.dt.from_np(a.dtype), kind="ExternalInput").ap()
         for n, a in arrays.items()}
    out = nc.dram_tensor("out_0", (B, S, D), F32, kind="ExternalOutput").ap()
    build(nc, T, out)
    r = run_bass_kernel_spmd(nc, [{"in_" + n: a for n, a in arrays.items()}], core_ids=[0])
    return r.results[0]["out_0"]
```

```python
from contextlib import ExitStack

import concourse.bass as bass
from concourse import mybir

P = 128
B, S, D, F = 4, 512, 256, 1024
H, DH = 16, 16
NT = S // P
ND = D // P
NF = F // P
A = 64
E16, E8 = 16, 8
GH = 4
NG = H // GH
HH = H // 2
UNITS = H * NT
QUADS = UNITS // GH
PT_RING = 8
ROW_RING = 16
BIAS_RING = 6
NEG = -1e30
PARTS_Q = 5
PARTS_K = 3
STACK = [(0, 2, 0, 0), (2, 3, 1, 0), (5, 3, 2, 0)]

ALU = mybir.AluOpType
ACT = mybir.ActivationFunctionType
AX_X = mybir.AxisListType.X
F32 = mybir.dt.float32
BF16 = mybir.dt.bfloat16
I32 = mybir.dt.int32
U8 = mybir.dt.uint8

TWO_PI = 6.283185307179586
PI_HI = 6.28125
PI_MID = round((TWO_PI - PI_HI) * 2 ** 23) / 2 ** 23
PI_LO = TWO_PI - PI_HI - PI_MID
PI_LIMIT = 3.1415925
ROUND = 12582912.0
RSQRT_MAGIC = 1597463007.0

ATTENTIONS = [(0, 0), (1, 0), (2, 0), (0, 1), (3, 0), (1, 1), (2, 1), (3, 1)]
ATT = {sl: a for a, sl in enumerate(ATTENTIONS)}
ALL_UNITS = UNITS * len(ATTENTIONS)
BIASED = {a: n for n, a in enumerate(a for a, (_, l) in enumerate(ATTENTIONS) if l == 1)}

TURN_LAG = 2
ACT_LAG = 3
VEC_LAG = 3
SUM_AT = 9
VALUES_AT = 8
SPREAD_AT = 13
SPREAD_COPY_AT = 14
NORM_AT = 15

EVENTS = []
SLOTS = 4
RSQRT_STEPS = 4 + 3 * 3


def at(tick, engine, step, *args):
    EVENTS.append((tick, engine, step, args))


def plan_norm(t, s, k):
    for i in range(2):
        at(t + i, "v", "stats", s, k, i)
    for i in range(RSQRT_STEPS):
        at(t + 2 + i // SLOTS, f"v{i % SLOTS}", "rsqrt", s, k, i)
    for i in range(2):
        if k in (3, 4, 5):
            at(t + 3 + i, "v", "apply", s, k, i)
            at(t + 5 + i, "v", "apply_late", s, k, i)
        else:
            at(t + 5, "v", "apply", s, k, i)
    if k == 1:
        at(t + 6, "p", "res_l0", s)
    if k == 6:
        at(t + 6, "p", "res_l3", s)


def plan_turn(t, s, k):
    at(t, "pe", "turn_tokens", s, k)
    at(t + 1, "v", "feature_half", s, k)
    at(t + 1, "a", "feature_half", s, k)


def plan_qkv(t, s, l):
    for c in range(2):
        for i in (2 * c, 2 * c + 1):
            u = t + 6 * c
            at(u + i % 2, "pe", "qk", s, l, i)
            at(u + 1, "a", "hi", s, l, i)
            at(u + 2, "v", "rest", s, l, i)
            at(u + 3, "a", "mid", s, l, i)
            at(u + 4, "v", "lo", s, l, i)
    at(t + 2, "pe", "v", s, l, 0)
    at(t + 3, "v", "v", s, l, 0)
    at(t + 4, "pe", "v", s, l, 1)
    at(t + 5, "v", "v", s, l, 1)


def plan_ffn(t, s, f):
    for j, (dt, da) in enumerate(zip((0, 0, 1, 3, 4, 5, 7, 8), (1, 1, 1, 5, 5, 5, 8, 8))):
        at(t + dt, "pe", "hidden", s, f, j)
        at(t + da, "a", "gelu", s, f, j)
    for i in range(NT):
        at(t + 9 + i, "pe", "ff_out", s, f, i)
    at(t + 11, "v", "ff_add", s, f, 0)
    at(t + 13, "v", "ff_add", s, f, 1)


def plan_out(t, s, l):
    for i in range(2):
        at(t + i, "pe", "project", s, l, i)
        at(t + i + 1, "v", "residual", s, l, i)


def qkv0(t, s):
    plan_turn(t, s, 0)
    plan_qkv(t + 3, s, 0)


def block0(t, s):
    plan_turn(t, s, 1)
    plan_ffn(t + 3, s, 0)
    t += 17
    at(t, "pe", "turn_expert", s)
    plan_turn(t, s, 2)
    at(t + 1, "v", "expert", s)
    at(t + 3, "pe", "down", s)
    at(t + 3, "a", "down", s)
    at(t + 5, "pe", "expert", s)
    at(t + 5, "a", "expert", s)
    at(t + 6, "pe", "up", s)
    at(t + 6, "v", "up_add", s, 0)
    at(t + 7, "v", "up_add", s, 1)


def block2(t, s):
    plan_turn(t, s, 3)
    at(t + 1, "p", "res_l2", s)
    plan_ffn(t + 3, s, 1)


def qkv3(t, s):
    plan_turn(t, s, 4)
    plan_qkv(t + 3, s, 1)


def block3(t, s):
    plan_turn(t, s, 5)
    plan_ffn(t + 3, s, 2)
    at(t + 17, "a", "store", s)


def norm(k):
    return lambda t, s: plan_norm(t, s, k)


STACKS_AT = [(-6, 5)] + [(-28, 4)] * 2 + [(-7, 4)] + [(-28, 4)] * 3 + [(-7, 4)]
BESIDE = [
    [(0, norm(0), 1), (6, qkv0, 1), (24, norm(0), 2)],
    [(11, qkv0, 2), (12, norm(1), 0), (23, block0, 0), (48, norm(3), 0), (55, block2, 0), (72, norm(4), 0)],
    [(21, block0, 1), (15, norm(1), 1), (22, norm(5), 0), (46, qkv3, 0), (47, norm(3), 1), (58, block2, 1),
     (54, norm(0), 3), (76, norm(4), 1)],
    [(15, qkv0, 3), (19, norm(1), 2), (27, block0, 2), (28, norm(5), 1), (52, norm(3), 2)],
    [(11, qkv3, 1), (12, norm(6), 0), (23, block2, 2), (40, block3, 0), (41, norm(4), 2), (48, norm(5), 2)],
    [(11, qkv3, 2), (12, norm(1), 3), (23, block0, 3), (48, norm(3), 3)],
    [(11, block2, 3), (12, norm(6), 1), (28, block3, 1), (29, norm(4), 3), (36, norm(5), 3), (45, qkv3, 3)],
    [(9, norm(6), 2), (15, block3, 2)],
    [(9, norm(6), 3), (15, block3, 3)],
]
OUTPUT_AT = [None, 8, 8, 12, 8, 8, 8, 8, 8]
for _a, (_s, _l) in enumerate(ATTENTIONS):
    for _c, _t in enumerate(STACKS_AT[_a]):
        at(UNITS * _a + _t, "a", "stack", _s, _l, _c)
plan_norm(-20, 0, 0)
at(-14, "v", "setup_scale")
qkv0(-14, 0)
at(10, "v", "setup_angles")
at(10, "a", "setup_sin")
at(20, "v", "setup_silu")
at(21, "pe", "setup")
at(22, "v", "setup_weights")
for _a, _stages in enumerate(BESIDE):
    if _a:
        plan_out(UNITS * _a + OUTPUT_AT[_a], *ATTENTIONS[_a - 1])
    for _t, _plan, _s in _stages:
        _plan(UNITS * _a + _t, _s)
LAST = max(e[0] for e in EVENTS)
FIRST = min(e[0] for e in EVENTS)


def dense_steps(engine):
    steps = {}
    for t, e, step, args in EVENTS:
        if e == engine:
            steps.setdefault(t, []).append((step, args))
    return steps


def order(engine, step, key):
    found = sorted(((t, n, key(args)) for n, (t, e, st, args) in enumerate(EVENTS) if e == engine and st == step),
                   key=lambda x: x[:2])
    out = {}
    for _, _, k in found:
        out.setdefault(k, len(out))
    return out


TURN = order("pe", "turn_tokens", lambda a: a)
NTH = {(s, k): sum(1 for x in TURN if x[1] == k and TURN[x] < n) for (s, k), n in TURN.items()}
FFN = order("pe", "hidden", lambda a: a[:2])
QKV = order("pe", "qk", lambda a: a[:2])
OUTP = order("pe", "project", lambda a: a[:2])
QKV_BEFORE = {sf: sum(1 for t, e, st, a in EVENTS if e == "pe" and st == "qk" and a[2] == 0 and t < t0)
              for t0, sf in sorted((t, a[:2]) for t, e, st, a in EVENTS if e == "pe" and st == "hidden" and a[2] == 0)}
ADAPT = order("pe", "down", lambda a: a[0])
assert QKV == ATT and OUTP == ATT and all(ADAPT[s] == s for s in range(B))

_gelus = {t for t, e, st, a in EVENTS if st == "gelu"}
ON_ACT = [U % 2 == 1 and not {U + ACT_LAG - 1, U + ACT_LAG - 2} & _gelus for U in range(ALL_UNITS)]
COPIES_A = [sum(ON_ACT[:U]) for U in range(ALL_UNITS + 1)]

LOADS_A = 12
LOADS_B = 9 + 2 * 7 + 6 + 3 + 4 + 1
EXPERT_LOADS = 3
ROW_LOADS = 5
BIAS_PAIRS = UNITS // 2 * len(BIASED)


def build(nc, T, out):
    with ExitStack() as ctx:
        def sb(name, shape, dt=F32):
            return ctx.enter_context(nc.sbuf_tensor(name, shape, dt))

        def sem(name):
            return ctx.enter_context(nc.semaphore(name))

        ident = sb("ident", [P, P])
        causal = sb("causal", [P, P], BF16)
        identb = sb("identb", [P, P], BF16)
        wq = [sb(f"wq{l}", [P, ND, D]) for l in range(2)]
        wk = [sb(f"wk{l}", [P, ND, D]) for l in range(2)]
        wv = [sb(f"wv{l}", [P, ND, D]) for l in range(2)]
        wo = [sb(f"wo{l}", [P, NG, D]) for l in range(2)]
        bqk = [sb(f"bqk{l}", [P, 4]) for l in range(2)]
        bv = [sb(f"bv{l}", [P, D]) for l in range(2)]
        bo = [sb(f"bo{l}", [P, D]) for l in range(2)]
        b2 = [sb(f"b2_{l}", [P, D]) for l in range(2)]
        b1 = [sb(f"b1_{l}", [P, NF]) for l in range(3)]
        norm_w = [sb(f"norm_w{l}", [P, 4]) for l in range(3)]
        w1 = sb("w1", [P, ND, F])
        w2 = sb("w2", [P, NF, D])
        down_t = sb("down_t", [P, ND, A])
        up_t = sb("up_t", [A + 1, D])
        down_b = sb("down_b", [A, 1])
        ln1 = sb("ln1", [P, 2, D])
        exp_w = sb("exp_w", [A, A])
        exp_wt = sb("exp_wt", [A, A])
        exp_b = sb("exp_b", [A, 3])
        l2row = sb("l2row", [P, 3, D])
        ada = sb("ada", [P, 2 * D])
        gate = sb("gate", [P, B])
        idx = sb("idx", [1, 2 * B], I32)

        xy = [sb(f"xy{i}", [P, NT, D]) for i in range(B)]
        x1 = sb("x1", [P, NT, D])
        h = sb("h", [P, NT, D])
        hT = sb("hT", [P, ND, S])
        qs = sb("qs", [P, H, S], BF16)
        ks = sb("ks", [P, H, S], BF16)
        va = [sb(f"va{i}", [P, NT, H, 32]) for i in range(2)]
        pT = sb("pT", [P, PT_RING, NT, P])
        gT = sb("gT", [P, NF, S])
        bias = sb("bias", [P, BIAS_RING, 2, S])
        prob = sb("prob", [P, 3, S])
        mrow = sb("mrow", [P, ROW_RING])
        rsum = sb("rsum", [P, ROW_RING])
        rinv = sb("rinv", [P, 2 * GH])
        rwide = sb("rwide", [P, 2, P])
        negmask = sb("negmask", [P, NT, S], BF16)
        maskraw = sb("maskraw", [P, 2, S], U8)
        spread = sb("spread", [P, 2 * P])
        ctxn = sb("ctxn", [P, NG, S])
        parts = [gT[:, 0:3, :].rearrange("p n t -> p (n t)").bitcast(BF16)[:, 3 * S * i:3 * S * (i + 1)]
                 .rearrange("p (n t) -> p n t", t=S) for i in range(2)]
        rest = [gT[:, 6 + i, :] for i in range(2)]
        aT = gT[0:A, 0, :]
        eT = sb("eT", [A + 1, S])
        stats = sb("stats", [P, NT, 6])
        mv = sb("mv", [P, NT, 2])
        rstd = sb("rstd", [P, NT])
        nwt = sb("nwt", [P, 3, NT])

        scratch = bias[:].rearrange("p r h k -> p (r h) k")
        w_ada = scratch[:, 0:2, :]
        b_ada = scratch[0:B, 2, :]
        ada4 = scratch[0:B, 3, :]
        down_raw = scratch[0:A, 4, 0:D]
        up_raw = scratch[:, 4, D:D + ND * A].rearrange("p (c a) -> p c a", a=A)
        sin_t = scratch[:, 5, 0:96].rearrange("p (n b) -> p n b", b=B)
        tok_i = scratch[:, 5, 96:96 + B].bitcast(I32)
        freq = scratch[:, 5, 104:105]

        q_dram = nc.dram_tensor("q_parts", (H, PARTS_Q, DH, S), BF16).ap()
        k_dram = nc.dram_tensor("k_parts", (H, PARTS_K, DH, S), BF16).ap()
        ada_dram = nc.dram_tensor("ada_rows", (B, 2 * D), F32).ap()

        bank = [ctx.enter_context(nc.psum_tensor(f"bank{i}", [P, S], F32)) for i in range(8)]
        score_bank, turn_bank, ctx_bank, dense_bank = bank[0:2], bank[2:4], bank[4], bank[5:8]

        load_a = sem("load_a")
        load_b = sem("load_b")
        consts = sem("consts")
        setup_v = sem("setup_v")
        setup_p = sem("setup_p")
        setup_a = sem("setup_a")
        setup_t = sem("setup_t")
        ada_out = sem("ada_out")
        x_in = [sem(f"x_in{s}") for s in range(B)]
        expert_in = sem("expert_in")
        rows_in = sem("rows_in")
        mask_in = [sem(f"mask_in{i}") for i in range(2)]
        mask_neg = sem("mask_neg")
        w1_in = sem("w1_in")
        w2_in = sem("w2_in")
        bias_in = [sem(f"bias_in{i}") for i in range(BIAS_RING)]
        masked = sem("masked")
        tok = [sem(f"tok{k}") for k in range(6)]
        t_psum = sem("t_psum")
        hT_a = sem("hT_a")
        hT_v = sem("hT_v")
        qk_psum = sem("qk_psum")
        v_psum = sem("v_psum")
        hi_done = sem("hi_done")
        rest_done = sem("rest_done")
        mid_done = sem("mid_done")
        lo_done = sem("lo_done")
        parts_out = [sem(f"parts_out{i}") for i in range(4)]
        stack_in = [sem(f"stack_in{i}") for i in range(2)]
        v_done = sem("v_done")
        s_psum = sem("s_psum")
        max_done = sem("max_done")
        p_done = sem("p_done")
        pt_psum = sem("pt_psum")
        pt_a = sem("pt_a")
        pt_v = sem("pt_v")
        inv_done = sem("inv_done")
        ctx_psum = sem("ctx_psum")
        spread_psum = sem("spread_psum")
        spread_done = sem("spread_done")
        ctx_norm = sem("ctx_norm")
        wo_psum = sem("wo_psum")
        wo_done = sem("wo_done")
        f1_psum = sem("f1_psum")
        g_done = sem("g_done")
        f2_psum = sem("f2_psum")
        ff_done = sem("ff_done")
        res_pool = sem("res_pool")
        ad_psum = sem("ad_psum")
        ad_act = sem("ad_act")
        ad_wt = sem("ad_wt")
        up_done = sem("up_done")
        vec = sem("vec")
        stored = sem("stored")

        ctx.enter_context(nc.allow_non_contiguous_dma(reason="vectors of a few hundred elements, features on the partitions"))
        block = ctx.enter_context(nc.Block())

        def unit(U):
            a, u = divmod(U, UNITS)
            l = ATTENTIONS[a][1]
            g, t, j = u // (NT * GH), u // GH % NT, u % GH
            return a, l, g, t, j, GH * g + j, (t + 1) * P if l == 0 else S

        def bias_pair(U):
            return (BIASED[U // UNITS] * UNITS + U % UNITS) // 2

        def prob_of(U):
            _, l, _, _, j, _, n = unit(U)
            return prob[:, U % 3, 0:n] if l == 0 else bias[:, bias_pair(U) % BIAS_RING, U % 2, :]

        def res_count(s, layer):
            name, n = {0: ("res_l0", 2), 2: ("res_l2", 1), 3: ("res_l3", 1)}[layer]
            total = 0
            for _, _, step, args in sorted((t, i, st, a) for i, (t, e, st, a) in enumerate(EVENTS)
                                           if e == "p" and st.startswith("res")):
                total += 2 if step == "res_l0" else 1
                if step == name and args[0] == s:
                    return total

        def load_bias(eng, n):
            a = [x for x in BIASED if BIASED[x] == n // (UNITS // 2)][0]
            _, _, _, t, _, hd, _ = unit(UNITS * a + n % (UNITS // 2) * 2)
            src = T["fside_Bx16xSxS_0"][ATTENTIONS[a][0], hd:hd + 2, t * P:(t + 1) * P, :]
            eng.dma_start(bias[:, n % BIAS_RING, :, :], src.rearrange("h p k -> p h k")).then_inc(bias_in[n % BIAS_RING], 16)

        @block.sync
        def _(sp):
            sp.dma_start(xy[0][:], T["x"][0].rearrange("(t p) d -> p t d", p=P)).then_inc(x_in[0], 16)
            sp.dma_start(norm_w[0][:, 0:2], T["L0_cond_gamma1"].rearrange("(c p) -> p c", p=P)).then_inc(load_a, 16)
            sp.dma_start(norm_w[0][:, 2:4], T["L0_cond_beta1"].rearrange("(c p) -> p c", p=P)).then_inc(load_a, 16)
            sp.dma_start(wq[0][:], T["L0_cond_Wq"].rearrange("(c p) n -> p c n", p=P)).then_inc(load_a, 16)
            sp.dma_start(wk[0][:], T["L0_cond_Wk"].rearrange("(c p) n -> p c n", p=P)).then_inc(load_a, 16)
            for c in range(2):
                sp.dma_start(bqk[0][:, 2 * c:2 * c + 1], T["L0_cond_bq"][c * P:(c + 1) * P].unsqueeze(1)).then_inc(load_a, 16)
                sp.dma_start(bqk[0][:, 2 * c + 1:2 * c + 2], T["L0_cond_bk"][c * P:(c + 1) * P].unsqueeze(1)).then_inc(load_a, 16)
            sp.dma_start(wv[0][:], T["L0_cond_Wv"].rearrange("(c p) n -> p c n", p=P)).then_inc(load_a, 16)
            sp.dma_start(bv[0][:], T["L0_cond_bv"].partition_broadcast(P)).then_inc(load_a, 16)
            sp.dma_start(idx[:, 0:B], T["itok_B_0_15"].unsqueeze(0)).then_inc(load_a, 16)
            sp.dma_start(idx[:, B:2 * B], T["itok_B_0_7"].unsqueeze(0)).then_inc(load_a, 16)
            for s in range(1, B):
                sp.dma_start(xy[s][:], T["x"][s].rearrange("(t p) d -> p t d", p=P)).then_inc(x_in[s], 16)

            def weights(n, w1_src, w2_src):
                if n:
                    sp.wait_ge(f1_psum, NF * n)
                sp.dma_start(w1[:], w1_src.rearrange("(c p) n -> p c n", p=P)).then_inc(w1_in, 16)
                if n:
                    sp.wait_ge(f2_psum, 2 * n)
                sp.dma_start(w2[:], w2_src.rearrange("(c p) n -> p c n", p=P)).then_inc(w2_in, 16)

            def parts_to_dram(s, l):
                a = ATT[s, l]
                for i in range(4):
                    c, is_k = i // 2, i % 2
                    hs = slice(c * HH, (c + 1) * HH)
                    if a:
                        sp.wait_ge(stack_in[c], 96 * a)
                    sp.wait_ge(lo_done, 4 * a + i + 1)
                    dram, n = (k_dram, PARTS_K) if is_k else (q_dram, PARTS_Q)
                    for j in range(n):
                        sp.dma_start(dram[hs, j].rearrange("h d t -> h (d t)"),
                                     parts[i % 2][:, j % 3, :]).then_inc(parts_out[i], 16)

            def expert(s):
                if s:
                    sp.wait_ge(ad_act, 2 * s)
                e16 = sp.value_load(idx[0:1, s:s + 1], min_val=0, max_val=E16 - 1)
                sp.dma_start(exp_w[:], T["L1_cond_expert_W"][bass.ds(e16, 1)].rearrange("a o i -> (a o) i")).then_inc(expert_in, 16)
                sp.dma_start(exp_b[:, 0:1], T["L1_cond_expert_b"][bass.ds(e16, 1)].rearrange("a o -> o a")).then_inc(expert_in, 16)
                sp.dma_start(exp_b[:, 1:2], T["L1_cond_domain_emb"][bass.ds(e16, 1)].rearrange("a o -> o a")).then_inc(expert_in, 16)

            def rows(s):
                if s:
                    sp.wait_ge(hT_a, TURN[s - 1, 4] + 1)
                    sp.wait_ge(hT_v, TURN[s - 1, 4] + 1)
                else:
                    sp.wait_ge(ada_out, 16)
                e8 = sp.value_load(idx[0:1, B + s:B + s + 1], min_val=0, max_val=E8 - 1)
                sp.dma_start(b1[1][:], T["L2_cond_bi"][bass.ds(e8, 1)].rearrange("a (j p) -> p (a j)", p=P)).then_inc(rows_in, 16)
                for j, name in enumerate(["L2_cond_bo", "L2_cond_gamma", "L2_cond_beta"]):
                    sp.dma_start(l2row[:, j, :], T[name][bass.ds(e8, 1)].rearrange("a d -> (a d)").partition_broadcast(P)).then_inc(rows_in, 16)
                sp.dma_start(ada[:], ada_dram[s].partition_broadcast(P)).then_inc(rows_in, 16)

            def layer_0(s):
                weights(FFN[s, 0], T["L0_cond_W1"], T["L0_cond_W2"])

            def layer_2(s):
                e8 = sp.value_load(idx[0:1, B + s:B + s + 1], min_val=0, max_val=E8 - 1)
                weights(FFN[s, 1], T["L2_cond_Wi"][bass.ds(e8, 1)].rearrange("a d f -> (a d) f"),
                        T["L2_cond_Wo"][bass.ds(e8, 1)].rearrange("a d f -> (a d) f"))

            def layer_3(s):
                weights(FFN[s, 2], T["L3_cond_W1"], T["L3_cond_W2"])

            sp.wait_ge(load_a, 16 * LOADS_A)
            parts_to_dram(0, 0)
            layer_0(0)
            expert(0)
            parts_to_dram(1, 0)
            rows(0)
            sp.wait_ge(setup_v, SETUP_V)
            for n in range(BIAS_RING):
                load_bias(sp, n)
            parts_to_dram(2, 0)
            layer_2(0)
            expert(1)
            layer_0(1)
            layer_2(1)
            rows(1)
            parts_to_dram(0, 1)
            expert(2)
            layer_0(2)
            parts_to_dram(3, 0)
            layer_2(2)
            expert(3)
            rows(2)
            parts_to_dram(1, 1)
            layer_3(0)
            layer_0(3)
            rows(3)
            parts_to_dram(2, 1)
            layer_2(3)
            layer_3(1)
            parts_to_dram(3, 1)
            layer_3(2)
            layer_3(3)

        @block.gpsimd
        def _(pool):
            n_const = [0]

            def const(ins):
                n_const[0] += 1
                ins.then_inc(consts, 1)
                pool.wait_ge(consts, n_const[0])

            const(pool.memset(ident[:], 0.0))
            const(pool.affine_select(out=ident[:], in_=ident[:], compare_op=ALU.not_equal, fill=1.0, base=0,
                                     pattern=[[-1, P]], channel_multiplier=1))
            for l in range(2):
                const(pool.memset(wo[l][:], 0.0))
            assert n_const[0] == CONST_WO

            def late(dst, src):
                pool.dma_start(dst, src).then_inc(load_b, 16)

            late(tok_i, T["itok_B_34_63"].partition_broadcast(P))
            late(freq, T["freqs"].unsqueeze(1))
            const(pool.memset(identb[:], 0.0))
            const(pool.affine_select(out=identb[:], in_=identb[:], compare_op=ALU.not_equal, fill=1.0, base=0,
                                     pattern=[[-1, P]], channel_multiplier=1))
            const(pool.memset(causal[:], 0.0))
            const(pool.affine_select(out=causal[:], in_=causal[:], compare_op=ALU.is_ge, fill=NEG, base=0,
                                     pattern=[[-1, P]], channel_multiplier=1))
            const(pool.memset(va[0][:], 0.0))
            const(pool.memset(va[1][:], 0.0))
            const(pool.memset(eT[A:A + 1, :], 1.0))
            assert n_const[0] == CONSTS
            late(w_ada, T["L3_cond_W_ada"].rearrange("(c p) n -> p c n", p=P))
            late(b_ada, T["L3_cond_b_ada"].partition_broadcast(B))
            late(down_raw, T["L1_cond_down_W"])
            late(up_raw, T["L1_cond_up_W"].rearrange("(c p) a -> p c a", p=P))
            late(up_t[A:A + 1, :], T["L1_cond_up_b"].unsqueeze(0))
            late(down_b[:], T["L1_cond_down_b"].unsqueeze(1))
            late(gate[:], T["condB_gatescore"].partition_broadcast(P))
            for l, name in enumerate(["L0", "L3"]):
                wo_rows = T[f"{name}_cond_Wo"].rearrange("(g j r) n -> j r g n", g=NG, j=GH)
                for j in range(GH):
                    late(wo[l][32 * j:32 * j + DH, :, :], wo_rows[j])
                late(bo[l][:], T[f"{name}_cond_bo"].partition_broadcast(P))
                late(b2[l][:], T[f"{name}_cond_b2"].partition_broadcast(P))
                late(b1[2 * l][:], T[f"{name}_cond_b1"].rearrange("(j p) -> p j", p=P))
            late(norm_w[1][:, 0:2], T["L0_cond_gamma2"].rearrange("(c p) -> p c", p=P))
            late(norm_w[1][:, 2:4], T["L0_cond_beta2"].rearrange("(c p) -> p c", p=P))
            late(norm_w[2][:, 0:2], T["L3_cond_g2"].rearrange("(c p) -> p c", p=P))
            late(norm_w[2][:, 2:4], T["L3_cond_beta2"].rearrange("(c p) -> p c", p=P))
            late(ln1[:, 0, :], T["L1_cond_ln_gamma"].partition_broadcast(P))
            late(ln1[:, 1, :], T["L1_cond_ln_beta"].partition_broadcast(P))
            late(wq[1][:], T["L3_cond_Wq"].rearrange("(c p) n -> p c n", p=P))
            late(wk[1][:], T["L3_cond_Wk"].rearrange("(c p) n -> p c n", p=P))
            late(wv[1][:], T["L3_cond_Wv"].rearrange("(c p) n -> p c n", p=P))
            for c in range(2):
                late(bqk[1][:, 2 * c:2 * c + 1], T["L3_cond_bq"][c * P:(c + 1) * P].unsqueeze(1))
                late(bqk[1][:, 2 * c + 1:2 * c + 2], T["L3_cond_bk"][c * P:(c + 1) * P].unsqueeze(1))
            late(bv[1][:], T["L3_cond_bv"].partition_broadcast(P))
            pool.wait_ge(load_b, 16 * LOADS_B)
            pool.tensor_copy(sin_t[:, 0, :], tok_i).then_inc(setup_p, 1)
            pool.wait_ge(setup_p, 1)
            pool.tensor_scalar(wq[1][:], wq[1][:], 0.25, None, ALU.mult).then_inc(setup_p, 1)
            pool.wait_ge(setup_p, 2)
            pool.tensor_scalar(bqk[1][:, 0:4:2], bqk[1][:, 0:4:2], 0.25, None, ALU.mult).then_inc(setup_p, 1)
            pool.wait_ge(setup_p, 3)

            pool.wait_ge(setup_v, SETUP_ADA)
            pool.dma_start(ada_dram, ada4).then_inc(ada_out, 16)

            pooled = [0]

            def res(ins):
                pooled[0] += 1
                ins.then_inc(res_pool, 1)
                pool.wait_ge(res_pool, pooled[0])

            def res_l0(s):
                pool.wait_ge(tok[1], NT * NTH[s, 1] + NT)
                res(pool.tensor_tensor(x1[:], x1[:], xy[s][:], ALU.subtract))
                res(pool.tensor_tensor(x1[:], x1[:], b2[0][:].unsqueeze(1).broadcast_to([P, NT, D]), ALU.add))

            def res_l2(s):
                pool.wait_ge(rows_in, 16 * ROW_LOADS * (s + 1))
                pool.wait_ge(t_psum, TURN[s, 3] + 1)
                res(pool.tensor_tensor(xy[s][:], xy[s][:], l2row[:, 0:1, :].broadcast_to([P, NT, D]), ALU.add))

            def res_l3(s):
                pool.wait_ge(tok[5], NT * NTH[s, 5] + NT)
                res(pool.tensor_tensor(xy[s][:], xy[s][:], b2[1][:].unsqueeze(1).broadcast_to([P, NT, D]), ALU.add))

            def mask_load(m):
                pool.dma_start(maskraw[:, m % 2, :],
                               T["mask_Bx1xSxS_bk0"][m // NT, 0, m % NT * P:(m % NT + 1) * P, :]).then_inc(mask_in[m % 2], 16)

            def mask_term(m):
                pool.wait_ge(mask_in[m % 2], 16 * (m // 2 + 1))
                pool.tensor_scalar(negmask[:, m % NT, :], maskraw[:, m % 2, :], NEG, None, ALU.mult).then_inc(mask_neg, 1)
                pool.wait_ge(mask_neg, m + 1)
                if m + 2 < NT * B:
                    mask_load(m + 2)

            def mask_pair(n, t):
                pool.wait_ge(bias_in[n % BIAS_RING], 16 * (n // BIAS_RING + 1))
                b_n = bias[:, n % BIAS_RING, :, :]
                pool.tensor_tensor(b_n, b_n, negmask[:, t:t + 1, :].broadcast_to([P, 2, S]), ALU.add).then_inc(masked, 1)
                pool.wait_ge(masked, n + 1)

            for m in range(2):
                mask_load(m)
            steps, do = dense_steps("p"), {"res_l0": res_l0, "res_l2": res_l2, "res_l3": res_l3}
            for U in range(FIRST, LAST + 1):
                V = U + MASK_AHEAD
                if 0 <= V < ALL_UNITS and V // UNITS in BIASED and V % 2 == 0:
                    _, _, g, t, j, _, _ = unit(V)
                    if g == 0 and j == 0:
                        mask_term(NT * ATTENTIONS[V // UNITS][0] + t)
                    mask_pair(bias_pair(V), t)
                for step, args in steps.get(U, []):
                    do[step](*args)

        @block.scalar
        def _(act):
            def exponentials(U):
                a, l, g, t, j, hd, n = unit(U)
                act.wait_ge(max_done, U + 1)
                if l == 0:
                    if U >= 3:
                        act.wait_ge(pt_psum, U - 2)
                    act.activation(prob_of(U), score_bank[U % 2][:, 0:n], ACT.Exp, bias=mrow[:, U % ROW_RING:U % ROW_RING + 1],
                                   accum_out=rsum[:, U % ROW_RING:U % ROW_RING + 1]).then_inc(p_done, 1)
                else:
                    act.activation(prob_of(U), prob_of(U), ACT.Exp, scale=-1.0, bias=mrow[:, U % ROW_RING:U % ROW_RING + 1],
                                   accum_out=rsum[:, U % ROW_RING:U % ROW_RING + 1]).then_inc(p_done, 1)

            def copy(U):
                a, l, g, t, j, hd, n = unit(U)
                act.wait_ge(pt_psum, U + 1)
                if U >= PT_RING:
                    act.wait_ge(ctx_psum, (U - PT_RING) // GH + 1)
                act.activation(pT[:, U % PT_RING, 0:n // P, :],
                               turn_bank[U % 2][:, 0:n].rearrange("p (k q) -> p k q", q=P),
                               ACT.Identity).then_inc(pt_a, 1)

            def spread_copy(p):
                act.wait_ge(spread_psum, p + 1)
                if p:
                    act.wait_ge(ctx_norm, p)
                act.activation(spread[:], ctx_bank[:, 2 * P:4 * P], ACT.Identity).then_inc(spread_done, 1)

            def stack(s, l, c):
                a, hs = ATT[s, l], slice(c * HH, (c + 1) * HH)
                act.wait_ge(parts_out[2 * c], 16 * PARTS_Q * (a + 1))
                act.wait_ge(parts_out[2 * c + 1], 16 * PARTS_K * (a + 1))
                if a:
                    act.wait_ge(s_psum, UNITS * (a - 1) + UNITS // 2 * (c + 1))
                for r, k, q0, k0 in STACK:
                    rows = slice(r * DH, (r + k) * DH)
                    act.dma_start(qs[rows, hs, :],
                                  q_dram[hs, q0:q0 + k].rearrange("h p d t -> (p d) h t")).then_inc(stack_in[c], 16)
                    act.dma_start(ks[rows, hs, :],
                                  k_dram[hs, k0:k0 + k].rearrange("h p d t -> (p d) h t")).then_inc(stack_in[c], 16)

            def feature_half(s, k):
                act.wait_ge(t_psum, TURN[s, k] + 1)
                w = {0: 0, 1: 1, 5: 2}.get(k)
                if w is None:
                    act.activation(hT[:, 0, :], dense_bank[0][:], ACT.Identity).then_inc(hT_a, 1)
                else:
                    act.activation(hT[:, 0, :], dense_bank[0][:], ACT.Identity, scale=norm_w[w][:, 0:1],
                                   bias=norm_w[w][:, 2:3]).then_inc(hT_a, 1)

            def hi(s, l, i):
                a = ATT[s, l]
                act.wait_ge(qk_psum, 4 * a + i + 1)
                n = PARTS_K if i % 2 else PARTS_Q
                if i >= 2:
                    act.wait_ge(parts_out[i - 2], 16 * n * (a + 1))
                elif a:
                    act.wait_ge(parts_out[i + 2], 16 * n * a)
                act.activation(parts[i % 2][:, 0, :], dense_bank[QK_BANK[i]][:], ACT.Identity,
                               bias=bqk[l][:, i:i + 1]).then_inc(hi_done, 1)

            def mid(s, l, i):
                act.wait_ge(rest_done, 4 * ATT[s, l] + i + 1)
                act.activation(parts[i % 2][:, 1, :], rest[i % 2], ACT.Identity).then_inc(mid_done, 1)

            def gelu(s, f, j):
                n = FFN[s, f]
                if j == 0:
                    for i in (2, 3):
                        act.wait_ge(parts_out[i], 16 * (PARTS_K if i % 2 else PARTS_Q) * QKV_BEFORE[s, f])
                if f == 1 and j == 0:
                    act.wait_ge(rows_in, 16 * ROW_LOADS * (s + 1))
                act.wait_ge(f1_psum, NF * n + j + 1)
                act.activation(gT[:, j, :], dense_bank[FF_BANK[j]][:], ACT.Gelu_apprx_sigmoid if f == 2 else ACT.Gelu,
                               bias=b1[f][:, j:j + 1]).then_inc(g_done, 1)

            def down(s):
                act.wait_ge(ad_psum, 5 * ADAPT[s] + 2)
                act.activation(aT, dense_bank[0][0:A, :], ACT.Gelu, bias=down_b[:]).then_inc(ad_act, 1)

            def expert(s):
                act.wait_ge(ad_psum, 5 * ADAPT[s] + 3)
                act.wait_ge(ad_wt, 2 * ADAPT[s] + 2)
                act.activation(eT[0:A, :], dense_bank[1][0:A, :], ACT.Identity, bias=exp_b[:, 2:3]).then_inc(ad_act, 1)

            def store(s):
                act.wait_ge(ff_done, 2 * FFN[s, 2] + 2)
                act.dma_start(out[s].rearrange("(t p) d -> p t d", p=P), xy[s][:]).then_inc(stored, 16)

            def setup_sin():
                act.wait_ge(setup_v, SETUP_ANGLES)
                act.activation(sin_t[:, 14:16, :], sin_t[:, 12:14, :], ACT.Sin).then_inc(setup_a, 1)
                act.wait_ge(setup_a, 1)
                act.activation(sin_t[:, 16:18, :], sin_t[:, 14:16, :], ACT.Exp, scale=-1.0).then_inc(setup_a, 1)

            steps = dense_steps("a")
            do = {"feature_half": feature_half, "stack": stack, "hi": hi, "mid": mid, "gelu": gelu, "down": down, "expert": expert,
                  "store": store, "setup_sin": setup_sin}
            act.wait_ge(load_a, 16 * LOADS_A)
            act.wait_ge(setup_v, SETUP_SCALE)
            for U in range(FIRST, max(LAST + 1, ALL_UNITS + NORM_AT)):
                V = U - ACT_LAG
                if 0 <= V < ALL_UNITS and ON_ACT[V]:
                    copy(V)
                if 0 <= V < ALL_UNITS and V % 2 == 1 and V // UNITS in BIASED and bias_pair(V) + BIAS_RING < BIAS_PAIRS:
                    act.wait_ge(pt_psum, V + 1)
                    load_bias(act, bias_pair(V) + BIAS_RING)
                if 0 <= U < ALL_UNITS:
                    exponentials(U)
                V = U - SPREAD_COPY_AT
                if 0 <= V < ALL_UNITS and V % (2 * GH) == 0:
                    spread_copy(V // (2 * GH))
                if U == 16:
                    act.wait_ge(load_b, 16 * LOADS_B)
                    act.wait_ge(setup_p, 3)
                for step, args in steps.get(U, []):
                    do[step](*args)
            act.wait_ge(stored, 16 * B)

        @block.vector
        def _(v):
            n_setup = [0]

            def step(ins):
                n_setup[0] += 1
                ins.then_inc(setup_v, 1)
                v.wait_ge(setup_v, n_setup[0])

            count = [0]

            def link(ins):
                count[0] += 1
                ins.then_inc(vec, 1)
                v.wait_ge(vec, count[0])

            r = lambda i: sin_t[:, i, :]

            def setup_scale():
                v.wait_ge(load_a, 16 * LOADS_A)
                step(v.tensor_scalar(wq[0][:], wq[0][:], 0.25, None, ALU.mult))
                step(v.tensor_scalar(bqk[0][:, 0:4:2], bqk[0][:, 0:4:2], 0.25, None, ALU.mult))
                assert n_setup[0] == SETUP_SCALE

            def setup_angles():
                v.wait_ge(setup_p, 1)
                step(v.tensor_scalar(r(2), r(0), 0.01, None, ALU.mult))
                step(v.scalar_tensor_tensor(out=r(3), in0=r(2), scalar=-64.0, in1=r(0), op0=ALU.mult, op1=ALU.add))
                step(v.scalar_tensor_tensor(out=r(4), in0=r(2), scalar=-32.0, in1=r(3), op0=ALU.mult, op1=ALU.add))
                step(v.scalar_tensor_tensor(out=r(5), in0=r(2), scalar=-4.0, in1=r(4), op0=ALU.mult, op1=ALU.add))
                step(v.scalar_tensor_tensor(out=r(1), in0=r(5), scalar=0.01, in1=r(2), op0=ALU.mult, op1=ALU.add))
                step(v.tensor_scalar(r(2), r(1), 4000.0, None, ALU.mult))
                step(v.tensor_scalar(r(3), r(2), freq, None, ALU.mult))
                for i, quarter in ((0, 0.0), (1, 0.25)):
                    step(v.tensor_scalar(r(4), r(3), 1.0 / TWO_PI, quarter, ALU.mult, ALU.add))
                    step(v.tensor_scalar(r(5), r(4), ROUND, None, ALU.add))
                    step(v.tensor_scalar(r(6), r(5), ROUND, None, ALU.subtract))
                    step(v.scalar_tensor_tensor(out=r(7), in0=r(6), scalar=-PI_HI, in1=r(3), op0=ALU.mult, op1=ALU.add))
                    step(v.scalar_tensor_tensor(out=r(8), in0=r(6), scalar=-PI_MID, in1=r(7), op0=ALU.mult, op1=ALU.add))
                    step(v.scalar_tensor_tensor(out=r(9), in0=r(6), scalar=-PI_LO, in1=r(8), op0=ALU.mult, op1=ALU.add))
                    step(v.tensor_scalar(r(10), r(9), quarter * TWO_PI, PI_LIMIT, ALU.add, ALU.min))
                    step(v.tensor_scalar(r(12 + i), r(10), -PI_LIMIT, None, ALU.max))
                assert n_setup[0] == SETUP_ANGLES

            def setup_silu():
                v.wait_ge(setup_a, 2)
                step(v.tensor_scalar(sin_t[:, 18:20, :], sin_t[:, 16:18, :], 1.0, None, ALU.add))
                step(v.reciprocal(sin_t[:, 20:22, :], sin_t[:, 18:20, :]))
                step(v.tensor_tensor(sin_t[:, 22:24, :], sin_t[:, 20:22, :], sin_t[:, 14:16, :], ALU.mult))
                assert n_setup[0] == SETUP_SILU

            def setup_weights():
                v.wait_ge(setup_t, 3)
                step(v.tensor_tensor(ada4, dense_bank[0][0:B, :], b_ada, ALU.add))
                step(v.tensor_scalar(ada4[:, 0:D], ada4[:, 0:D], 1.0, None, ALU.add))
                assert n_setup[0] == SETUP_ADA
                step(v.tensor_copy(down_t[:], dense_bank[1][:, 0:ND * A].rearrange("p (c a) -> p c a", a=A)))
                step(v.tensor_copy(up_t[0:A, :], dense_bank[2][0:A, 0:D]))
                assert n_setup[0] == SETUP_V

            def state(s, k):
                return x1 if k == 1 else xy[s]

            def stats_of(s, k, i):
                if k == 0:
                    v.wait_ge(x_in[s], 16)
                for t in (2 * i, 2 * i + 1):
                    count[0] += 1
                    v.bn_stats(stats[:, t, :], state(s, k)[:, t, :]).then_inc(vec, 1)

            chain = [0]

            def rsqrt(s, k, i):
                var, bits, guess, sq = nwt[:, 0, :], nwt[:, 1, :], rstd[:], nwt[:, 2, :]
                v.wait_ge(vec, chain[0] if i else count[0])
                if i == 0:
                    for t in range(NT):
                        count[0] += 1
                        ins = v.bn_aggr(mv[:, t, :], stats[:, t, :])
                        if t < NT - 1:
                            ins.then_inc(vec, 1)
                elif i == 1:
                    ins = v.tensor_scalar(var, mv[:, :, 1], 1e-12 if k == 4 else 1e-5, None, ALU.add)
                elif i == 2:
                    ins = v.tensor_scalar(bits.bitcast(I32), var.bitcast(I32), 1, None, ALU.logical_shift_right)
                elif i == 3:
                    ins = v.tensor_scalar(guess.bitcast(I32), bits.bitcast(I32), -1.0, RSQRT_MAGIC, ALU.mult, ALU.add)
                elif i % 3 == 1:
                    ins = v.tensor_tensor(sq, guess, guess, ALU.mult)
                elif i % 3 == 2:
                    ins = v.scalar_tensor_tensor(out=bits, in0=sq, scalar=-0.5, in1=var, op0=ALU.mult, op1=ALU.mult)
                else:
                    ins = v.scalar_tensor_tensor(out=guess, in0=bits, scalar=1.5, in1=guess, op0=ALU.add, op1=ALU.mult)
                if i:
                    count[0] += 1
                ins.then_inc(vec, 1)
                chain[0] = count[0]

            def norm_rows(k):
                return {3: (ln1[:, 0, :], ln1[:, 1, :]), 4: (l2row[:, 1, :], l2row[:, 2, :]),
                        5: (ada[:, 0:D], ada[:, D:2 * D])}[k]

            def apply(s, k, i):
                v.wait_ge(vec, chain[0])
                if k in (0, 1, 6):
                    for t in (2 * i, 2 * i + 1):
                        v.tensor_scalar(h[:, t, :], state(s, k)[:, t, :], mv[:, t, 0:1], rstd[:, t:t + 1],
                                        ALU.subtract, ALU.mult).then_inc(tok[min(k, 5)], 1)
                else:
                    y = xy[s]
                    if k == 4:
                        v.wait_ge(rows_in, 16 * ROW_LOADS * (s + 1))
                    for t in (2 * i, 2 * i + 1):
                        count[0] += 1
                        v.scalar_tensor_tensor(out=y[:, t, :], in0=y[:, t, :], scalar=mv[:, t, 0:1], in1=norm_rows(k)[0],
                                               op0=ALU.subtract, op1=ALU.mult).then_inc(vec, 1)

            def apply_late(s, k, i):
                y = xy[s]
                v.wait_ge(vec, count[0])
                for t in (2 * i, 2 * i + 1):
                    ins = v.scalar_tensor_tensor(out=y[:, t, :], in0=y[:, t, :], scalar=rstd[:, t:t + 1],
                                                 in1=norm_rows(k)[1], op0=ALU.mult, op1=ALU.add)
                    if k == 4:
                        count[0] += 1
                        ins.then_inc(vec, 1)
                    else:
                        ins.then_inc(tok[3 if k == 3 else 4], 1)
                if k == 4:
                    v.wait_ge(vec, count[0])

            def feature_half(s, k):
                v.wait_ge(t_psum, TURN[s, k] + 1)
                w = {0: 0, 1: 1, 5: 2}.get(k)
                if w is None:
                    v.tensor_copy(hT[:, 1, :], dense_bank[1][:]).then_inc(hT_v, 1)
                else:
                    v.tensor_scalar(hT[:, 1, :], dense_bank[1][:], norm_w[w][:, 1:2], norm_w[w][:, 3:4],
                                    ALU.mult, ALU.add).then_inc(hT_v, 1)

            def rest_of(s, l, i):
                v.wait_ge(hi_done, 4 * ATT[s, l] + i + 1)
                v.scalar_tensor_tensor(out=rest[i % 2], in0=dense_bank[QK_BANK[i]][:], scalar=bqk[l][:, i:i + 1],
                                       in1=parts[i % 2][:, 0, :], op0=ALU.add, op1=ALU.subtract).then_inc(rest_done, 1)

            def lo(s, l, i):
                v.wait_ge(mid_done, 4 * ATT[s, l] + i + 1)
                v.tensor_tensor(parts[i % 2][:, 2, :], rest[i % 2], parts[i % 2][:, 1, :],
                                ALU.subtract).then_inc(lo_done, 1)

            def values_out(s, l, i):
                a = ATT[s, l]
                if a < 2:
                    v.wait_ge(consts, CONSTS)
                v.wait_ge(v_psum, 2 * a + i + 1)
                for t in (2 * i, 2 * i + 1):
                    v.tensor_tensor(va[a % 2][:, t, :, 0:DH],
                                    dense_bank[V_BANK[i]][:, (t % 2) * D:(t % 2 + 1) * D].rearrange("p (h d) -> p h d", d=DH),
                                    bv[l][:].rearrange("p (h d) -> p h d", d=DH), ALU.add).then_inc(v_done, 1)

            def pairs(psum):
                return psum[:].rearrange("p (t d) -> p t d", d=D)

            def residual(s, l, i):
                v.wait_ge(wo_psum, 2 * ATT[s, l] + i + 1)
                tt = slice(2 * i, 2 * i + 2)
                dst = xy[s] if l else x1
                link(v.tensor_tensor(dst[:, tt, :], pairs(dense_bank[i]), xy[s][:, tt, :], ALU.add))
                v.tensor_tensor(dst[:, tt, :], dst[:, tt, :], bo[l][:].unsqueeze(1).broadcast_to([P, 2, D]),
                                ALU.add).then_inc(wo_done, 1)
                v.wait_ge(wo_done, 2 * ATT[s, l] + i + 1)

            def ff_add(s, f, i):
                n, tt = FFN[s, f], slice(2 * i, 2 * i + 2)
                if i == 0:
                    v.wait_ge(res_pool, res_count(s, (0, 2, 3)[f]))
                v.wait_ge(f2_psum, 2 * n + i + 1)
                psum = pairs(dense_bank[FF_OUT_BANK[i]])
                dst = xy[s] if f else x1
                v.tensor_tensor(dst[:, tt, :], psum, dst[:, tt, :], ALU.add).then_inc(ff_done, 1)
                v.wait_ge(ff_done, 2 * n + i + 1)
                if f == 0:
                    for t in (2 * i, 2 * i + 1):
                        v.scalar_tensor_tensor(out=xy[s][:, t, :], in0=x1[:, t, :], scalar=gate[:, s:s + 1],
                                               in1=xy[s][:, t, :], op0=ALU.mult, op1=ALU.add).then_inc(tok[2], 1)
                        v.wait_ge(tok[2], NT * NTH[s, 2] + t + 1)

            def expert(s):
                v.wait_ge(ad_psum, 5 * ADAPT[s] + 1)
                v.tensor_copy(exp_wt[:], dense_bank[2][0:A, 0:A]).then_inc(ad_wt, 1)
                v.wait_ge(expert_in, 16 * EXPERT_LOADS * (s + 1))
                v.tensor_tensor(exp_b[:, 2:3], exp_b[:, 0:1], exp_b[:, 1:2], ALU.add).then_inc(ad_wt, 1)

            def up_add(s, i):
                v.wait_ge(ad_psum, 5 * ADAPT[s] + 4 + i)
                tt = slice(2 * i, 2 * i + 2)
                v.tensor_tensor(xy[s][:, tt, :], pairs(dense_bank[UP_BANK[i]]), xy[s][:, tt, :], ALU.add).then_inc(up_done, 1)
                v.wait_ge(up_done, 2 * ADAPT[s] + i + 1)

            def maxima(U):
                a, l, g, t, j, hd, n = unit(U)
                m = mrow[:, U % ROW_RING:U % ROW_RING + 1]
                if l == 0:
                    v.wait_ge(s_psum, U + 1)
                    v.tensor_reduce(m, score_bank[U % 2][:, 0:n], AX_X, ALU.max, negate=True).then_inc(max_done, 1)
                else:
                    if j % 2 == 0:
                        v.wait_ge(masked, bias_pair(U) + 1)
                    v.wait_ge(s_psum, U + 1)
                    v.tensor_tensor_reduce(out=prob_of(U), in0=score_bank[U % 2][:], in1=prob_of(U), scale=-1.0,
                                           scalar=3e38, op0=ALU.add, op1=ALU.min, accum_out=m).then_inc(max_done, 1)

            def copy(U):
                a, l, g, t, j, hd, n = unit(U)
                v.wait_ge(pt_psum, U + 1)
                if U >= PT_RING:
                    v.wait_ge(ctx_psum, (U - PT_RING) // GH + 1)
                v.tensor_copy(pT[:, U % PT_RING, 0:n // P, :],
                              turn_bank[U % 2][:, 0:n].rearrange("p (k q) -> p k q", q=P)).then_inc(pt_v, 1)

            def invert(p):
                u = 2 * GH * p % ROW_RING
                v.wait_ge(p_done, 2 * GH * (p + 1))
                link(v.reciprocal(rinv[:], rsum[:, u:u + 2 * GH]))
                if p:
                    v.wait_ge(spread_psum, p)
                v.tensor_copy(rwide[:].rearrange("p w (j r) -> p (w j) r", r=32),
                              rinv[:].unsqueeze(2).broadcast_to([P, 2 * GH, 32])).then_inc(inv_done, 1)

            def normalize(p):
                a, w = p // (QUADS // 2), p % (QUADS // 2) * 2
                g, t = divmod(w, NT)
                if w == 0 and a:
                    v.wait_ge(wo_psum, 2 * a)
                v.wait_ge(spread_done, p + 1)
                v.tensor_tensor(ctxn[:, g, t * P:(t + 2) * P], ctx_bank[:, 0:2 * P], spread[:], ALU.mult).then_inc(ctx_norm, 1)

            steps = dense_steps("v")
            do = {"stats": stats_of, "rsqrt": rsqrt, "apply": apply, "apply_late": apply_late,
                  "feature_half": feature_half, "rest": rest_of, "lo": lo, "v": values_out, "residual": residual,
                  "ff_add": ff_add, "expert": expert, "up_add": up_add, "setup_angles": setup_angles, "setup_scale": setup_scale,
                  "setup_silu": setup_silu, "setup_weights": setup_weights}
            small = [dense_steps(f"v{i}") for i in range(SLOTS)]

            def slot(i, U):
                for name, args in small[i].get(U, []):
                    do[name](*args)

            for U in range(FIRST, max(LAST + 1, ALL_UNITS + NORM_AT + 1)):
                slot(0, U)
                V = U - VEC_LAG
                if 0 <= V < ALL_UNITS and not ON_ACT[V]:
                    copy(V)
                slot(1, U)
                if 0 <= U < ALL_UNITS:
                    maxima(U)
                slot(2, U)
                V = U - SUM_AT
                if 0 <= V < ALL_UNITS and V % (2 * GH) == 0:
                    invert(V // (2 * GH))
                V = U - NORM_AT
                if 0 <= V < ALL_UNITS and V % (2 * GH) == 0:
                    normalize(V // (2 * GH))
                if U == 16:
                    v.wait_ge(load_b, 16 * LOADS_B)
                slot(3, U)
                for name, args in steps.get(U, []):
                    do[name](*args)

        @block.tensor
        def _(pe):
            def dense_banks_free(upto):
                if upto["qkv"]:
                    pe.wait_ge(v_done, 4 * upto["qkv"])
                    pe.wait_ge(rest_done, 4 * upto["qkv"])
                if upto["ffn"]:
                    pe.wait_ge(ff_done, 2 * upto["ffn"])
                if upto["out"]:
                    pe.wait_ge(wo_done, 2 * upto["out"])
                if upto["up"]:
                    pe.wait_ge(up_done, 2 * upto["up"])
                if upto["turn"]:
                    pe.wait_ge(hT_a, upto["turn"])
                    pe.wait_ge(hT_v, upto["turn"])

            issued = {"up": 0, "qkv": 0, "ffn": 0, "out": 0, "turn": 0}

            def turn_tokens(s, k):
                dense_banks_free(issued)
                src = h if k in (0, 1, 5) else xy[s]
                for t in range(NT):
                    pe.wait_ge(tok[k], NT * NTH[s, k] + t + 1)
                    for c in range(ND):
                        mm = pe.transpose(dense_bank[c][:, t * P:(t + 1) * P], src[:, t, c * P:(c + 1) * P], ident[:])
                mm.then_inc(t_psum, 1)
                issued["turn"] += 1

            def hT_ready(s, k):
                pe.wait_ge(hT_a, TURN[s, k] + 1)
                pe.wait_ge(hT_v, TURN[s, k] + 1)

            def qk(s, l, i):
                if i == 0:
                    hT_ready(s, 0 if l == 0 else 4)
                if l == 0 and i == 0:
                    pe.wait_ge(load_a, 16 * LOADS_A)
                    pe.wait_ge(setup_v, SETUP_SCALE)
                if l == 1 and i == 0:
                    pe.wait_ge(setup_p, 3)
                if i == 2:
                    pe.wait_ge(v_done, 4 * ATT[s, l] + 2)
                if i == 3:
                    pe.wait_ge(rest_done, 4 * ATT[s, l] + 1)
                w, c0 = (wk[l] if i % 2 else wq[l]), (i // 2) * P
                for c in range(ND):
                    mm = pe.matmul(dense_bank[QK_BANK[i]][:], w[:, c, c0:c0 + P], hT[:, c, :], start=c == 0, stop=c == ND - 1)
                mm.then_inc(qk_psum, 1)
                if i == 3:
                    issued["qkv"] += 1

            def v_rows(s, l, i):
                if i:
                    pe.wait_ge(rest_done, 4 * ATT[s, l] + 2)
                for t in (2 * i, 2 * i + 1):
                    for c in range(ND):
                        mm = pe.matmul(dense_bank[V_BANK[i]][:, (t % 2) * D:(t % 2 + 1) * D], hT[:, c, t * P:(t + 1) * P],
                                       wv[l][:, c, :], start=c == 0, stop=c == ND - 1)
                mm.then_inc(v_psum, 1)

            def project(s, l, i):
                if i == 0:
                    dense_banks_free(issued)
                    pe.wait_ge(ctx_norm, QUADS // 2 * (ATT[s, l] + 1))
                for t in (2 * i, 2 * i + 1):
                    for g in range(NG):
                        mm = pe.matmul(dense_bank[i][:, (t % 2) * D:(t % 2 + 1) * D], ctxn[:, g, t * P:(t + 1) * P],
                                       wo[l][:, g, :], start=g == 0, stop=g == NG - 1)
                mm.then_inc(wo_psum, 1)
                if i == 1:
                    issued["out"] += 1

            def hidden(s, f, j):
                n = FFN[s, f]
                if j == 0:
                    hT_ready(s, (1, 3, 5)[f])
                    pe.wait_ge(w1_in, 16 * (n + 1))
                if j >= 3:
                    pe.wait_ge(g_done, NF * n + j - 2)
                for c in range(ND):
                    mm = pe.matmul(dense_bank[FF_BANK[j]][:], w1[:, c, j * P:(j + 1) * P], hT[:, c, :],
                                   start=c == 0, stop=c == ND - 1)
                mm.then_inc(f1_psum, 1)

            def ff_out(s, f, t):
                n = FFN[s, f]
                if t == 0:
                    pe.wait_ge(w2_in, 16 * (n + 1))
                for j in range(NF):
                    if t == 0 and j in (0, 6, 7):
                        pe.wait_ge(g_done, NF * n + max(6, j + 1))
                    mm = pe.matmul(dense_bank[FF_OUT_BANK[t // 2]][:, (t % 2) * D:(t % 2 + 1) * D],
                                   gT[:, j, t * P:(t + 1) * P], w2[:, j, :], start=j == 0, stop=j == NF - 1)
                if t % 2:
                    mm.then_inc(f2_psum, 1)
                if t == NT - 1:
                    issued["ffn"] += 1

            def turn_expert(s):
                pe.wait_ge(expert_in, 16 * EXPERT_LOADS * (s + 1))
                pe.wait_ge(ff_done, 2 * FFN[s, 0] + 2)
                pe.transpose(dense_bank[2][0:A, 0:A], exp_w[:], ident[0:A, 0:A]).then_inc(ad_psum, 1)

            def down(s):
                hT_ready(s, 2)
                if not ADAPT[s]:
                    pe.wait_ge(setup_v, SETUP_V)
                for c in range(ND):
                    mm = pe.matmul(dense_bank[0][0:A, :], down_t[:, c, :], hT[:, c, :], start=c == 0, stop=c == ND - 1)
                mm.then_inc(ad_psum, 1)

            def expert(s):
                pe.wait_ge(ad_act, 2 * ADAPT[s] + 1)
                pe.wait_ge(ad_wt, 2 * ADAPT[s] + 1)
                pe.matmul(dense_bank[1][0:A, :], exp_wt[:], aT, start=True, stop=True).then_inc(ad_psum, 1)

            def up(s):
                pe.wait_ge(ad_act, 2 * ADAPT[s] + 2)
                for t in range(NT):
                    mm = pe.matmul(dense_bank[UP_BANK[t // 2]][:, (t % 2) * D:(t % 2 + 1) * D], eT[:, t * P:(t + 1) * P],
                                   up_t[:], start=True, stop=True)
                    if t % 2:
                        mm.then_inc(ad_psum, 1)
                issued["up"] += 1

            def setup():
                dense_banks_free(issued)
                pe.wait_ge(load_b, 16 * LOADS_B)
                pe.wait_ge(setup_v, SETUP_SILU)
                for c in range(ND):
                    mm = pe.matmul(dense_bank[0][0:B, :], sin_t[:, 22 + c, :], w_ada[:, c, :], start=c == 0, stop=c == ND - 1)
                mm.then_inc(setup_t, 1)
                for c in range(ND):
                    mm = pe.transpose(dense_bank[1][:, c * A:(c + 1) * A], down_raw[:, c * P:(c + 1) * P], ident[0:A, 0:A])
                mm.then_inc(setup_t, 1)
                for c in range(ND):
                    mm = pe.transpose(dense_bank[2][0:A, c * P:(c + 1) * P], up_raw[:, c, :], ident[:])
                mm.then_inc(setup_t, 1)

            def scores(U):
                a, l, g, t, j, hd, n = unit(U)
                if U % (UNITS // 2) == 0:
                    pe.wait_ge(stack_in[hd // HH], 96 * (a + 1))
                if U >= 2:
                    pe.wait_ge(p_done if unit(U - 2)[1] == 0 else max_done, U - 1)
                mm = pe.matmul(score_bank[U % 2][:, 0:n], qs[:, hd, t * P:(t + 1) * P], ks[:, hd, 0:n],
                               start=True, stop=l == 1)
                if l == 0:
                    mm = pe.matmul(score_bank[U % 2][:, n - P:n], identb[:], causal[:], start=False, stop=True)
                mm.then_inc(s_psum, 1)

            def copied(U):
                pe.wait_ge(pt_v, U - COPIES_A[U])
                if COPIES_A[U]:
                    pe.wait_ge(pt_a, COPIES_A[U])

            def turn(U):
                a, l, g, t, j, hd, n = unit(U)
                pe.wait_ge(p_done, U + 1)
                if U >= 2:
                    copied(U - 1)
                for k in range(n // P):
                    mm = pe.transpose(turn_bank[U % 2][:, k * P:(k + 1) * P], prob_of(U)[:, k * P:(k + 1) * P], ident[:])
                mm.then_inc(pt_psum, 1)

            def values(w):
                a, l, g, t, _, _, n = unit(GH * w)
                copied(GH * (w + 1))
                if w % QUADS == 0:
                    pe.wait_ge(v_done, 4 * (a + 1))
                if w % 2 == 0 and w:
                    pe.wait_ge(ctx_norm, w // 2)
                for k in range(n // P):
                    for j in range(GH):
                        mm = pe.matmul(ctx_bank[32 * j:32 * (j + 1), w % 2 * P:(w % 2 + 1) * P], va[a % 2][:, k, GH * g + j, :],
                                       pT[:, (GH * w + j) % PT_RING, k, :], start=k == 0, stop=k == n // P - 1)
                mm.then_inc(ctx_psum, 1)

            def spread_sums(p):
                pe.wait_ge(inv_done, p + 1)
                if p:
                    pe.wait_ge(spread_done, p)
                for w in range(2):
                    mm = pe.transpose(ctx_bank[:, (2 + w) * P:(3 + w) * P], rwide[:, w, :], ident[:])
                mm.then_inc(spread_psum, 1)

            steps = dense_steps("pe")
            do = {"turn_tokens": turn_tokens, "qk": qk, "v": v_rows, "project": project, "hidden": hidden,
                  "ff_out": ff_out, "turn_expert": turn_expert, "down": down, "expert": expert, "up": up, "setup": setup}
            pe.wait_ge(consts, 2)
            for U in range(FIRST, max(LAST + 1, ALL_UNITS + NORM_AT + 1)):
                if U == 0:
                    pe.wait_ge(consts, CONSTS)
                if 0 <= U < ALL_UNITS:
                    scores(U)
                V = U - TURN_LAG
                if 0 <= V < ALL_UNITS:
                    turn(V)
                V = U - VALUES_AT
                if 0 <= V < ALL_UNITS and V % GH == 0:
                    values(V // GH)
                V = U - SPREAD_AT
                if 0 <= V < ALL_UNITS and V % (2 * GH) == 0:
                    spread_sums(V // (2 * GH))
                for step, args in steps.get(U, []):
                    do[step](*args)


QK_BANK = (2, 0, 1, 2)
V_BANK = (1, 0)
FF_BANK = (2, 0, 1, 2, 0, 1, 2, 0)
FF_OUT_BANK = (1, 2)
UP_BANK = (2, 0)
MASK_AHEAD = 4
CONST_WO = 4
CONSTS = CONST_WO + 7
SETUP_SCALE = 2
SETUP_ANGLES = SETUP_SCALE + 5 + 2 + 2 * 8
SETUP_SILU = SETUP_ANGLES + 3
SETUP_ADA = SETUP_SILU + 2
SETUP_V = SETUP_ADA + 2

_NAMES = ["x", "condB_gatescore", "itok_B_0_15", "itok_B_0_7", "itok_B_34_63", "fside_Bx16xSxS_0", "mask_Bx1xSxS_bk0"]
_NAMES += ["L0_cond_" + n for n in "Wq bq Wk bk Wv bv Wo bo W1 b1 W2 b2 gamma1 beta1 gamma2 beta2".split()]
_NAMES += ["L1_cond_" + n for n in "down_W down_b up_W up_b expert_W expert_b domain_emb ln_gamma ln_beta".split()]
_NAMES += ["L2_cond_" + n for n in "Wi bi Wo bo gamma beta".split()]
_NAMES += ["L3_cond_" + n for n in "W_ada b_ada Wq bq Wk bk Wv bv Wo bo W1 b1 W2 b2 g2 beta2".split()]


def kernel(**inputs):
    import math
    import numpy as np
    from concourse import bacc
    from concourse.bass_utils import run_bass_kernel_spmd

    nc = bacc.Bacc("TRN2", target_bir_lowering=False, num_devices=1)
    arrays = {name: np.ascontiguousarray(inputs[name]) for name in _NAMES}
    half = D // 2
    step = np.float32(-math.log(10000.0) / (half - 1))
    arrays["freqs"] = np.exp(np.arange(half, dtype=np.float32) * step).astype(np.float32)
    T = {n: nc.dram_tensor("in_" + n, a.shape, mybir.dt.from_np(a.dtype), kind="ExternalInput").ap()
         for n, a in arrays.items()}
    out = nc.dram_tensor("out_0", (B, S, D), F32, kind="ExternalOutput").ap()
    build(nc, T, out)
    r = run_bass_kernel_spmd(nc, [{"in_" + n: a for n, a in arrays.items()}], core_ids=[0])
    return r.results[0]["out_0"]
```
